# Optimizing a Trainium2 kernel written in Bass

```python
import numpy as np
import jax
import jax.numpy as jnp

def _softmax(x, axis=-1):
    return jax.nn.softmax(x, axis=axis)

def _gelu(x):
    return jax.nn.gelu(x, approximate=True)

def _silu(x):
    return jax.nn.silu(x)

def _sigmoid(x):
    return jax.nn.sigmoid(x)

def _layernorm(x, axis=-1, eps=1e-05):
    m = jnp.mean(x, axis=axis, keepdims=True)
    v = jnp.var(x, axis=axis, keepdims=True)
    return (x - m) / jnp.sqrt(v + eps)

def _scatter_add(tgt, idx, src, axis=0):
    return tgt.at[idx].add(src)

def _segment_sum(src, seg, n):
    return jax.ops.segment_sum(src, seg, n)
kernel_name = 'mk_seq_postln_d2_jaxref_r8_3eb74a'

def setup_inputs(seed: int=0):
    np.random.seed(seed)
    _w = jnp.asarray

    def _L0_attn_setup():
        import jax, jax.numpy as jnp
        import numpy as np
        HIDDEN = 256
        HEADS = 8
        HEAD_DIM = HIDDEN // HEADS
        EPS = 1e-05

        def _position_thetas(head_dim, scale=10000.0):
            x = jnp.linspace(0.0, 1.0, head_dim // 2)
            thetas = 1.0 / scale ** x
            return jnp.repeat(thetas, 2)

        def _decay_gammas(num_heads):
            x = jnp.linspace(np.log(1 / 32), np.log(1 / 64), num_heads)
            return 1.0 - jnp.exp(x)

        def _decay_mask(n, s, gammas):
            qpos = jnp.arange(n, dtype=jnp.float32)[:, None]
            kpos = jnp.arange(s, dtype=jnp.float32)[None, :]
            dist = qpos - kpos
            dist = jnp.where(dist < 0, jnp.inf, dist)
            return gammas[:, None, None] ** dist[None]

        def _multiply_by_i(x):
            xe = x[..., ::2]
            xo = x[..., 1::2]
            return jnp.stack((-xo, xe), axis=-1).reshape(x.shape)

        def _theta_shift(x, sin, cos):
            return x * cos + _multiply_by_i(x) * sin
        key = jax.random.key(seed)
        ks = jax.random.split(key, 10)
        std = 0.02
        x = jax.random.normal(ks[0], (2, 512, HIDDEN), dtype=jnp.float32)

        def lin(k):
            return jax.random.normal(k, (HIDDEN, HIDDEN), dtype=jnp.float32) * std
        return {'x': x, 'w_q': lin(ks[1]), 'b_q': jnp.zeros((HIDDEN,), jnp.float32), 'w_k': lin(ks[2]), 'b_k': jnp.zeros((HIDDEN,), jnp.float32), 'w_v': lin(ks[3]), 'b_v': jnp.zeros((HIDDEN,), jnp.float32), 'w_g': lin(ks[4]), 'b_g': jnp.zeros((HIDDEN,), jnp.float32), 'w_o': lin(ks[5]), 'b_o': jnp.zeros((HIDDEN,), jnp.float32), 'gn_weight': jnp.ones((HIDDEN,), jnp.float32), 'gn_bias': jnp.zeros((HIDDEN,), jnp.float32)}
    _L0_attn_in = _L0_attn_setup()

    def _L0_ffn_setup():
        import jax, jax.numpy as jnp
        import numpy as np
        EPS = 1e-08

        def _quantize(w):
            gamma = jnp.mean(jnp.abs(w))
            return jnp.clip(jnp.round(w / (gamma + EPS)), -1.0, 1.0)

        def _bitlinear(x, w):
            return jnp.matmul(x, _quantize(w).T)
        key = jax.random.key(seed)
        k1, k2, k3, k4 = jax.random.split(key, 4)
        d, h = (256, 704)
        x = jax.random.normal(k1, (4, 256, d), dtype=jnp.float32)
        w1 = jax.random.normal(k2, (h, d), dtype=jnp.float32)
        w2 = jax.random.normal(k3, (h, d), dtype=jnp.float32)
        w3 = jax.random.normal(k4, (d, h), dtype=jnp.float32)
        return {'x': x, 'w1': w1, 'w2': w2, 'w3': w3}
    _L0_ffn_in = _L0_ffn_setup()

    def _L1_attn_setup():
        import jax, jax.numpy as jnp
        import numpy as np
        D_MODEL = 256
        N_HEADS = 16
        HEAD_DIM = D_MODEL // N_HEADS
        B, T = (2, 256)
        key = jax.random.key(seed)
        ks = jax.random.split(key, 9)
        s = 0.02
        x = jax.random.normal(ks[0], (B, T, D_MODEL), dtype=jnp.float32)
        Wq = jax.random.normal(ks[1], (N_HEADS, D_MODEL, HEAD_DIM), dtype=jnp.float32) * s
        bq = jax.random.normal(ks[2], (N_HEADS, HEAD_DIM), dtype=jnp.float32) * s
        Wk = jax.random.normal(ks[3], (N_HEADS, D_MODEL, HEAD_DIM), dtype=jnp.float32) * s
        bk = jax.random.normal(ks[4], (N_HEADS, HEAD_DIM), dtype=jnp.float32) * s
        Wv = jax.random.normal(ks[5], (N_HEADS, D_MODEL, HEAD_DIM), dtype=jnp.float32) * s
        bv = jax.random.normal(ks[6], (N_HEADS, HEAD_DIM), dtype=jnp.float32) * s
        Wo = jax.random.normal(ks[7], (D_MODEL, D_MODEL), dtype=jnp.float32) * s
        bo = jax.random.normal(ks[8], (D_MODEL,), dtype=jnp.float32) * s
        return {'x': x, 'Wq': Wq, 'bq': bq, 'Wk': Wk, 'bk': bk, 'Wv': Wv, 'bv': bv, 'Wo': Wo, 'bo': bo}
    _L1_attn_in = _L1_attn_setup()

    def _L1_ffn_setup():
        import jax, jax.numpy as jnp
        import numpy as np
        H = 256
        I_MOE = 176
        I_SH = 704
        E = 8
        TOP_K = 2
        B, S = (1, 256)

        def _silu_and_mul(gu, inter):
            return jax.nn.silu(gu[..., :inter]) * gu[..., inter:]
        key = jax.random.key(seed)
        ks = jax.random.split(key, 7)
        sc = 0.02
        return {'hidden_states': jax.random.normal(ks[0], (B, S, H), jnp.float32), 'W_router': jax.random.normal(ks[1], (E, H), jnp.float32) * sc, 'W_sgate': jax.random.normal(ks[2], (1, H), jnp.float32) * sc, 'Ws_gate_up': jax.random.normal(ks[3], (H, 2 * I_SH), jnp.float32) * sc, 'Ws_down': jax.random.normal(ks[4], (I_SH, H), jnp.float32) * sc, 'We_gate_up': jax.random.normal(ks[5], (E, H, 2 * I_MOE), jnp.float32) * sc, 'We_down': jax.random.normal(ks[6], (E, I_MOE, H), jnp.float32) * sc}
    _L1_ffn_in = _L1_ffn_setup()
    _d = {'L0_attn_x': _L0_attn_in['x'], 'L0_attn_w_q': _L0_attn_in['w_q'], 'L0_attn_b_q': _L0_attn_in['b_q'], 'L0_attn_w_k': _L0_attn_in['w_k'], 'L0_attn_b_k': _L0_attn_in['b_k'], 'L0_attn_w_v': _L0_attn_in['w_v'], 'L0_attn_b_v': _L0_attn_in['b_v'], 'L0_attn_w_g': _L0_attn_in['w_g'], 'L0_attn_b_g': _L0_attn_in['b_g'], 'L0_attn_w_o': _L0_attn_in['w_o'], 'L0_attn_b_o': _L0_attn_in['b_o'], 'L0_attn_gn_weight': _L0_attn_in['gn_weight'], 'L0_attn_gn_bias': _L0_attn_in['gn_bias'], 'L0_ffn_w1': _L0_ffn_in['w1'], 'L0_ffn_w2': _L0_ffn_in['w2'], 'L0_ffn_w3': _L0_ffn_in['w3'], 'L1_attn_Wq': _L1_attn_in['Wq'], 'L1_attn_bq': _L1_attn_in['bq'], 'L1_attn_Wk': _L1_attn_in['Wk'], 'L1_attn_bk': _L1_attn_in['bk'], 'L1_attn_Wv': _L1_attn_in['Wv'], 'L1_attn_bv': _L1_attn_in['bv'], 'L1_attn_Wo': _L1_attn_in['Wo'], 'L1_attn_bo': _L1_attn_in['bo'], 'L1_ffn_W_router': _L1_ffn_in['W_router'], 'L1_ffn_W_sgate': _L1_ffn_in['W_sgate'], 'L1_ffn_Ws_gate_up': _L1_ffn_in['Ws_gate_up'], 'L1_ffn_Ws_down': _L1_ffn_in['Ws_down'], 'L1_ffn_We_gate_up': _L1_ffn_in['We_gate_up'], 'L1_ffn_We_down': _L1_ffn_in['We_down']}
    _x0 = _d['L0_attn_x']
    _d['L0_attn_x'] = jax.random.normal(jax.random.fold_in(jax.random.key(seed), 1), (2, 512, 256), dtype=_x0.dtype)
    del _x0
    return _d

def reference(L0_attn_x, L0_attn_w_q, L0_attn_b_q, L0_attn_w_k, L0_attn_b_k, L0_attn_w_v, L0_attn_b_v, L0_attn_w_g, L0_attn_b_g, L0_attn_w_o, L0_attn_b_o, L0_attn_gn_weight, L0_attn_gn_bias, L0_ffn_w1, L0_ffn_w2, L0_ffn_w3, L1_attn_Wq, L1_attn_bq, L1_attn_Wk, L1_attn_bk, L1_attn_Wv, L1_attn_bv, L1_attn_Wo, L1_attn_bo, L1_ffn_W_router, L1_ffn_W_sgate, L1_ffn_Ws_gate_up, L1_ffn_Ws_down, L1_ffn_We_gate_up, L1_ffn_We_down):

    def _L0_attn_ref(x, w_q, b_q, w_k, b_k, w_v, b_v, w_g, b_g, w_o, b_o, gn_weight, gn_bias):
        import jax, jax.numpy as jnp
        import numpy as np
        HIDDEN = 256
        HEADS = 8
        HEAD_DIM = HIDDEN // HEADS
        EPS = 1e-05

        def _position_thetas(head_dim, scale=10000.0):
            x = jnp.linspace(0.0, 1.0, head_dim // 2)
            thetas = 1.0 / scale ** x
            return jnp.repeat(thetas, 2)

        def _decay_gammas(num_heads):
            x = jnp.linspace(np.log(1 / 32), np.log(1 / 64), num_heads)
            return 1.0 - jnp.exp(x)

        def _decay_mask(n, s, gammas):
            qpos = jnp.arange(n, dtype=jnp.float32)[:, None]
            kpos = jnp.arange(s, dtype=jnp.float32)[None, :]
            dist = qpos - kpos
            dist = jnp.where(dist < 0, jnp.inf, dist)
            return gammas[:, None, None] ** dist[None]

        def _multiply_by_i(x):
            xe = x[..., ::2]
            xo = x[..., 1::2]
            return jnp.stack((-xo, xe), axis=-1).reshape(x.shape)

        def _theta_shift(x, sin, cos):
            return x * cos + _multiply_by_i(x) * sin
        B, N, _ = x.shape
        q = x @ w_q + b_q
        k = x @ w_k + b_k
        v = x @ w_v + b_v
        g = x @ w_g + b_g

        def split(t):
            return t.reshape(B, N, HEADS, HEAD_DIM).transpose(0, 2, 1, 3)
        q, k, v = (split(q), split(k), split(v))
        thetas = _position_thetas(HEAD_DIM)
        pos = jnp.arange(N, dtype=jnp.float32)[:, None] * thetas[None, :]
        sin = jnp.sin(pos)[None, None]
        cos = jnp.cos(pos)[None, None]
        q = _theta_shift(q, sin, cos)
        k = _theta_shift(k, sin, cos)
        gammas = _decay_gammas(HEADS)
        mask = _decay_mask(N, N, gammas)
        scale = HEAD_DIM ** 0.5
        sim = jnp.einsum('bhnd,bhsd->bhns', q, k / scale) * mask[None]
        ret = jnp.einsum('bhns,bhsd->bhnd', sim, v)
        ret = ret.transpose(0, 2, 1, 3).reshape(B, N, HIDDEN)
        r = ret.reshape(B, N, HEADS, HEAD_DIM)
        mean = r.mean(axis=-1, keepdims=True)
        var = r.var(axis=-1, keepdims=True)
        r = (r - mean) / jnp.sqrt(var + EPS)
        ret = r.reshape(B, N, HIDDEN) * gn_weight + gn_bias
        gate = jax.nn.silu(g) * ret
        return gate @ w_o + b_o

    def _L0_ffn_ref(x, w1, w2, w3):
        import jax, jax.numpy as jnp
        import numpy as np
        EPS = 1e-08

        def _quantize(w):
            gamma = jnp.mean(jnp.abs(w))
            return jnp.clip(jnp.round(w / (gamma + EPS)), -1.0, 1.0)

        def _bitlinear(x, w):
            return jnp.matmul(x, _quantize(w).T)
        x1 = _bitlinear(x, w1)
        x2 = _bitlinear(x, w2)
        hidden = jax.nn.sigmoid(x1) * x2
        return _bitlinear(hidden, w3)

    def _L1_attn_ref(x, Wq, bq, Wk, bk, Wv, bv, Wo, bo):
        import jax, jax.numpy as jnp
        import numpy as np
        D_MODEL = 256
        N_HEADS = 16
        HEAD_DIM = D_MODEL // N_HEADS
        B, T = (2, 256)
        Bn, Tn, C = x.shape
        H, _, D = Wq.shape
        scale = D ** (-0.5)
        q = jnp.einsum('btc,hcd->bhtd', x, Wq) + bq[None, :, None, :]
        k = jnp.einsum('btc,hcd->bhtd', x, Wk) + bk[None, :, None, :]
        v = jnp.einsum('btc,hcd->bhtd', x, Wv) + bv[None, :, None, :]
        scores = jnp.einsum('bhtd,bhsd->bhts', q, k) * scale
        neg = jnp.finfo(scores.dtype).min
        causal = jnp.triu(jnp.full((Tn, Tn), neg, dtype=scores.dtype), k=1)
        probs = jax.nn.softmax(scores + causal, axis=-1)
        y = jnp.einsum('bhts,bhsd->bhtd', probs, v)
        y = y.transpose(0, 2, 1, 3).reshape(Bn, Tn, H * D)
        return y @ Wo + bo

    def _L1_ffn_ref(hidden_states, W_router, W_sgate, Ws_gate_up, Ws_down, We_gate_up, We_down):
        import jax, jax.numpy as jnp
        import numpy as np
        H = 256
        I_MOE = 176
        I_SH = 704
        E = 8
        TOP_K = 2
        B, S = (1, 256)

        def _silu_and_mul(gu, inter):
            return jax.nn.silu(gu[..., :inter]) * gu[..., inter:]
        orig_shape = hidden_states.shape
        x = hidden_states.reshape(-1, H)
        T = x.shape[0]
        logits = x @ W_router.T
        probs = jax.nn.softmax(logits.astype(jnp.float32), axis=-1)
        rw, sel = jax.lax.top_k(probs, TOP_K)
        rw = rw.astype(x.dtype)
        combine = jnp.zeros((T, E), x.dtype).at[jnp.arange(T)[:, None], sel].add(rw)
        sh = _silu_and_mul(x @ Ws_gate_up, I_SH) @ Ws_down
        shared_out = sh * jax.nn.sigmoid(x @ W_sgate.T)
        gu = jnp.einsum('th,ehi->eti', x, We_gate_up)
        h = _silu_and_mul(gu, I_MOE)
        eo = jnp.einsum('eti,eih->eth', h, We_down)
        sparse_out = jnp.einsum('eth,te->th', eo, combine)
        return (shared_out + sparse_out).reshape(orig_shape)
    x = L0_attn_x
    x = _layernorm(x + _L0_attn_ref(x, L0_attn_w_q, L0_attn_b_q, L0_attn_w_k, L0_attn_b_k, L0_attn_w_v, L0_attn_b_v, L0_attn_w_g, L0_attn_b_g, L0_attn_w_o, L0_attn_b_o, L0_attn_gn_weight, L0_attn_gn_bias), axis=-1)
    x = _layernorm(x + _L0_ffn_ref(x, L0_ffn_w1, L0_ffn_w2, L0_ffn_w3), axis=-1)
    x = _layernorm(x + _L1_attn_ref(x, L1_attn_Wq, L1_attn_bq, L1_attn_Wk, L1_attn_bk, L1_attn_Wv, L1_attn_bv, L1_attn_Wo, L1_attn_bo), axis=-1)
    x = _layernorm(x + _L1_ffn_ref(x, L1_ffn_W_router, L1_ffn_W_sgate, L1_ffn_Ws_gate_up, L1_ffn_Ws_down, L1_ffn_We_gate_up, L1_ffn_We_down), axis=-1)
    return x

_drawn_inputs = setup_inputs


def setup_inputs(seed=0):
    import zlib

    import numpy as np

    out = dict(_drawn_inputs(seed))
    spreads = {'L0_attn_b_q': (0.0, 0.1),
     'L0_attn_b_k': (0.0, 0.1),
     'L0_attn_b_v': (0.0, 0.1),
     'L0_attn_b_g': (0.0, 0.1),
     'L0_attn_b_o': (0.0, 0.1),
     'L0_attn_gn_weight': (1.0, 0.6),
     'L0_attn_gn_bias': (0.0, 0.8)}
    factors = {'L1_attn_Wq': 8.0,
     'L1_attn_bq': 8.0,
     'L1_attn_Wk': 8.0,
     'L1_attn_bk': 8.0,
     'L1_attn_Wv': 4.026,
     'L1_attn_bv': 8.0,
     'L1_attn_Wo': 3.558,
     'L1_attn_bo': 2.954,
     'L1_ffn_W_router': 8.0,
     'L1_ffn_W_sgate': 8.0,
     'L1_ffn_Ws_gate_up': 4.049,
     'L1_ffn_Ws_down': 4.038,
     'L1_ffn_We_gate_up': 8.0,
     'L1_ffn_We_down': 8.0}
    for name, (base, spread) in spreads.items():
        noise = np.random.default_rng([zlib.crc32(name.encode()), seed]).standard_normal(out[name].shape)
        drawn = base * np.exp(spread * noise) if base else spread * noise
        out[name] = jnp.asarray(drawn.astype(out[name].dtype))
    for name, factor in factors.items():
        out[name] = (out[name] * factor).astype(out[name].dtype)
    return out
```

```python
import concourse.bass as bass
from concourse import mybir
from contextlib import ExitStack
import numpy as np

P = 128
D = 256
KD = D // P
NT = 8
NB = 2
TB = NT // NB
RH, RD = 8, 32
AH, AD = 16, 16
F0 = 704
FM = 6
NE, FE, FS = 8, 176, 704
HID = NE * FE + FS
MC, MCW = 6, 352
HK = (HID + P - 1) // P
LAST = F0 % P
EPS = 1e-5

SA = 16.0
SW = 64.0
UN = 1.0 / (SA * SW)

W_QKVG = 0
W_O0 = W_QKVG + KD * 4 * D
W_O1 = W_O0 + KD * D
W_QKV1 = W_O1 + KD * D
W_UP = W_QKV1 + KD * 3 * D
W_DOWN = W_UP + KD * 2 * HID
W_TAIL = W_DOWN + (HK - 1) * D
W_ROUT = W_TAIL + D
NR = NE + 1
W_TOT = W_ROUT + KD * NR
STAGE = 1024
NSTAGE = 3


C_ID = 0
C_KEEP = C_ID + P
C_G128 = C_KEEP + P
C_COS = C_G128 + KD
C_SIN = C_COS + TB * RD // 2
C_DEC = C_SIN + TB * RD // 2
C_IOTA = C_DEC + 2 * RH
C_TOT = C_IOTA + NE


def pieces():
    out = [("xT", 0, 1024, 0), ("xT", 1024, 1024, 1024)]
    at = [("wqkvg", W_QKVG, KD * 4 * D, 1024), ("wo", W_O0, 2 * KD * D, 1024),
          ("wqkv1", W_QKV1, KD * 3 * D, 768), ("wup", W_UP, KD * 2 * HID, STAGE),
          ("wdown", W_DOWN, (HK - 1) * D, 1024), ("wtail", W_TAIL, D + KD * NR, STAGE)]
    for name, first, n, step in at:
        for a in range(0, n, step):
            out.append((name, a, min(step, n - a), first + a))
    return out


PIECES = pieces()


def schedule():
    out = [("split", 0), ("tables",)] + [("split", i) for i in range(1, 4)]
    later = [("split", i) for i in range(4, len(PIECES))]
    later.insert(1, ("wsum",))
    later.insert(3, ("gsum",))
    for i in range(3):
        later.insert(5 + 2 * i, ("quant", i))

    for s in range(NT + 7):
        for lag, kinds in ((6, ("ln", "tx")), (5, ("wo",)), (4, ("gn", "ty")), (3, ("ret",)),
                           (2, ("sc0", "sc1", "kv")), (1, ("rot", "tqk")), (0, ("proj",))):
            t = s - lag
            if not 0 <= t < NT:
                continue
            for kind in kinds:
                if kind in ("ln", "tx", "ty", "wo"):
                    out.append((kind, 0, t))
                elif kind in ("sc0", "sc1"):
                    out.append(("sc", t, int(kind[2])))
                elif kind != "kv" or t % TB < TB - 1:
                    out.append((kind, t))
        for _ in range(2):
            if s >= 1 and later:
                out.append(later.pop(0))
    out += later

    def tail(layer, tiles, product):
        steps = []
        for s in range(len(tiles) + 2):
            if s >= 2 and layer < 3:
                steps.append(("tx", layer, tiles[s - 2]))
            if s < len(tiles):
                steps += product(tiles[s])
            if 1 <= s <= len(tiles):
                steps.append(("ln", layer, tiles[s - 1]))
        return steps

    def ffn0(n):
        steps = []
        for m in range(FM + 1):
            if m < FM:
                steps.append(("up", n, m))
            if m:
                steps.append(("cut", n, m - 1))
        return steps + tail(1, range(TB * n, TB * n + TB), lambda t: [("dn", t)])

    def attn1(b):
        steps = []
        for s in range(TB + 2):
            if s < TB:
                steps.append(("qk", b, s))
            if 1 <= s <= TB:
                steps += [("st", b, s - 1), ("tq", b, s - 1)]
        for i in range(TB):
            steps += [("mx", b, i, p) for p in range(AH // 2)]
            if i:
                steps.append(("tm", b, i - 1))
        steps.append(("tm", b, TB - 1))
        waiting = []
        for g in range(AH // 4):
            for j in range(TB):
                steps += [("se", b, g, j, 0), ("se", b, g, j, 1)]
                waiting.append(("pv", b, g, j))
                if len(waiting) > 1:
                    steps.append(waiting.pop(0))
        steps += waiting
        tiles = range(TB * b, TB * b + TB)
        steps += [("ya", b, 0)]

        def product(t):
            more = [("ya", b, t % TB + 1)] if t % TB + 1 < TB else []
            return [("ty", 2, t)] + more + [("wo", 2, t)]
        return steps + tail(2, tiles, product)

    def moe():
        steps = [("rt", 0)]
        for t in range(NT + 1):
            for c in range(MC):
                if t < NT:
                    if c == 0:
                        steps.append(("rc", t))
                    steps.append(("mu", t, c))
                    if c == 3:
                        steps.append(("mt", t, 0))
                if c == 1 and t:
                    steps += [("mt", t - 1, 1), ("mt", t - 1, 2)]
                if c == 2 and t:
                    steps.append(("md", t - 1))
                if c == 3 and t:
                    steps.append(("ln", 3, t - 1))
                if c == 4 and t + 1 < NT:
                    steps.append(("rt", t + 1))
        return steps

    out += ffn0(0) + ffn0(1) + attn1(0) + attn1(1) + moe()
    return out


SCHEDULE = schedule()

RING_A, RING_B = 3, 2
RING_OF = {"proj": "A", "tqk": "B", "sc": "A", "kv": "B", "ret": "B", "ty": "B", "wo": "B", "tx": "B",
           "gsum": "B", "up": "A", "dn": "B", "qk": "A", "tq": "A", "mx": "A", "tm": "B", "se": "A",
           "pv": "B", "ya": "B", "rt": "B", "mu": "A", "mt": "A", "md": "B"}


def occurrences():
    seen, out = {}, {}
    for step in SCHEDULE:
        seen[step[0]] = seen.get(step[0], 0) + 1
        out[step] = seen[step[0]]
    return out


NTH = occurrences()
LAYER = {"dn": 1, "md": 3}


def psum_places():
    turns, done, out, user = {"A": 0, "B": 0}, 0, {}, {}
    size = {"A": RING_A, "B": RING_B}
    for step in SCHEDULE:
        if step[0] not in RING_OF:
            continue
        ring = "B" if step[0] == "mt" and step[2] == 2 else RING_OF[step[0]]
        done += 1
        if step[0] == "pv" and step[3]:
            at, before = out[("pv", step[1], step[2], 0)][1:3]
        else:
            at = turns[ring] % size[ring]
            before = user.get((ring, at))
            user[ring, at] = step
            turns[ring] += 1
        out[step] = (ring, at, before, done)
    return out


PLACE = psum_places()


def build_two_layers(nc: bass.Bass, xT, x, wqkvg, wo, wqkv1, wup, wdown, wtail, w12, w3, rows0, rows1,
                     consts, consts16, block_decay, out):
    f32, f16, u32 = mybir.dt.float32, mybir.dt.float16, mybir.dt.uint32
    ALU, ACT, AX = mybir.AluOpType, mybir.ActivationFunctionType, mybir.AxisListType
    source = {"xT": xT, "wqkvg": wqkvg, "wo": wo, "wqkv1": wqkv1, "wup": wup, "wdown": wdown, "wtail": wtail}

    with ExitStack() as ctx:
        def sb(name, shape, dt=f32):
            return ctx.enter_context(nc.sbuf_tensor(name, shape, dt))

        def sem(name):
            return ctx.enter_context(nc.semaphore(name))

        ws = sb("cut_weights", [P, 2, W_TOT], f16)
        stage = sb("stage", [P, NSTAGE, STAGE])
        X = sb("residual", [P, NT, D])
        XT = sb("x_transposed", [P, 2, KD, NT * P], f16)
        con = sb("constants", [P, C_TOT])
        con16 = sb("constants16", [P, 2 * P], f16)
        row1 = sb("rows_layer1", [P, 4 * D])
        Y = sb("y", [P, 2, D])
        YT = sb("y_transposed", [P, 2, D], f16)
        Z = sb("z", [P, 2, D])
        stats = sb("ln_stats", [P, 3, 6])
        mv = sb("ln_mean_var", [P, 3, 2])
        veps = sb("ln_var_eps", [P, 3])
        rstd = sb("ln_rstd", [P, 3])
        half = sb("minus_half", [P, RH])
        gs = sb("weight_sums", [P, 4])
        thr = sb("thresholds", [P, 2, 3])
        small = sb("router", [P, 2, 64])
        small_i = sb("router_index", [P, 2, 8], u32)

        arena1 = sb("arena_mixers", [P, 17448])
        arena2 = sb("arena_ffn", [P, 7872])

        class Carve:
            def __init__(self, arena):
                self.arena, self.at = arena, 0

            def __call__(self, dims, dt=f32):
                n = int(np.prod(dims)) // (2 if dt == f16 else 1)
                view = self.arena[:, self.at:self.at + n]
                self.at += n
                assert self.at <= self.arena.shape[1], self.at
                if dt == f16:
                    view = view.bitcast(f16)
                if len(dims) == 1:
                    return view
                names = "abcdef"[:len(dims)]
                return view.rearrange(f"p ({' '.join(names)}) -> p {' '.join(names)}",
                                      **{c: d for c, d in zip(names, dims)})

        cut = Carve(arena1)
        row0 = cut([7 * D])
        tab_cos = cut([TB, 2 * RH, RD // 2])
        tab_sin = cut([TB, 2 * RH, RD // 2])
        QK0 = cut([2, 2 * D])
        VG = cut([4, 2 * D])
        ROT = cut([2, 2 * D])
        R1 = cut([2, 2 * D])
        R2 = cut([2, 2 * D])
        QKT = cut([2, 4, P])
        PT = cut([2, 2, 2, 2, P])
        TS = cut([TB - 1, D])
        block_g = cut([D])
        ones = cut([P])
        KVM = cut([D])
        CENT = cut([2, D])
        SQ = cut([D])
        GA = cut([3, D])
        GC = cut([3, D])
        TH = cut([2, D])
        gsmall = cut([2, 4, RH])
        cut = Carve(arena1)
        QK32 = cut([2, 2, AH, AD])
        ST = cut([TB, 2, AH, 64], f16)
        QT = cut([AH // 2, TB * P], f16)
        KT = cut([AH // 2, TB * P], f16)
        V = cut([TB, AH, 32])
        PE1 = cut([2, 4, TB * P])
        YU = cut([AH // 4, TB * P])
        rden = cut([2, AH])
        cut = Carve(arena2)
        Q12 = cut([KD, 2 * F0], f16)
        Q3 = cut([FM, D], f16)
        work_at = cut.at
        raw12 = cut([KD, 2 * F0])
        raw3 = cut([FM, D])
        cut.at = work_at
        HT0 = cut([2, FM, TB * P], f16)
        HF = cut([2, TB * P])
        THF = cut([2, TB * P])
        cut = Carve(arena2)
        H = cut([HID])
        HT = cut([2, 2, HK, P], f16)
        TG = cut([2, MCW])
        AG = cut([2, MCW])

        psA = [ctx.enter_context(nc.psum_tensor(f"psum_a{i}", [P, 2, 512], f32)) for i in range(RING_A)]
        psB = [ctx.enter_context(nc.psum_tensor(f"psum_b{i}", [P, 512], f32)) for i in range(RING_B)]

        def psum(step):
            ring, at, _, _ = PLACE[step]
            return psA[at] if ring == "A" else psB[at]

        def psum16(step):
            ring, at, _, _ = PLACE[step]
            return psA[at][:, :, :].bitcast(f16) if ring == "A" else psB[at][:, :].bitcast(f16)

        pe_done = sem("pe_done")
        piece_in = [sem(f"piece_in{i}") for i in range(len(PIECES))]
        head_cut, rest_cut = sem("head_cut"), sem("rest_cut")
        con_in, con16_in, x_in, row0_in, row1_in = (sem(n) for n in ("con_in", "con16_in", "x_in", "row0_in", "row1_in"))
        raw_in = sem("raw_in")
        tables, resid, ready0 = sem("tables_ready"), sem("residual_biased"), sem("memsets_done")
        block_in = sem("block_in")
        evac0, rot2, rotated = sem("qkvg_copied"), sem("rot_second_term"), sem("rotated")
        qkT, pT, state = sem("qk_transposed"), sem("masked_scores"), sem("state_ready")
        tanh0, gates, gvar, grstd = sem("gate_tanh"), sem("gates_ready"), sem("gn_var"), sem("gn_rstd")
        y_ready, y_head, y_rest = sem("y_ready"), sem("y_head"), sem("y_rest")
        ln_var, ln_rstd, ln_done = sem("ln_var"), sem("ln_rstd"), sem("ln_done")
        x_head, x_rest = sem("x_head"), sem("x_rest")
        sums, quant = sem("weight_sums_ready"), sem("quantized")
        up_tanh, hidden, h_head, h_rest = sem("up_tanh"), sem("hidden"), sem("h_head"), sem("h_rest")
        qk_evac, st_head, st_rest = sem("qk_copied"), sem("stack_heads"), sem("stack_rests")
        st_second, centered, z_ready = sem("stack_second_heads"), sem("centered"), sem("z_ready")
        thresholds, logit_read = sem("thresholds_ready"), sem("logits_read")
        q_up, k_up = sem("q_stack_transposed"), sem("k_stack_transposed")
        maxed, q_max = sem("row_max"), sem("q_max_transposed")
        exped, causal, yu = sem("exp_done"), sem("causal_done"), sem("pv_copied")
        st_init = sem("stack_init")
        logits, r_exp, coef = sem("logits"), sem("router_exp"), sem("coefficients")
        mu_tanh, mu_h, mt_head, mt_rest = sem("mu_tanh"), sem("mu_hidden"), sem("mt_head"), sem("mt_rest")
        dve_order, pool_order, out_done = sem("dve_order"), sem("pool_order"), sem("out_done")

        ident = con[:, C_ID:C_ID + P]
        ident16 = con16[:, 0:P]
        below16 = con16[:, P:2 * P]

        def bc(ap, shape):
            return ap.to_broadcast(shape)

        block = ctx.enter_context(nc.Block())

        @block.sync
        def _(sp):
            def load(i):
                name, a, n, _ = PIECES[i]
                if i >= NSTAGE:
                    sp.wait_ge(rest_cut, NTH[("split", i - NSTAGE)])
                sp.dma_start(stage[:, i % NSTAGE, 0:n], source[name][:, a:a + n]).then_inc(piece_in[i], 16)

            for i in range(NSTAGE):
                load(i)
            sp.dma_start(row0, rows0.partition_broadcast(P)).then_inc(row0_in, 16)
            sp.dma_start(con[:, :], consts).then_inc(con_in, 16)
            sp.dma_start(block_g, block_decay).then_inc(block_in, 16)
            sp.dma_start(X[:, :, :], x.rearrange("(t p) d -> p t d", p=P)).then_inc(x_in, 16)
            load(NSTAGE)
            sp.dma_start(raw12, w12.rearrange("(k p) n -> p k n", p=P)).then_inc(raw_in, 16)
            sp.dma_start(raw3[:, 0:FM - 1, :], w3[0:(FM - 1) * P, :].rearrange("(k p) n -> p k n", p=P)).then_inc(raw_in, 16)
            sp.dma_start(raw3[0:LAST, FM - 1, :], w3[(FM - 1) * P:F0, :]).then_inc(raw_in, 16)
            sp.dma_start(con16[:, :], consts16).then_inc(con16_in, 16)
            sp.dma_start(row1[:, :], rows1.partition_broadcast(P)).then_inc(row1_in, 16)
            for i in range(NSTAGE + 1, len(PIECES)):
                load(i)
            for t in range(NT):
                sp.wait_ge(ln_done, NTH[("ln", 3, t)])
                sp.dma_start(out[t * P:(t + 1) * P, :], X[:, t, :]).then_inc(out_done, 16)
            sp.wait_ge(out_done, 16 * NT)

        @block.tensor
        def _(pe):
            mm = nc.tensor.matmul

            reader = {"proj": evac0, "tqk": qkT, "sc": pT, "kv": state, "ret": centered, "ty": y_rest, "tx": x_rest,
                      "gsum": thresholds, "up": hidden, "qk": qk_evac, "mx": maxed, "tm": q_max, "se": exped,
                      "ya": y_ready, "rt": logit_read, "mu": mu_h, "mt": mt_rest}

            def claim(step):
                last = PLACE[step][2]
                if last is None:
                    return
                if last[0] == "tq":
                    pe.wait_ge(q_up, NTH[last])
                    pe.wait_ge(k_up, NTH[last])
                elif last[0] == "pv":
                    pe.wait_ge(yu, NTH[("pv", last[1], last[2], TB - 1)] // TB)
                elif last[0] in ("wo", "dn", "md"):
                    pe.wait_ge(z_ready, NTH[("ln", LAYER.get(last[0], last[1]), last[-1])])
                elif last[0] == "ya":
                    pe.wait_ge(y_ready, NTH[("ty", 2, last[1] * TB + last[2])])
                else:
                    pe.wait_ge(reader[last[0]], NTH[last])

            def cut_product(out_of, lhs, rhs, last):
                n = len(lhs)
                ins = None
                for k in range(n):
                    for a, b in ((0, 0), (0, 1), (1, 0)):
                        for dst, col in out_of:
                            ins = mm(dst, lhs[k][a], rhs(k, b, col), start=(k == 0 and a == 0 and b == 0),
                                     stop=(k == n - 1 and a == 1))
                return ins

            def x_tiles(t):
                return [[XT[:, a, k, t * P:(t + 1) * P] for a in range(2)] for k in range(KD)]

            for step in SCHEDULE:
                kind = step[0]
                if kind not in RING_OF:
                    continue
                ps = psum(step)
                if kind == "proj":
                    t = step[1]
                    if t == 0:
                        pe.wait_ge(rest_cut, NTH[("split", 3)])
                    claim(step)
                    w = ws[:, :, W_QKVG:W_O0].rearrange("p a (k n) -> p a k n", k=KD)
                    ins = cut_product([(ps[:, 0, :], 0), (ps[:, 1, :], 512)], x_tiles(t),
                                      lambda k, b, c: w[:, b, k, c:c + 512], True)
                elif kind == "tqk":
                    t = step[1]
                    pe.wait_ge(rotated, t + 1)
                    claim(step)
                    for j in range(4):
                        ins = nc.tensor.transpose(ps[:, j * P:(j + 1) * P], ROT[:, t % 2, j * P:(j + 1) * P], ident)
                elif kind == "sc":
                    _, t, hf = step
                    pe.wait_ge(qkT, t + 1)
                    claim(step)
                    for g in range(2):
                        for s in range(2):
                            r = 32 * (2 * hf + s)
                            ins = mm(ps[:, s, g * P:(g + 1) * P], QKT[r:r + 32, t % 2, 2 + g, :],
                                     QKT[r:r + 32, t % 2, g, :], start=True, stop=True)
                elif kind == "kv":
                    t = step[1]
                    claim(step)
                    for g in range(2):
                        ins = mm(ps[:, g * P:(g + 1) * P], ROT[:, t % 2, D + g * P:D + (g + 1) * P],
                                 VG[:, t % 4, g * P:(g + 1) * P], start=True, stop=True)
                elif kind == "ret":
                    t = step[1]
                    c = t % TB
                    pe.wait_ge(pT, NTH[("sc", t, 1)])
                    if c:
                        pe.wait_ge(state, NTH[("kv", t - 1)])
                    claim(step)
                    if t == 0:
                        pe.wait_ge(con_in, 16)
                    if c:
                        for g in range(2):
                            mm(ps[:, g * P:(g + 1) * P], QKT[:, t % 2, g, :], TS[:, c - 1, g * P:(g + 1) * P],
                               start=(g == 0), stop=False, skip_group_check=True)
                    for h in range(RH):
                        g, s = divmod(h, 4)
                        ins = mm(ps[:, h * RD:(h + 1) * RD], PT[:, t % 2, s // 2, s % 2, g, :],
                                 VG[:, t % 4, h * RD:(h + 1) * RD],
                                 start=(h == 0 and not c), stop=(h == RH - 1), skip_group_check=True)
                elif kind == "ty":
                    pe.wait_ge(y_ready, NTH[step])
                    claim(step)
                    for k in range(KD):
                        ins = nc.tensor.transpose(ps[:, k * P:(k + 1) * P], Y[:, NTH[step] % 2, k * P:(k + 1) * P], ident)
                elif kind == "wo":
                    _, layer, t = step
                    pe.wait_ge(y_rest, NTH[step])
                    if layer == 0 and t == 0:
                        pe.wait_ge(rest_cut, NTH[("split", 4)])
                    claim(step)
                    first = W_O1 if layer else W_O0
                    w = ws[:, :, first:first + KD * D].rearrange("p a (k n) -> p a k n", k=KD)
                    ins = cut_product([(ps[:, 0:D], 0)], [[YT[:, a, k * P:(k + 1) * P] for a in range(2)] for k in range(KD)],
                                      lambda k, b, c: w[:, b, k, :], True)
                elif kind == "tx":
                    _, layer, t = step
                    pe.wait_ge(ln_done, NTH[("ln", layer, t)])
                    claim(step)
                    for k in range(KD):
                        ins = nc.tensor.transpose(ps[:, k * P:(k + 1) * P], X[:, t, k * P:(k + 1) * P], ident)
                elif kind == "gsum":
                    pe.wait_ge(sums, 1)
                    claim(step)
                    ins = mm(ps[:, 0:4], ones, gs[:, :], start=True, stop=True)
                elif kind == "up":
                    _, n, m = step
                    rows = P if m < FM - 1 else LAST
                    if m == 0:
                        pe.wait_ge(x_rest, NTH[("tx", 0, TB * n + TB - 1)])
                        pe.wait_ge(quant, 3)
                    claim(step)
                    for k in range(KD):
                        for gu in range(2):
                            w = Q12[:, k, gu * F0 + m * P:gu * F0 + m * P + rows]
                            for a in range(2):
                                ins = mm(ps[0:rows, gu, :], w, XT[:, a, k, n * TB * P:(n + 1) * TB * P],
                                         start=(k == 0 and a == 0), stop=(k == KD - 1 and a == 1))
                elif kind == "dn":
                    t = step[1]
                    pe.wait_ge(h_rest, NTH[("cut", t // TB, FM - 1)])
                    pe.wait_ge(h_head, NTH[("cut", t // TB, FM - 1)])
                    claim(step)
                    c = (t % TB) * P
                    for m in range(FM):
                        rows = P if m < FM - 1 else LAST
                        for a in range(2):
                            ins = mm(ps[:, 0:D], HT0[0:rows, a, m, c:c + P], Q3[0:rows, m, :],
                                     start=(m == 0 and a == 0), stop=(m == FM - 1 and a == 1))
                elif kind == "qk":
                    _, b, i = step
                    t = b * TB + i
                    pe.wait_ge(x_rest, NTH[("tx", 1, t)])
                    claim(step)
                    w = ws[:, :, W_QKV1:W_UP].rearrange("p a (k n) -> p a k n", k=KD)
                    ins = cut_product([(ps[:, 0, :], 0), (ps[:, 1, 0:D], 512)], x_tiles(t),
                                      lambda k, b_, c: w[:, b_, k, c:c + (D if c else 512)], True)
                elif kind == "tq":
                    _, b, i = step
                    pe.wait_ge(st_rest, NTH[("st", b, i)])
                    pe.wait_ge(st_second, NTH[("st", b, i)])
                    if step == ("tq", 0, 0):
                        pe.wait_ge(con16_in, 16)
                    claim(step)
                    p16 = psum16(step)
                    for w in range(2):
                        for p in range(AH // 2):
                            ins = nc.tensor.transpose(p16[:, w, p * P:(p + 1) * P],
                                                      ST[:, i, w, 2 * p:2 * p + 2, :], ident16)
                elif kind == "mx":
                    _, b, i, p = step
                    if p == 0:
                        pe.wait_ge(q_up, NTH[("tq", b, i)])
                        pe.wait_ge(k_up, NTH[("tq", b, i)])
                    claim(step)
                    for s in range(2):
                        mm(ps[:, s, i * P:(i + 1) * P], ident16, below16, start=True, stop=True)
                    for s in range(2):
                        r = 64 * s
                        ins = mm(ps[:, s, 0:(i + 1) * P], QT[r:r + 48, p, i * P:(i + 1) * P],
                                 KT[r:r + 48, p, 0:(i + 1) * P], start=False, stop=True, skip_group_check=True)
                elif kind == "tm":
                    _, b, i = step
                    pe.wait_ge(maxed, NTH[("mx", b, i, AH // 2 - 1)])
                    claim(step)
                    p16 = psum16(step)
                    for p in range(AH // 2):
                        ins = nc.tensor.transpose(p16[:, p * P:(p + 1) * P], ST[:, i, 0, 2 * p:2 * p + 2, :], ident16)
                elif kind == "se":
                    _, b, g, j, hf = step
                    pe.wait_ge(q_max, NTH[("tm", b, TB - 1)])
                    claim(step)
                    for s in range(2):
                        r, p = 64 * s, 2 * g + hf
                        ins = mm(ps[:, s, 0:(TB - j) * P], KT[r:r + 64, p, j * P:(j + 1) * P],
                                 QT[r:r + 64, p, j * P:TB * P], start=True, stop=True)
                elif kind == "pv":
                    _, b, g, j = step
                    pe.wait_ge(causal, NTH[("se", b, g, j, 1)])
                    if j == 0:
                        claim(step)
                    for s in range(4):
                        ins = mm(ps[32 * s:32 * s + 32, j * P:TB * P], V[:, j, 4 * g + s, :],
                                 PE1[:, j % 2, s, 0:(TB - j) * P], start=(j == 0), stop=(j == TB - 1))
                elif kind == "ya":
                    _, b, i = step
                    pe.wait_ge(yu, NTH[("pv", b, AH // 4 - 1, TB - 1)] // TB)
                    claim(step)
                    for g in range(AH // 4):
                        ins = nc.tensor.transpose(ps[:, g * P:(g + 1) * P], YU[:, g, i * P:(i + 1) * P], ident)
                elif kind == "rt":
                    t = step[1]
                    pe.wait_ge(x_rest, NTH[("tx", 2, t)])
                    pe.wait_ge(rest_cut, len(PIECES))
                    claim(step)
                    w = ws[:, :, W_ROUT:W_TOT].rearrange("p a (k n) -> p a k n", k=KD)
                    ins = cut_product([(ps[:, 0:NR], 0)], x_tiles(t), lambda k, b, c: w[:, b, k, :], True)
                elif kind == "mu":
                    _, t, c = step
                    claim(step)
                    w = ws[:, :, W_UP:W_DOWN].rearrange("p a (k c u n) -> p a k c u n", k=KD, c=MC, u=2)
                    ins = cut_product([(ps[:, 0, 0:MCW], 0), (ps[:, 1, 0:MCW], 1)], x_tiles(t),
                                      lambda k, b, u: w[:, b, k, c, u, :], True)
                elif kind == "mt":
                    _, t, part = step
                    if part == 0:
                        pe.wait_ge(mu_h, NTH[("mu", t, 2)])
                        claim(step)
                        for k in range(8):
                            ins = nc.tensor.transpose(ps[:, k // 4, (k % 4) * P:(k % 4 + 1) * P], H[:, k * P:(k + 1) * P], ident)
                    elif part == 1:
                        pe.wait_ge(mu_h, NTH[("mu", t, MC - 1)])
                        claim(step)
                        for k in range(8):
                            ins = nc.tensor.transpose(ps[:, k // 4, (k % 4) * P:(k % 4 + 1) * P],
                                                      H[:, (8 + k) * P:(9 + k) * P], ident)
                    else:
                        claim(step)
                        ins = nc.tensor.transpose(ps[0:LAST, 0:P], H[:, 16 * P:HID], ident)
                elif kind == "md":
                    t = step[1]
                    pe.wait_ge(mt_rest, NTH[("mt", t, 2)])
                    claim(step)
                    w = ws[:, :, W_DOWN:W_ROUT].rearrange("p a (k n) -> p a k n", k=HK)

                    def rows(k):
                        return LAST if k == HK - 1 else P
                    ins = cut_product([(ps[:, 0:D], 0)], [[HT[0:rows(k), t % 2, a, k, :] for a in range(2)] for k in range(HK)],
                                      lambda k, b, c: w[0:rows(k), b, k, :], True)
                ins.then_inc(pe_done, 1)

        @block.scalar
        def _(act):
            for step in SCHEDULE:
                kind, n = step[0], NTH[step]
                ps = psum(step) if kind in RING_OF else None
                if kind == "split":
                    i = step[1]
                    name, _, cols, first = PIECES[i]
                    act.wait_ge(piece_in[i], 16)
                    dst = (XT[:, 0, :, :].rearrange("p k t -> p (k t)") if name == "xT" else ws[:, 0, :])[:, first:first + cols]
                    nc.scalar.activation(dst, stage[:, i % NSTAGE, 0:cols], ACT.Copy,
                                         scale=SA if name == "xT" else SW).then_inc(head_cut, 1)
                elif kind == "wsum":
                    act.wait_ge(raw_in, 48)
                    act.wait_ge(ready0, 3)
                    for i in range(2):
                        nc.scalar.activation(Q12[:, :, i * F0:(i + 1) * F0], raw12[:, :, i * F0:(i + 1) * F0], ACT.Abs,
                                             accum_out=gs[:, i:i + 1])
                    nc.scalar.activation(Q3[:, 0:FM - 1, :], raw3[:, 0:FM - 1, :], ACT.Abs, accum_out=gs[:, 2:3])
                    nc.scalar.activation(Q3[0:LAST, FM - 1, :], raw3[0:LAST, FM - 1, :], ACT.Abs,
                                         accum_out=gs[0:LAST, 3:4]).then_inc(sums, 1)
                elif kind == "proj":
                    t = step[1]
                    act.wait_ge(evac0, t + 1)
                    if t >= 2:
                        act.wait_ge(gates, t - 1)
                    nc.scalar.activation(TH[:, t % 2, :], VG[:, t % 4, D:2 * D], ACT.Tanh, scale=0.5).then_inc(tanh0, 1)
                elif kind == "tqk":
                    t = step[1]
                    act.wait_ge(pe_done, PLACE[step][3])
                    ins = nc.scalar.activation(QKT[:, t % 2, :, :].rearrange("p a b -> p (a b)"), ps[:, :], ACT.Copy)
                    ins.then_inc(qkT, 1)
                elif kind == "ty":
                    act.wait_ge(pe_done, PLACE[step][3])
                    nc.scalar.activation(YT[:, 0, :], ps[:, 0:D], ACT.Copy, scale=SA * (1.0 if step[1] else 0.5)).then_inc(y_head, 1)
                elif kind == "tx":
                    t = step[2]
                    act.wait_ge(pe_done, PLACE[step][3])
                    nc.scalar.activation(XT[:, 0, :, t * P:(t + 1) * P], ps[:, 0:D].rearrange("p (k t) -> p k t", k=KD),
                                         ACT.Copy, scale=SA).then_inc(x_head, 1)
                elif kind == "up":
                    m = step[2]
                    rows = P if m < FM - 1 else LAST
                    act.wait_ge(pe_done, PLACE[step][3])
                    if n > 2:
                        act.wait_ge(hidden, n - 2)
                    nc.scalar.activation(THF[0:rows, n % 2, :], ps[0:rows, 0, :], ACT.Tanh, scale=0.5 / SA).then_inc(up_tanh, 1)
                elif kind == "cut":
                    m = step[2]
                    rows = P if m < FM - 1 else LAST
                    act.wait_ge(hidden, n)
                    if step == ("cut", 1, 0):
                        act.wait_ge(pe_done, PLACE[("dn", TB - 1)][3])
                    nc.scalar.activation(HT0[0:rows, 0, m, :], HF[0:rows, n % 2, :], ACT.Copy).then_inc(h_head, 1)
                elif kind == "qk":
                    i = step[2]
                    act.wait_ge(qk_evac, n)
                    if n == 1:
                        act.wait_ge(st_init, 1)
                    nc.scalar.activation(ST[:, i, :, :, 0:16], QK32[:, n % 2], ACT.Copy).then_inc(st_head, 1)
                elif kind == "st":
                    i = step[2]
                    nc.scalar.activation(ST[:, i, 0, :, 16:32], QK32[:, n % 2, 0], ACT.Copy)
                    nc.scalar.activation(ST[:, i, 1, :, 32:48], QK32[:, n % 2, 1], ACT.Copy).then_inc(st_second, 1)
                elif kind == "tq":
                    i = step[2]
                    act.wait_ge(pe_done, PLACE[step][3])
                    nc.scalar.activation(QT[:, :, i * P:(i + 1) * P],
                                         psum16(step)[:, 0, :].rearrange("p (a b) -> p a b", b=P), ACT.Copy).then_inc(q_up, 1)
                elif kind == "tm":
                    i = step[2]
                    act.wait_ge(pe_done, PLACE[step][3])
                    ins = nc.scalar.activation(QT[:, :, i * P:(i + 1) * P],
                                               psum16(step).rearrange("p (a b) -> p a b", b=P), ACT.Copy)
                    ins.then_inc(q_max, 1)
                elif kind == "se":
                    _, b, g, j, hf = step
                    act.wait_ge(pe_done, PLACE[step][3])
                    w = (TB - j) * P
                    ins = nc.scalar.activation(PE1[:, j % 2, 2 * hf:2 * hf + 2, 0:w], ps[:, :, 0:w], ACT.Exp, scale=1.0 / 16)
                    ins.then_inc(exped, 1)
                elif kind == "pv" and step[3] == TB - 1:
                    act.wait_ge(pe_done, PLACE[step][3])
                    nc.scalar.activation(YU[:, step[2], :], ps[:, :], ACT.Copy).then_inc(yu, 1)
                elif kind == "rc":
                    t = step[1]
                    r = small[:, t % 2, :]
                    act.wait_ge(logits, n)
                    nc.scalar.activation(r[:, 24:32], r[:, 16:24], ACT.Exp, bias=r[:, 9:10], accum_out=r[:, 32:33])
                    nc.scalar.activation(r[:, 33:34], r[:, 8:9], ACT.Tanh, scale=0.5).then_inc(r_exp, 1)
                elif kind == "mu":
                    act.wait_ge(pe_done, PLACE[step][3])
                    if n > 2:
                        act.wait_ge(mu_h, n - 2)
                    nc.scalar.activation(TG[:, n % 2, :], ps[:, 0, 0:MCW], ACT.Tanh, scale=0.5 * UN).then_inc(mu_tanh, 1)
                elif kind == "mt":
                    _, t, part = step
                    act.wait_ge(pe_done, PLACE[step][3])
                    if part < 2:
                        nc.scalar.activation(HT[:, t % 2, 0, 8 * part:8 * part + 8, :].rearrange("p a b -> p (a b)"),
                                             ps[:, :, :].rearrange("p a b -> p (a b)"), ACT.Copy).then_inc(mt_head, 1)
                    else:
                        nc.scalar.activation(HT[0:LAST, t % 2, 0, 16, :], ps[0:LAST, 0:P], ACT.Copy).then_inc(mt_head, 1)

        @block.vector
        def _(dve):
            v = nc.vector
            count = [0]

            def mark(ins):
                count[0] += 1
                ins.then_inc(dve_order, 1)
                return count[0]

            def link(ins):
                dve.wait_ge(dve_order, mark(ins))

            def finished(step):
                dve.wait_ge(pe_done, PLACE[step][3])

            def norm_input(step, ps, scale):
                layer, t = LAYER.get(step[0], step[1]), step[-1]
                n = NTH[("ln", layer, t)]
                r = n % 3
                finished(step)
                if layer == 0:
                    dve.wait_ge(resid, t + 1)
                elif layer == 2:
                    dve.wait_ge(resid, NT + NTH[("qk", t // TB, t % TB)])
                v.scalar_tensor_tensor(Z[:, n % 2, :], ps[:, 0:D], scale, X[:, t, :], ALU.mult, ALU.add).then_inc(z_ready, 1)
                dve.wait_ge(z_ready, n)
                link(v.bn_stats(stats[:, r, :], Z[:, n % 2, :]))
                link(v.bn_aggr(mv[:, r, :], stats[:, r, :]))
                v.tensor_scalar(veps[:, r:r + 1], mv[:, r, 1:2], EPS, None, ALU.add).then_inc(ln_var, 1)

            first_term = {}
            for step in SCHEDULE:
                kind, n = step[0], NTH[step]
                ps = psum(step) if kind in RING_OF else None
                if kind == "split":
                    i = step[1]
                    name, _, cols, first = PIECES[i]
                    dst = (XT[:, :, :, :].rearrange("p a k t -> p a (k t)") if name == "xT" else ws)
                    dve.wait_ge(head_cut, n)
                    v.scalar_tensor_tensor(dst[:, 1, first:first + cols], stage[:, i % NSTAGE, 0:cols],
                                           SA if name == "xT" else SW, dst[:, 0, first:first + cols],
                                           ALU.mult, ALU.subtract).then_inc(rest_cut, 1)
                elif kind == "tables":
                    dve.wait_ge(con_in, 16)
                    dec = con[:, C_DEC:C_DEC + 2 * RH].unsqueeze(1).unsqueeze(3).to_broadcast([P, TB, 2 * RH, RD // 2])
                    for tab, at in ((tab_cos, C_COS), (tab_sin, C_SIN)):
                        src = con[:, at:at + TB * RD // 2].rearrange("p (c j) -> p c j", c=TB)
                        ins = v.tensor_tensor(tab, src.unsqueeze(2).to_broadcast([P, TB, 2 * RH, RD // 2]), dec, ALU.mult)
                    ins.then_inc(tables, 1)
                elif kind == "proj":
                    t = step[1]
                    finished(step)
                    if t == 0:
                        dve.wait_ge(row0_in, 16)
                        dve.wait_ge(tables, 1)
                    if t >= 2:
                        dve.wait_ge(rot2, t - 1)
                    v.scalar_tensor_tensor(QK0[:, t % 2], ps[:, 0, :], UN, row0[:, 0:2 * D], ALU.mult, ALU.add)
                    v.scalar_tensor_tensor(VG[:, t % 4], ps[:, 1, :], UN, row0[:, 2 * D:4 * D],
                                           ALU.mult, ALU.add).then_inc(evac0, 1)
                    dve.wait_ge(evac0, t + 1)
                    qk = QK0[:, t % 2].rearrange("p (s u j) -> p s u j", u=2, j=RD // 2)
                    cos = tab_cos[:, t % TB].unsqueeze(2).to_broadcast([P, 2 * RH, 2, RD // 2])
                    first_term[t] = mark(v.tensor_tensor(R1[:, t % 2].rearrange("p (s u j) -> p s u j", u=2, j=RD // 2),
                                                         qk, cos, ALU.mult))
                elif kind == "rot":
                    t = step[1]
                    dve.wait_ge(dve_order, first_term[t])
                    dve.wait_ge(rot2, t + 1)
                    a, b, o = (w[:, t % 2].rearrange("p (s u j) -> p s u j", u=2, j=RD // 2) for w in (R1, R2, ROT))
                    v.tensor_tensor(o[:, :, 0], a[:, :, 0], b[:, :, 0], ALU.subtract)
                    v.tensor_tensor(o[:, :, 1], a[:, :, 1], b[:, :, 1], ALU.add).then_inc(rotated, 1)
                elif kind == "sc":
                    _, t, hf = step
                    finished(step)
                    keep = con[:, C_KEEP:C_KEEP + P].unsqueeze(1).unsqueeze(1).to_broadcast([P, 2, 2, P])
                    v.tensor_tensor(PT[:, t % 2, hf], ps[:, :, 0:2 * P].rearrange("p s (g q) -> p s g q", g=2), keep,
                                    ALU.mult).then_inc(pT, 1)
                elif kind == "kv":
                    t = step[1]
                    c = t % TB
                    finished(step)
                    if t == 0:
                        dve.wait_ge(block_in, 16)
                    if c == 0:
                        v.tensor_tensor(TS[:, 0], ps[:, 0:D], block_g, ALU.mult).then_inc(state, 1)
                    else:
                        link(v.tensor_tensor(KVM, ps[:, 0:D], block_g, ALU.mult))
                        for g in range(2):
                            w = slice(g * P, (g + 1) * P)
                            ins = v.scalar_tensor_tensor(TS[:, c, w], TS[:, c - 1, w], con[:, C_G128 + g:C_G128 + g + 1],
                                                         KVM[:, w], ALU.mult, ALU.add)
                        ins.then_inc(state, 1)
                    dve.wait_ge(state, n)
                elif kind == "ret":
                    t = step[1]
                    finished(step)
                    sm = gsmall[:, t % 2]
                    heads = ps[:, 0:D].rearrange("p (h d) -> p h d", h=RH)
                    cent = CENT[:, t % 2].rearrange("p (h d) -> p h d", h=RH)
                    link(v.tensor_reduce(sm[:, 0], heads, AX.X, ALU.add))
                    link(v.tensor_scalar(sm[:, 1], sm[:, 0], -1.0 / RD, None, ALU.mult))
                    v.tensor_tensor(cent, heads, sm[:, 1].unsqueeze(2).to_broadcast([P, RH, RD]), ALU.add)\
                        .then_inc(centered, 1)
                    dve.wait_ge(centered, n)
                    link(v.tensor_tensor(SQ, CENT[:, t % 2], CENT[:, t % 2], ALU.mult))
                    link(v.tensor_reduce(sm[:, 2], SQ.rearrange("p (h d) -> p h d", h=RH), AX.X, ALU.add))
                    v.tensor_scalar(sm[:, 2], sm[:, 2], 1.0 / RD, EPS, ALU.mult, ALU.add).then_inc(gvar, 1)
                elif kind == "gn":
                    t = step[1]
                    y = Y[:, NTH[("ty", 0, t)] % 2, :]
                    dve.wait_ge(grstd, n)
                    dve.wait_ge(gates, n)
                    link(v.tensor_tensor(y.rearrange("p (h d) -> p h d", h=RH),
                                         CENT[:, t % 2].rearrange("p (h d) -> p h d", h=RH),
                                         gsmall[:, t % 2, 3].unsqueeze(2).to_broadcast([P, RH, RD]), ALU.mult))
                    link(v.tensor_tensor(y, y, GA[:, t % 3], ALU.mult))
                    v.tensor_tensor(y, y, GC[:, t % 3], ALU.add).then_inc(y_ready, 1)
                elif kind == "ty":
                    finished(step)
                    dve.wait_ge(y_head, n)
                    v.scalar_tensor_tensor(YT[:, 1, :], ps[:, 0:D], SA * (1.0 if step[1] else 0.5), YT[:, 0, :],
                                           ALU.mult, ALU.subtract).then_inc(y_rest, 1)
                elif kind == "wo":
                    norm_input(step, ps, UN)
                elif kind == "dn":
                    norm_input(step, ps, 0.5 / SA)
                elif kind == "md":
                    norm_input(step, ps, UN)
                elif kind == "ln":
                    t, r = step[2], n % 3
                    dve.wait_ge(ln_rstd, n)
                    v.tensor_scalar(X[:, t, :], Z[:, n % 2, :], mv[:, r, 0:1], rstd[:, r:r + 1],
                                    ALU.subtract, ALU.mult).then_inc(ln_done, 1)
                    dve.wait_ge(ln_done, n)
                elif kind == "tx":
                    t = step[2]
                    finished(step)
                    dve.wait_ge(x_head, n)
                    w = slice(t * P, (t + 1) * P)
                    v.scalar_tensor_tensor(XT[:, 1, :, w], ps[:, 0:D].rearrange("p (k t) -> p k t", k=KD), SA,
                                           XT[:, 0, :, w], ALU.mult, ALU.subtract).then_inc(x_rest, 1)
                elif kind == "gsum":
                    finished(step)
                    link(v.tensor_scalar(thr[:, 0, 0:3], ps[:, 0:3], 0.5 / (D * F0), 0.5e-8, ALU.mult, ALU.add))
                    link(v.scalar_tensor_tensor(thr[:, 0, 2:3], ps[:, 3:4], 0.5 / (D * F0), thr[:, 0, 2:3], ALU.mult, ALU.add))
                    v.tensor_scalar(thr[:, 1, :], thr[:, 0, :], -1.0, None, ALU.mult).then_inc(thresholds, 1)
                    dve.wait_ge(thresholds, 1)
                elif kind == "quant":
                    i = step[1]
                    if i < 2:
                        parts = [(P, raw12[:, :, i * F0:(i + 1) * F0], Q12[:, :, i * F0:(i + 1) * F0])]
                    else:
                        parts = [(P, raw3[:, 0:FM - 1, :], Q3[:, 0:FM - 1, :]),
                                 (LAST, raw3[0:LAST, FM - 1, :], Q3[0:LAST, FM - 1, :])]
                    for rows, raw, q in parts:
                        link(v.tensor_scalar(q, raw, thr[0:rows, 1, i:i + 1], None, ALU.is_lt))
                        ins = v.scalar_tensor_tensor(q, raw, thr[0:rows, 0, i:i + 1], q, ALU.is_gt, ALU.subtract)
                    ins.then_inc(quant, 1)
                elif kind == "up":
                    m = step[2]
                    rows = P if m < FM - 1 else LAST
                    finished(step)
                    dve.wait_ge(up_tanh, n)
                    if n == 1:
                        dve.wait_ge(quant, 3)
                    if n > 2:
                        dve.wait_ge(h_head, n - 2)
                        dve.wait_ge(h_rest, n - 2)
                    v.scalar_tensor_tensor(HF[0:rows, n % 2, :], THF[0:rows, n % 2, :], 1.0, ps[0:rows, 1, :],
                                           ALU.add, ALU.mult).then_inc(hidden, 1)
                elif kind == "qk":
                    i = step[2]
                    finished(step)
                    if n == 1:
                        dve.wait_ge(row1_in, 16)
                        link(v.tensor_scalar(row1[:, D:2 * D], row1[:, D:2 * D], 4.0, None, ALU.mult))
                        v.memset(ST[:, :, :, :, 48:64], 0.0)
                        v.memset(V[:, :, :, 16:32], 0.0).then_inc(st_init, 1)
                        dve.wait_ge(st_init, 1)
                        v.memset(ST[:, :, 1, :, 48:49], 1.0)
                        v.memset(V[:, :, :, 16:17], 1.0).then_inc(st_init, 1)
                    if n > 2:
                        dve.wait_ge(st_second, n - 2)
                    v.scalar_tensor_tensor(QK32[:, n % 2, 0].rearrange("p a b -> p (a b)"), ps[:, 0, 0:D], UN, row1[:, 0:D],
                                           ALU.mult, ALU.add)
                    v.scalar_tensor_tensor(QK32[:, n % 2, 1].rearrange("p a b -> p (a b)"), ps[:, 0, D:2 * D], 4 * UN,
                                           row1[:, D:2 * D], ALU.mult, ALU.add)
                    v.scalar_tensor_tensor(V[:, i, :, 0:16], ps[:, 1, 0:D].rearrange("p (h d) -> p h d", h=AH), UN,
                                           row1[:, 2 * D:3 * D].rearrange("p (h d) -> p h d", h=AH),
                                           ALU.mult, ALU.add).then_inc(qk_evac, 1)
                elif kind == "st":
                    i = step[2]
                    dve.wait_ge(st_head, n)
                    v.tensor_tensor(ST[:, i, 0, :, 32:48], QK32[:, n % 2, 0], ST[:, i, 0, :, 0:16], ALU.subtract)
                    v.tensor_tensor(ST[:, i, 1, :, 16:32], QK32[:, n % 2, 1], ST[:, i, 1, :, 0:16], ALU.subtract)\
                        .then_inc(st_rest, 1)
                elif kind == "tq":
                    i = step[2]
                    finished(step)
                    v.tensor_copy(KT[:, :, i * P:(i + 1) * P],
                                  psum16(step)[:, 1, :].rearrange("p (a b) -> p a b", b=P)).then_inc(k_up, 1)
                elif kind == "mx":
                    _, b, i, p = step
                    finished(step)
                    v.tensor_reduce(ST[:, i, 0, 2 * p:2 * p + 2, 48], ps[:, :, 0:(i + 1) * P], AX.X, ALU.max,
                                    negate=True).then_inc(maxed, 1)
                elif kind == "ya":
                    _, b, i = step
                    m = NTH[("ty", 2, b * TB + i)]
                    finished(step)
                    heads = ps[:, :].rearrange("p (h d) -> p h d", h=AH)
                    link(v.reciprocal(rden[:, m % 2].unsqueeze(2), heads[:, :, AD:AD + 1]))
                    v.tensor_tensor(Y[:, m % 2].rearrange("p (h d) -> p h d", h=AH), heads[:, :, 0:AD],
                                    rden[:, m % 2].unsqueeze(2).to_broadcast([P, AH, AD]), ALU.mult).then_inc(y_ready, 1)
                elif kind == "rt":
                    t = step[1]
                    r = small[:, t % 2, :]
                    finished(step)
                    v.tensor_scalar(r[:, 0:NR], ps[:, 0:NR], UN, None, ALU.mult).then_inc(logit_read, 1)
                    dve.wait_ge(logit_read, n)
                    link(v.max(r[:, 16:24], r[:, 0:NE]))
                    link(v.max_index(small_i[:, t % 2, :], r[:, 16:24], r[:, 0:NE]))
                    v.tensor_scalar(r[:, 9:10], r[:, 16:17], -1.0, None, ALU.mult).then_inc(logits, 1)
                    link(v.tensor_copy(r[:, 34:36], small_i[:, t % 2, 0:2]))
                elif kind == "rc":
                    t = step[1]
                    r = small[:, t % 2, :]
                    scale = 0.5 * SA * UN * UN
                    iota = con[:, C_IOTA:C_IOTA + NE]
                    dve.wait_ge(r_exp, n)
                    link(v.reciprocal(r[:, 36:37], r[:, 32:33]))
                    link(v.tensor_scalar(r[:, 37:39], r[:, 24:26], r[:, 36:37], scale, ALU.mult, ALU.mult))
                    v.tensor_scalar(r[:, 40:48], iota, r[:, 34:35], r[:, 37:38], ALU.is_equal, ALU.mult)
                    link(v.tensor_scalar(r[:, 48:56], iota, r[:, 35:36], r[:, 38:39], ALU.is_equal, ALU.mult))
                    v.tensor_tensor(r[:, 48:56], r[:, 48:56], r[:, 40:48], ALU.add)
                    link(v.tensor_scalar(r[:, 56:57], r[:, 33:34], 1.0, 0.5 * scale, ALU.add, ALU.mult))
                elif kind == "mu":
                    _, t, c = step
                    finished(step)
                    dve.wait_ge(mu_tanh, n)
                    if n > 2:
                        dve.wait_ge(mu_h, n - 2)
                    link(v.scalar_tensor_tensor(AG[:, n % 2, :], TG[:, n % 2, :], 1.0, ps[:, 0, 0:MCW], ALU.add, ALU.mult))
                    coef_at = [(0, FE, 2 * c), (FE, FE, 2 * c + 1)] if 2 * c < NE else [(0, MCW, NE)]
                    for at, w, e in coef_at:
                        ins = v.scalar_tensor_tensor(H[:, c * MCW + at:c * MCW + at + w], AG[:, n % 2, at:at + w],
                                                     small[:, t % 2, 48 + e:49 + e], ps[:, 1, at:at + w], ALU.mult, ALU.mult)
                    ins.then_inc(mu_h, 1)
                elif kind == "mt":
                    _, t, part = step
                    finished(step)
                    dve.wait_ge(mt_head, n)
                    if part < 2:
                        k = slice(8 * part, 8 * part + 8)
                        v.tensor_tensor(HT[:, t % 2, 1, k, :].rearrange("p a b -> p (a b)"),
                                        ps[:, :, :].rearrange("p a b -> p (a b)"),
                                        HT[:, t % 2, 0, k, :].rearrange("p a b -> p (a b)"), ALU.subtract).then_inc(mt_rest, 1)
                    else:
                        v.tensor_tensor(HT[0:LAST, t % 2, 1, 16, :], ps[0:LAST, 0:P], HT[0:LAST, t % 2, 0, 16, :],
                                        ALU.subtract).then_inc(mt_rest, 1)

        @block.gpsimd
        def _(pool):
            g_ = nc.gpsimd
            count = [0]

            def link(ins):
                count[0] += 1
                ins.then_inc(pool_order, 1)
                pool.wait_ge(pool_order, count[0])

            g_.memset(ones, 1.0).then_inc(ready0, 1)
            g_.memset(gs[:, :], 0.0).then_inc(ready0, 1)
            g_.memset(half[:, :], -0.5).then_inc(ready0, 1)
            pool.wait_ge(ready0, 3)
            for step in SCHEDULE:
                kind, n = step[0], NTH[step]
                if kind == "proj":
                    t = step[1]
                    if t == 0:
                        pool.wait_ge(tables, 1)
                        pool.wait_ge(row0_in, 16)
                        pool.wait_ge(x_in, 16)
                    if t >= 2:
                        pool.wait_ge(rotated, t - 1)
                    pool.wait_ge(evac0, t + 1)
                    qk = QK0[:, t % 2].rearrange("p (s u j) -> p s u j", u=2, j=RD // 2)
                    o = R2[:, t % 2].rearrange("p (s u j) -> p s u j", u=2, j=RD // 2)
                    g_.tensor_tensor(o[:, :, 0], qk[:, :, 1], tab_sin[:, t % TB], ALU.mult)
                    g_.tensor_tensor(o[:, :, 1], qk[:, :, 0], tab_sin[:, t % TB], ALU.mult).then_inc(rot2, 1)
                    pool.wait_ge(tanh0, t + 1)
                    if t >= 3:
                        pool.wait_ge(y_ready, NTH[("ty", 0, t - 3)])
                    gate = VG[:, t % 4, D:2 * D]
                    link(g_.tensor_tensor(GC[:, t % 3], TH[:, t % 2], gate, ALU.mult))
                    link(g_.tensor_tensor(GC[:, t % 3], GC[:, t % 3], gate, ALU.add))
                    link(g_.tensor_tensor(GA[:, t % 3], GC[:, t % 3], row0[:, 5 * D:6 * D], ALU.mult))
                    g_.tensor_tensor(GC[:, t % 3], GC[:, t % 3], row0[:, 6 * D:7 * D], ALU.mult).then_inc(gates, 1)
                    g_.tensor_tensor(X[:, t, :], X[:, t, :], row0[:, 4 * D:5 * D], ALU.add).then_inc(resid, 1)
                elif kind == "ret":
                    t = step[1]
                    pool.wait_ge(gvar, n)
                    g_.tensor_tensor(gsmall[:, t % 2, 3], gsmall[:, t % 2, 2], half[:, 0:RH], ALU.pow).then_inc(grstd, 1)
                elif kind in ("wo", "dn", "md"):
                    m = NTH[("ln", LAYER.get(kind, step[1]), step[-1])]
                    r = m % 3
                    pool.wait_ge(ln_var, m)
                    g_.tensor_tensor(rstd[:, r:r + 1], veps[:, r:r + 1], half[:, 0:1], ALU.pow).then_inc(ln_rstd, 1)
                elif kind == "cut":
                    m = step[2]
                    rows = P if m < FM - 1 else LAST
                    pool.wait_ge(h_head, n)
                    g_.tensor_tensor(HT0[0:rows, 1, m, :], HF[0:rows, n % 2, :], HT0[0:rows, 0, m, :],
                                     ALU.subtract).then_inc(h_rest, 1)
                elif kind == "qk":
                    _, b, i = step
                    t = b * TB + i
                    if n == 1:
                        pool.wait_ge(row1_in, 16)
                    pool.wait_ge(pe_done, PLACE[("tx", 1, t)][3])
                    g_.tensor_tensor(X[:, t, :], X[:, t, :], row1[:, 3 * D:4 * D], ALU.add).then_inc(resid, 1)
                elif kind == "se":
                    _, b, g, j, hf = step
                    pool.wait_ge(exped, n)
                    part = PE1[:, j % 2, 2 * hf:2 * hf + 2, 0:P]
                    g_.affine_select(out=part, in_=part, compare_op=ALU.is_ge, fill=0.0, base=0,
                                     pattern=[[0, 2], [1, P]], channel_multiplier=-1).then_inc(causal, 1)


def constants():
    gammas = (1.0 - np.exp(np.linspace(np.log(1 / 32), np.log(1 / 64), RH))).astype(np.float32).astype(np.float64)
    con = np.zeros((P, C_TOT))
    part = np.arange(P)
    block = np.zeros((P, D))
    con[:, C_ID:C_ID + P] = np.eye(P)
    con[:, C_KEEP:C_KEEP + P] = part[None, :] >= part[:, None]
    for g in range(2):
        own = gammas[4 * g + part // RD] ** P
        block[:, g * P:(g + 1) * P] = own[:, None] * (part[:, None] // RD == part[None, :] // RD)
        con[:, C_G128 + g] = own
    thetas = (1.0 / np.float32(10000.0) ** np.linspace(0.0, 1.0, RD // 2, dtype=np.float32)).astype(np.float32)
    for c in range(TB):
        angle = ((c * P + part).astype(np.float32)[:, None] * thetas[None, :]).astype(np.float32).astype(np.float64)
        con[:, C_COS + c * RD // 2:C_COS + (c + 1) * RD // 2] = np.cos(angle)
        con[:, C_SIN + c * RD // 2:C_SIN + (c + 1) * RD // 2] = np.sin(angle)
    con[:, C_DEC:C_DEC + RH] = gammas[None, :] ** part[:, None]
    con[:, C_DEC + RH:C_DEC + 2 * RH] = gammas[None, :] ** -part[:, None].astype(np.float64) / np.sqrt(RD)
    con[:, C_IOTA:C_IOTA + NE] = np.arange(NE)
    con16 = np.zeros((P, 2 * P))
    con16[:, 0:P] = np.eye(P)
    con16[:, P:2 * P] = np.where(part[None, :] > part[:, None], -60000.0, 0.0)
    return con.astype(np.float32), con16.astype(np.float16), block.astype(np.float32)


def tiled(w):
    k = w.shape[0] // P
    return np.ascontiguousarray(w.reshape(k, P, -1).transpose(1, 0, 2).reshape(P, -1))


def layout(i):
    turn = np.concatenate([np.concatenate([np.arange(0, RD, 2), np.arange(1, RD, 2)]) + h * RD for h in range(RH)])
    x = i["L0_attn_x"].reshape(NT * P, D)
    a = {"xT": tiled(x.T), "x": np.ascontiguousarray(x)}
    a["wqkvg"] = tiled(np.concatenate([i["L0_attn_w_q"][:, turn], i["L0_attn_w_k"][:, turn], i["L0_attn_w_v"],
                                       i["L0_attn_w_g"]], 1))
    a["wo"] = np.concatenate([tiled(i["L0_attn_w_o"]), tiled(i["L1_attn_Wo"])], 1)
    a["wqkv1"] = tiled(np.concatenate([i[f"L1_attn_W{c}"].transpose(1, 0, 2).reshape(D, D) for c in "qkv"], 1))
    gate = np.concatenate([i["L1_ffn_We_gate_up"][e, :, :FE] for e in range(NE)] + [i["L1_ffn_Ws_gate_up"][:, :FS]], 1)
    up = np.concatenate([i["L1_ffn_We_gate_up"][e, :, FE:] for e in range(NE)] + [i["L1_ffn_Ws_gate_up"][:, FS:]], 1)
    a["wup"] = tiled(np.stack([gate.reshape(D, MC, MCW), up.reshape(D, MC, MCW)], 2).reshape(D, -1))
    down = np.concatenate([i["L1_ffn_We_down"].reshape(NE * FE, D), i["L1_ffn_Ws_down"]], 0)
    a["wdown"] = tiled(down[:(HK - 1) * P])
    last = np.concatenate([down[(HK - 1) * P:], np.zeros((P - LAST, D), np.float32)], 0)
    a["wtail"] = np.concatenate([last, tiled(np.concatenate([i["L1_ffn_W_router"].T, i["L1_ffn_W_sgate"].T], 1))], 1)
    a["w12"] = np.concatenate([i["L0_ffn_w1"].T, i["L0_ffn_w2"].T], 1)
    a["w3"] = np.ascontiguousarray(i["L0_ffn_w3"].T)
    a["rows0"] = np.concatenate([i["L0_attn_b_q"][turn], i["L0_attn_b_k"][turn], i["L0_attn_b_v"], i["L0_attn_b_g"],
                                 i["L0_attn_b_o"], i["L0_attn_gn_weight"], i["L0_attn_gn_bias"]])
    a["rows1"] = np.concatenate([i["L1_attn_bq"].reshape(-1), i["L1_attn_bk"].reshape(-1), i["L1_attn_bv"].reshape(-1),
                                 i["L1_attn_bo"]])
    a["consts"], a["consts16"], a["block_decay"] = constants()
    return a


def kernel(**inputs):
    import concourse.bacc as _bacc
    from concourse.bass_utils import run_bass_kernel_spmd as _run

    nc = _bacc.Bacc("TRN2", target_bir_lowering=False, num_devices=1)
    arrays, args = {}, []
    for name, a in layout({k: np.asarray(v) for k, v in inputs.items()}).items():
        a = np.ascontiguousarray(a)
        arrays[f"in_{name}"] = a
        args.append(nc.dram_tensor(f"in_{name}", a.shape, mybir.dt.from_np(a.dtype), kind="ExternalInput").ap())
    out = nc.dram_tensor("out", (NT * P, D), mybir.dt.float32, kind="ExternalOutput").ap()
    build_two_layers(nc, *args, out)
    r = _run(nc, [arrays], core_ids=[0])
    return r.results[0]["out"].reshape(NB, TB * P, D)
```

```python
import concourse.bass as bass
from concourse import mybir
from contextlib import ExitStack
import numpy as np

P = 128
D = 256
KD = D // P
NT = 8
NB = 2
TB = NT // NB
RH, RD = 8, 32
AH, AD = 16, 16
F0 = 704
FM = 6
NE, FE, FS = 8, 176, 704
HID = NE * FE + FS
MC, MCW = 6, 352
HK = (HID + P - 1) // P
LAST = F0 % P
EPS = 1e-5

SA = 16.0
SW = 64.0
UN = 1.0 / (SA * SW)

W_QKVG = 0
W_O0 = W_QKVG + KD * 4 * D
W_O1 = W_O0 + KD * D
W_QKV1 = W_O1 + KD * D
W_UP = W_QKV1 + KD * 3 * D
W_DOWN = W_UP + KD * 2 * HID
W_TAIL = W_DOWN + (HK - 9) * D
W_ROUT = W_TAIL + D
NR = NE + 1
W_TOT = W_ROUT + KD * NR
STAGE = 1024
NSTAGE = 3


C_ID = 0
C_G128 = C_ID + P
C_REST = C_G128 + KD
C_COS = C_REST + 1
C_SIN = C_COS + TB * RD // 2
C_DEC = C_SIN + TB * RD // 2
C_IOTA = C_DEC + 2 * RH
C_TOT = C_IOTA + NE


def pieces():
    out = [("xT", 0, KD * TB * P, 0), ("wqkvg", 0, 4 * D, W_QKVG), ("wqkvg", 4 * D, 4 * D, W_QKVG + 4 * D),
           ("xT", KD * TB * P, KD * TB * P, TB * P)]
    at = [("wo", W_O0, 2 * KD * D, 1024),
          ("wqkv1", W_QKV1, KD * 3 * D, 768), ("wup", W_UP, KD * 2 * HID, STAGE),
          ("wdown", None, (HK - 1) * D, 1024), ("wtail", W_TAIL, D + KD * NR, STAGE)]
    for name, first, n, step in at:
        for a in range(0, n, step):
            at = first + a if name != "wdown" else a if a < 8 * D else W_DOWN + a - 8 * D
            out.append((name, a, min(step, n - a), at))
    return out


PIECES = pieces()


WEIGHT = {"proj": 2.6, "tqk": 0.4, "sc": 0.9, "kv": 0.4, "ret": 2.0, "ty": 0.2, "wo": 0.7, "tx": 0.2, "up": 1.7,
          "dn": 1.3, "qk": 2.2, "tq": 0.9, "mx": 0.5, "tm": 0.5, "se": 0.3, "pv": 0.8, "ya": 0.4, "rt": 0.1,
          "mu": 1.8, "mt": 0.5, "md": 5.6, "split": 0.3, "wsum": 0.3, "quant": 0.3}


def weave(a, b):
    cost = [[WEIGHT.get(step[0], 0.0) for step in steps] for steps in (a, b)]
    whole = [max(sum(c), 1e-9) for c in cost]
    i = j = 0
    spent = [0.0, 0.0]
    out = []
    while i < len(a) or j < len(b):
        if j == len(b) or (i < len(a) and spent[0] / whole[0] <= spent[1] / whole[1]):
            out.append(a[i])
            spent[0] += cost[0][i]
            i += 1
        else:
            out.append(b[j])
            spent[1] += cost[1][j]
            j += 1
    return out


def retention(turns):
    out = []
    for s in turns:
        for lag, kind in ((6, "ln"), (4, "gn"), (1, "rot"), (0, "proj"), (5, "wo"), (6, "tx"), (4, "ty"),
                          (1, "tqk"), (3, "ret"), (2, "sc0"), (2, "sc1"), (2, "kv")):
            t = s - lag
            if not 0 <= t < NT:
                continue
            if kind in ("ln", "tx", "ty", "wo"):
                out.append((kind, 0, t))
            elif kind in ("sc0", "sc1"):
                out.append(("sc", t, int(kind[2])))
            elif kind != "kv" or t % TB < TB - 1:
                out.append((kind, t))
    return out


def norm_tail(layer, tiles, product):
    out = []
    for s in range(len(tiles) + 2):
        if s >= 2 and layer < 3:
            out.append(("tx", layer, tiles[s - 2]))
        if s < len(tiles):
            out += product(tiles[s])
        if 1 <= s <= len(tiles):
            out.append(("ln", layer, tiles[s - 1]))
    return out


def ffn0(b):
    out = []
    for m in range(FM + 1):
        if m < FM:
            out.append(("up", b, m))
        if m:
            out.append(("cut", b, m - 1))
    return out + norm_tail(1, range(TB * b, TB * b + TB), lambda t: [("dn", t)])


def attention_inputs(b):
    out = []
    for s in range(TB + 1):
        if s < TB:
            out.append(("qk", b, s))
        if s:
            out += [("tq", b, s - 1)]
    return out


def attention_core(b):
    out = []
    for i in range(TB):
        out += [("mx", b, i, p) for p in range(AH // 2)]
        if i:
            out.append(("tm", b, i - 1))
    out.append(("tm", b, TB - 1))
    waiting = []
    for g in range(AH // 4):
        for j in range(TB):
            out += [("se", b, g, j, 0), ("se", b, g, j, 1)]
            waiting.append(("pv", b, g, j))
            if len(waiting) > 1:
                out.append(waiting.pop(0))
    return out + waiting


def attention_outputs(b):
    def product(t):
        more = [("ya", b, t % TB + 1)] if t % TB + 1 < TB else []
        return [("ty", 2, t)] + more + [("wo", 2, t)]
    return [("ya", b, 0)] + norm_tail(2, range(TB * b, TB * b + TB), product)


def experts():
    out = [("rt", 0)]
    for t in range(NT + 1):
        for c in range(MC):
            if t < NT:
                if c == 0:
                    out.append(("rc", t))
                out.append(("mu", t, c))
                if c == 3:
                    out.append(("mt", t, 0))
            if c == 1 and t:
                out += [("mt", t - 1, 1), ("mt", t - 1, 2)]
            if c == 2 and t:
                out.append(("md", t - 1))
            if c == 3 and t:
                out.append(("ln", 3, t - 1))
            if c == 4 and t + 1 < NT:
                out.append(("rt", t + 1))
    return out


def schedule():
    first = [("split", 0), ("split", 1), ("bias", 0), ("split", 2)]
    early = [("wsum", 0), ("wsum", 1), ("wsum", 2), ("gsum",), ("quant", 0), ("quant", 1), ("quant", 2), ("bias", 1)]
    splits = [("split", i) for i in range(5, len(PIECES))]
    half = len(splits) // 2
    moe = experts()
    at = moe.index(("rt", TB))
    return (first + retention(range(1))
            + weave(retention(range(1, 4)), [("split", 3), ("split", 4), early[0]])
            + weave(retention(range(4, 7)), early[1:4]) + weave(retention(range(7, 10)), early[4:])
            + weave(weave(retention(range(10, NT + 6)), splits[:half]), ffn0(0))
            + weave(attention_inputs(0) + attention_core(0), weave(ffn0(1), splits[half:]))
            + weave(attention_outputs(0), attention_inputs(1))
            + weave(attention_core(1) + attention_outputs(1), moe[:at]) + moe[at:])


SCHEDULE = schedule()

RING_A, RING_B = 3, 2
RING_OF = {"proj": "A", "tqk": "B", "sc": "A", "kv": "B", "ret": "B", "ty": "B", "wo": "B", "tx": "B",
           "gsum": "B", "up": "A", "dn": "B", "qk": "A", "tq": "A", "mx": "A", "tm": "B", "se": "A",
           "pv": "B", "ya": "B", "rt": "B", "mu": "A", "mt": "A", "md": "B"}


def occurrences():
    seen, out = {}, {}
    for step in SCHEDULE:
        key = step[:2] if step[0] in ("ln", "tx") else step[0]
        seen[key] = seen.get(key, 0) + 1
        out[step] = seen[key]
    return out


NTH = occurrences()
LAYER = {"dn": 1, "md": 3}


def psum_places():
    tiles = [("A", i) for i in range(RING_A)] + [("B", i) for i in range(RING_B)]
    used, user, kept, done, out = {tile: -1 for tile in tiles}, {}, None, 0, {}
    for step in SCHEDULE:
        if step[0] not in RING_OF:
            continue
        ring = "B" if step[0] == "mt" and step[2] == 2 else RING_OF[step[0]]
        done += 1
        if step[0] == "pv" and step[3]:
            tile, before = kept, None
            if step[3] == TB - 1:
                kept = None
        else:
            fit = [tile for tile in tiles if tile != kept and (tile[0] == ring or (ring == "B" and kept))]
            tile = min(fit, key=lambda x: used[x])
            before = user.get(tile)
            user[tile] = step
            if step[0] == "pv":
                kept = tile
        used[tile] = done
        out[step] = (*tile, before, done)
    return out


PLACE = psum_places()


def build_two_layers(nc: bass.Bass, xT, x, wqkvg, wo, wqkv1, wup, wdown, wtail, w12, w3, bias_rows, gnorm_rows,
                     consts, consts16, block_decay, out):
    f32, f16, u32 = mybir.dt.float32, mybir.dt.float16, mybir.dt.uint32
    ALU, ACT, AX = mybir.AluOpType, mybir.ActivationFunctionType, mybir.AxisListType
    source = {"xT": xT, "wqkvg": wqkvg, "wo": wo, "wqkv1": wqkv1, "wup": wup, "wdown": wdown, "wtail": wtail}

    with ExitStack() as ctx:
        def sb(name, shape, dt=f32):
            return ctx.enter_context(nc.sbuf_tensor(name, shape, dt))

        def sem(name):
            return ctx.enter_context(nc.semaphore(name))

        ws = sb("cut_weights", [P, 2, W_TOT], f16)
        stage = sb("stage", [P, NSTAGE, STAGE])
        X = sb("residual", [P, NT, D])
        XT = sb("x_transposed", [P, 2, KD, NT * P], f16)
        con = sb("constants", [P, C_TOT])
        con16 = sb("constants16", [P, 3 * P], f16)
        bias = sb("bias_rows", [P, 9 * D], f16)
        Y = sb("y", [P, 2, D])
        YT = sb("y_transposed", [P, 2, D], f16)
        Z = sb("z", [P, 4, D])
        stats = sb("ln_stats", [P, 4, 6])
        mv = sb("ln_mean_var", [P, 4, 2])
        veps = sb("ln_var_eps", [P, 4])
        rstd = sb("ln_rstd", [P, 4])
        half = sb("minus_half", [P, RH])
        gs = sb("weight_sums", [P, 4])
        thr = sb("thresholds", [P, 2, 3])
        small = sb("router", [P, 2, 64])
        small_i = sb("router_index", [P, 2, 8], u32)

        arena1 = sb("arena_mixers", [P, 18480])
        arena2 = sb("arena_ffn", [P, 7872])

        class Carve:
            def __init__(self, arena):
                self.arena, self.at = arena, 0

            def __call__(self, dims, dt=f32):
                n = int(np.prod(dims)) // (2 if dt == f16 else 1)
                view = self.arena[:, self.at:self.at + n]
                self.at += n
                assert self.at <= self.arena.shape[1], self.at
                if dt == f16:
                    view = view.bitcast(f16)
                if len(dims) == 1:
                    return view
                names = "abcdef"[:len(dims)]
                return view.rearrange(f"p ({' '.join(names)}) -> p {' '.join(names)}",
                                      **{c: d for c, d in zip(names, dims)})

        cut = Carve(arena1)
        bias_raw = cut([9 * D])
        gnorm = cut([2 * D])
        tab_cos = cut([TB, 2 * RH, RD // 2])
        tab_sin = cut([TB, 2 * RH, RD // 2])
        QK0 = cut([2, 2 * D])
        VG = cut([4, 2 * D])
        ROT = cut([2, 2 * D])
        R1 = cut([2, 2 * D])
        R2 = cut([2, 2 * D])
        QKT = cut([3, 4, P])
        PT = cut([2, 2, 2, 2, P])
        TS = cut([TB - 1, D])
        block_g = cut([D])
        ones = cut([P])
        KVM = cut([D])
        CENT = cut([2, D])
        SQ = cut([D])
        GA = cut([2, D])
        GC = cut([2, D])
        TH = cut([2, D])
        gsmall = cut([2, 4, RH])
        cut = Carve(arena1)
        ST = cut([TB, 2, AH, 64], f16)
        QT = cut([AH // 2, TB * P], f16)
        KT = cut([AH // 2, TB * P], f16)
        V = cut([TB, AH, 32])
        PE1 = cut([2, 4, TB * P])
        YU = cut([AH // 4, TB * P])
        rden = cut([2, AH])
        cut = Carve(arena2)
        Q12 = cut([KD, 2 * F0], f16)
        Q3 = cut([FM, D], f16)
        work_at = cut.at
        raw12 = cut([KD, 2 * F0])
        raw3 = cut([FM, D])
        cut.at = work_at
        HT0 = cut([2, FM, TB * P], f16)
        HF = cut([2, TB * P])
        THF = cut([2, TB * P])
        cut = Carve(arena2)
        H = cut([HID])
        HT = cut([2, 2, HK, P], f16)
        TG = cut([2, MCW])
        AG = cut([2, MCW])

        psA = [ctx.enter_context(nc.psum_tensor(f"psum_a{i}", [P, 2, 512], f32)) for i in range(RING_A)]
        psB = [ctx.enter_context(nc.psum_tensor(f"psum_b{i}", [P, 512], f32)) for i in range(RING_B)]

        def psum(step):
            ring, at, _, _ = PLACE[step]
            if ring == "B":
                return psB[at]
            return psA[at][:, 0, :] if RING_OF[step[0]] == "B" or (step[0] == "mt" and step[2] == 2) else psA[at]

        def psum16(step):
            ring, at, _, _ = PLACE[step]
            if ring == "B":
                return psB[at][:, :].bitcast(f16)
            return psA[at][:, 0, :].bitcast(f16) if RING_OF[step[0]] == "B" else psA[at][:, :, :].bitcast(f16)

        pe_done = sem("pe_done")
        piece_in = [sem(f"piece_in{i}") for i in range(len(PIECES))]
        head_cut, rest_cut = sem("head_cut"), sem("rest_cut")
        con_in, con16_in, bias_in, gnorm_in = (sem(n) for n in ("con_in", "con16_in", "bias_in", "gnorm_in"))
        x_in = [sem(f"x_in{b}") for b in range(NB)]
        raw_in = sem("raw_in")
        tables, ready0 = sem("tables_ready"), sem("memsets_done")
        bias_head, bias_cut = sem("bias_heads"), sem("bias_cut")
        block_in = sem("block_in")
        evac0, rot1, rot2, rotated = sem("qkvg_copied"), sem("rot_first_term"), sem("rot_second_term"), sem("rotated")
        sc_copied = sem("scores_copied")
        qkT, pT, state = sem("qk_transposed"), sem("masked_scores"), sem("state_ready")
        tanh0, gates, gvar, grstd = sem("gate_tanh"), sem("gates_ready"), sem("gn_var"), sem("gn_rstd")
        y_ready, y_head, y_rest = sem("y_ready"), sem("y_head"), sem("y_rest")
        ln_var, ln_rstd, ln_done, z_ready, x_head, x_rest = (
            [sem(f"{what}{layer}") for layer in range(4)]
            for what in ("ln_var", "ln_rstd", "ln_done", "z_ready", "x_head", "x_rest"))
        sums, quant = sem("weight_sums_ready"), sem("quantized")
        up_tanh, hidden, h_head, h_rest = sem("up_tanh"), sem("hidden"), sem("h_head"), sem("h_rest")
        st_head, st_rest, qkv_copied = sem("stack_heads"), sem("stack_rests"), sem("qkv_copied")
        centered = sem("centered")
        thresholds, logit_read = sem("thresholds_ready"), sem("logits_read")
        q_up, k_up = sem("q_stack_transposed"), sem("k_stack_transposed")
        maxed, q_max = sem("row_max"), sem("q_max_transposed")
        exped, causal, yu = sem("exp_done"), sem("causal_done"), sem("pv_copied")
        st_init = sem("stack_init")
        logits, r_exp, coef = sem("logits"), sem("router_exp"), sem("coefficients")
        mu_tanh, mu_h, mt_head, mt_rest = sem("mu_tanh"), sem("mu_hidden"), sem("mt_head"), sem("mt_rest")
        dve_order, pool_order, out_done = sem("dve_order"), sem("pool_order"), sem("out_done")

        ident = con[:, C_ID:C_ID + P]
        ident16 = con16[:, 0:P]
        below16 = con16[:, P:2 * P]
        pick16 = con16[:, 2 * P:3 * P]

        def bc(ap, shape):
            return ap.to_broadcast(shape)

        def split_views(i, a):
            name, _, cols, first = PIECES[i]
            piece = stage[:, i % NSTAGE, 0:cols]
            if name == "xT":
                return XT[:, a, :, first:first + TB * P], piece.rearrange("p (k t) -> p k t", k=KD)
            return ws[:, a, first:first + cols], piece

        block = ctx.enter_context(nc.Block())

        @block.sync
        def _(sp):
            def load(i):
                name, a, n, _ = PIECES[i]
                if i >= NSTAGE:
                    sp.wait_ge(rest_cut, NTH[("split", i - NSTAGE)])
                sp.dma_start(stage[:, i % NSTAGE, 0:n], source[name][:, a:a + n]).then_inc(piece_in[i], 16)

            load(0)
            load(1)
            sp.dma_start(bias_raw[0:2, :], bias_rows.partition_broadcast(2)).then_inc(bias_in, 16)
            load(2)
            sp.dma_start(con[:, :], consts).then_inc(con_in, 16)
            sp.dma_start(con16[:, :], consts16).then_inc(con16_in, 16)
            sp.dma_start(gnorm, gnorm_rows.partition_broadcast(P)).then_inc(gnorm_in, 16)
            load(3)
            sp.dma_start(block_g, block_decay).then_inc(block_in, 16)
            sp.dma_start(X[:, 0:TB, :], x[0:TB * P, :].rearrange("(t p) d -> p t d", p=P)).then_inc(x_in[0], 16)
            load(4)
            sp.dma_start(raw12, w12.rearrange("(k p) n -> p k n", p=P)).then_inc(raw_in, 16)
            sp.dma_start(raw3[:, 0:FM - 1, :], w3[0:(FM - 1) * P, :].rearrange("(k p) n -> p k n", p=P)).then_inc(raw_in, 16)
            sp.dma_start(raw3[0:LAST, FM - 1, :], w3[(FM - 1) * P:F0, :]).then_inc(raw_in, 16)
            sp.dma_start(X[:, TB:NT, :], x[TB * P:NT * P, :].rearrange("(t p) d -> p t d", p=P)).then_inc(x_in[1], 16)
            for i in range(5, len(PIECES)):
                load(i)
            for t in range(NT):
                sp.wait_ge(ln_done[3], NTH[("ln", 3, t)])
                sp.dma_start(out[t * P:(t + 1) * P, :], X[:, t, :]).then_inc(out_done, 16)
            sp.wait_ge(out_done, 16 * NT)

        @block.tensor
        def _(pe):
            mm = nc.tensor.matmul

            reader = {"proj": evac0, "tqk": qkT, "sc": sc_copied, "kv": state, "ret": centered, "ty": y_rest,
                      "gsum": thresholds, "up": hidden, "mx": maxed, "tm": q_max, "se": exped,
                      "ya": y_ready, "rt": logit_read, "mu": mu_h, "mt": mt_rest}

            def claim(step):
                last = PLACE[step][2]
                if last is None:
                    return
                if last[0] == "tq":
                    pe.wait_ge(q_up, NTH[last])
                    pe.wait_ge(k_up, NTH[last])
                elif last[0] == "qk":
                    pe.wait_ge(st_rest, NTH[last])
                    pe.wait_ge(qkv_copied, NTH[last])
                elif last[0] == "pv":
                    pe.wait_ge(yu, NTH[("pv", last[1], last[2], TB - 1)] // TB)
                elif last[0] in ("wo", "dn", "md"):
                    layer = LAYER.get(last[0], last[1])
                    pe.wait_ge(z_ready[layer], NTH[("ln", layer, last[-1])])
                elif last[0] == "tx":
                    pe.wait_ge(x_rest[last[1]], NTH[last])
                elif last[0] == "ya":
                    pe.wait_ge(y_ready, NTH[("ty", 2, last[1] * TB + last[2])])
                else:
                    pe.wait_ge(reader[last[0]], NTH[last])

            def cut_product(out_of, lhs, rhs, bias_at=None, piece_of=None):
                n = len(lhs)
                ins = None
                for k in range(n):
                    if piece_of:
                        pe.wait_ge(rest_cut, NTH[("split", piece_of[k])])
                    for a, b in ((0, 0), (0, 1), (1, 0)):
                        for dst, col in out_of:
                            ins = mm(dst, lhs[k][a], rhs(k, b, col), start=(k == 0 and a == 0 and b == 0),
                                     stop=(bias_at is None and k == n - 1 and a == 1))
                if bias_at is not None:
                    if piece_of:
                        pe.wait_ge(bias_cut, 1)
                        pe.wait_ge(con16_in, 16)
                    for dst, col in out_of:
                        at = bias_at + col
                        ins = mm(dst, pick16, bias[:, at:at + dst.shape[-1]], start=False, stop=True)
                return ins

            def x_tiles(t):
                return [[XT[:, a, k, t * P:(t + 1) * P] for a in range(2)] for k in range(KD)]

            for step in SCHEDULE:
                kind = step[0]
                if kind not in RING_OF:
                    continue
                ps = psum(step)
                if kind == "proj":
                    t = step[1]
                    if t == 0:
                        pe.wait_ge(rest_cut, NTH[("split", 0)])
                    if t == TB:
                        pe.wait_ge(rest_cut, NTH[("split", 3)])
                    claim(step)
                    w = ws[:, :, W_QKVG:W_O0].rearrange("p a (k n) -> p a k n", k=KD)
                    ins = cut_product([(ps[:, 0, :], 0), (ps[:, 1, :], 512)], x_tiles(t),
                                      lambda k, b, c: w[:, b, k, c:c + 512], 0, (1, 2) if t == 0 else None)
                elif kind == "tqk":
                    t = step[1]
                    pe.wait_ge(rotated, t + 1)
                    claim(step)
                    for j in range(4):
                        ins = nc.tensor.transpose(ps[:, j * P:(j + 1) * P], ROT[:, t % 2, j * P:(j + 1) * P], ident)
                elif kind == "sc":
                    _, t, hf = step
                    pe.wait_ge(qkT, t + 1)
                    claim(step)
                    for g in range(2):
                        for s in range(2):
                            r = 32 * (2 * hf + s)
                            ins = mm(ps[:, s, g * P:(g + 1) * P], QKT[r:r + 32, t % 3, 2 + g, :],
                                     QKT[r:r + 32, t % 3, g, :], start=True, stop=True)
                elif kind == "kv":
                    t = step[1]
                    claim(step)
                    for g in range(2):
                        ins = mm(ps[:, g * P:(g + 1) * P], ROT[:, t % 2, D + g * P:D + (g + 1) * P],
                                 VG[:, t % 4, g * P:(g + 1) * P], start=True, stop=True)
                elif kind == "ret":
                    t = step[1]
                    c = t % TB
                    pe.wait_ge(pT, NTH[("sc", t, 1)])
                    if c:
                        pe.wait_ge(state, NTH[("kv", t - 1)])
                    claim(step)
                    if t == 0:
                        pe.wait_ge(con_in, 16)
                    if c:
                        for g in range(2):
                            mm(ps[:, g * P:(g + 1) * P], QKT[:, t % 3, g, :], TS[:, c - 1, g * P:(g + 1) * P],
                               start=(g == 0), stop=False, skip_group_check=True)
                    for h in range(RH):
                        g, s = divmod(h, 4)
                        ins = mm(ps[:, h * RD:(h + 1) * RD], PT[:, t % 2, s // 2, s % 2, g, :],
                                 VG[:, t % 4, h * RD:(h + 1) * RD],
                                 start=(h == 0 and not c), stop=(h == RH - 1), skip_group_check=True)
                elif kind == "ty":
                    pe.wait_ge(y_ready, NTH[step])
                    claim(step)
                    for k in range(KD):
                        ins = nc.tensor.transpose(ps[:, k * P:(k + 1) * P], Y[:, NTH[step] % 2, k * P:(k + 1) * P], ident)
                elif kind == "wo":
                    _, layer, t = step
                    pe.wait_ge(y_rest, NTH[step])
                    if layer == 0 and t == 0:
                        pe.wait_ge(rest_cut, NTH[("split", 4)])
                    claim(step)
                    first = W_O1 if layer else W_O0
                    w = ws[:, :, first:first + KD * D].rearrange("p a (k n) -> p a k n", k=KD)
                    ins = cut_product([(ps[:, 0:D], 0)], [[YT[:, a, k * P:(k + 1) * P] for a in range(2)] for k in range(KD)],
                                      lambda k, b, c: w[:, b, k, :], (8 if layer else 4) * D)
                elif kind == "tx":
                    _, layer, t = step
                    pe.wait_ge(ln_done[layer], NTH[("ln", layer, t)])
                    claim(step)
                    for k in range(KD):
                        ins = nc.tensor.transpose(ps[:, k * P:(k + 1) * P], X[:, t, k * P:(k + 1) * P], ident)
                elif kind == "gsum":
                    pe.wait_ge(sums, 3)
                    claim(step)
                    ins = mm(ps[:, 0:4], ones, gs[:, :], start=True, stop=True)
                elif kind == "up":
                    _, n, m = step
                    rows = P if m < FM - 1 else LAST
                    if m == 0:
                        pe.wait_ge(x_rest[0], NTH[("tx", 0, TB * n + TB - 1)])
                        pe.wait_ge(quant, 3)
                    claim(step)
                    for k in range(KD):
                        for gu in range(2):
                            w = Q12[:, k, gu * F0 + m * P:gu * F0 + m * P + rows]
                            for a in range(2):
                                ins = mm(ps[0:rows, gu, :], w, XT[:, a, k, n * TB * P:(n + 1) * TB * P],
                                         start=(k == 0 and a == 0), stop=(k == KD - 1 and a == 1))
                elif kind == "dn":
                    t = step[1]
                    pe.wait_ge(h_rest, NTH[("cut", t // TB, FM - 1)])
                    pe.wait_ge(h_head, NTH[("cut", t // TB, FM - 1)])
                    claim(step)
                    c = (t % TB) * P
                    for m in range(FM):
                        rows = P if m < FM - 1 else LAST
                        for a in range(2):
                            ins = mm(ps[:, 0:D], HT0[0:rows, a, m, c:c + P], Q3[0:rows, m, :],
                                     start=(m == 0 and a == 0), stop=(m == FM - 1 and a == 1))
                elif kind == "qk":
                    _, b, i = step
                    t = b * TB + i
                    pe.wait_ge(x_rest[1], NTH[("tx", 1, t)])
                    claim(step)
                    if (b, i) == (0, 0):
                        pe.wait_ge(rest_cut, NTH[("split", 6)])
                        pe.wait_ge(bias_cut, 2)
                    w = ws[:, :, W_QKV1:W_UP].rearrange("p a (k n) -> p a k n", k=KD)
                    ins = cut_product([(ps[:, 0, :], 0), (ps[:, 1, 0:D], 512)], x_tiles(t),
                                      lambda k, b_, c: w[:, b_, k, c:c + (D if c else 512)], 5 * D)
                elif kind == "tq":
                    _, b, i = step
                    pe.wait_ge(st_rest, NTH[("qk", b, i)])
                    pe.wait_ge(qkv_copied, NTH[("qk", b, i)])
                    claim(step)
                    p16 = psum16(step)
                    for w in range(2):
                        for p in range(AH // 2):
                            ins = nc.tensor.transpose(p16[:, w, p * P:(p + 1) * P],
                                                      ST[:, i, w, 2 * p:2 * p + 2, :], ident16)
                elif kind == "mx":
                    _, b, i, p = step
                    if p == 0:
                        pe.wait_ge(q_up, NTH[("tq", b, i)])
                        pe.wait_ge(k_up, NTH[("tq", b, i)])
                    claim(step)
                    for s in range(2):
                        mm(ps[:, s, i * P:(i + 1) * P], ident16, below16, start=True, stop=True)
                    for s in range(2):
                        r = 64 * s
                        ins = mm(ps[:, s, 0:(i + 1) * P], QT[r:r + 64, p, i * P:(i + 1) * P],
                                 KT[r:r + 64, p, 0:(i + 1) * P], start=False, stop=True, skip_group_check=True)
                elif kind == "tm":
                    _, b, i = step
                    pe.wait_ge(maxed, NTH[("mx", b, i, AH // 2 - 1)])
                    claim(step)
                    p16 = psum16(step)
                    for p in range(AH // 2):
                        ins = nc.tensor.transpose(p16[:, p * P:(p + 1) * P], ST[:, i, 0, 2 * p:2 * p + 2, :], ident16)
                elif kind == "se":
                    _, b, g, j, hf = step
                    pe.wait_ge(q_max, NTH[("tm", b, TB - 1)])
                    claim(step)
                    for s in range(2):
                        r, p = 64 * s, 2 * g + hf
                        ins = mm(ps[:, s, 0:(TB - j) * P], KT[r:r + 64, p, j * P:(j + 1) * P],
                                 QT[r:r + 64, p, j * P:TB * P], start=True, stop=True)
                elif kind == "pv":
                    _, b, g, j = step
                    pe.wait_ge(causal, NTH[("se", b, g, j, 1)])
                    if j == 0:
                        claim(step)
                    for s in range(4):
                        ins = mm(ps[32 * s:32 * s + 32, j * P:TB * P], V[:, j, 4 * g + s, :],
                                 PE1[:, j % 2, s, 0:(TB - j) * P], start=(j == 0), stop=(j == TB - 1))
                elif kind == "ya":
                    _, b, i = step
                    pe.wait_ge(yu, NTH[("pv", b, AH // 4 - 1, TB - 1)] // TB)
                    claim(step)
                    for g in range(AH // 4):
                        ins = nc.tensor.transpose(ps[:, g * P:(g + 1) * P], YU[:, g, i * P:(i + 1) * P], ident)
                elif kind == "rt":
                    t = step[1]
                    pe.wait_ge(x_rest[2], NTH[("tx", 2, t)])
                    pe.wait_ge(rest_cut, len(PIECES))
                    claim(step)
                    w = ws[:, :, W_ROUT:W_TOT].rearrange("p a (k n) -> p a k n", k=KD)
                    ins = cut_product([(ps[:, 0:NR], 0)], x_tiles(t), lambda k, b, c: w[:, b, k, :])
                elif kind == "mu":
                    _, t, c = step
                    claim(step)
                    w = ws[:, :, W_UP:W_DOWN].rearrange("p a (k c u n) -> p a k c u n", k=KD, c=MC, u=2)
                    ins = cut_product([(ps[:, 0, 0:MCW], 0), (ps[:, 1, 0:MCW], 1)], x_tiles(t),
                                      lambda k, b, u: w[:, b, k, c, u, :])
                elif kind == "mt":
                    _, t, part = step
                    if part == 0:
                        pe.wait_ge(mu_h, NTH[("mu", t, 2)])
                        claim(step)
                        for k in range(8):
                            ins = nc.tensor.transpose(ps[:, k // 4, (k % 4) * P:(k % 4 + 1) * P], H[:, k * P:(k + 1) * P], ident)
                    elif part == 1:
                        pe.wait_ge(mu_h, NTH[("mu", t, MC - 1)])
                        claim(step)
                        for k in range(8):
                            ins = nc.tensor.transpose(ps[:, k // 4, (k % 4) * P:(k % 4 + 1) * P],
                                                      H[:, (8 + k) * P:(9 + k) * P], ident)
                    else:
                        claim(step)
                        ins = nc.tensor.transpose(ps[0:LAST, 0:P], H[:, 16 * P:HID], ident)
                elif kind == "md":
                    t = step[1]
                    pe.wait_ge(mt_rest, NTH[("mt", t, 2)])
                    claim(step)

                    def rows(k):
                        return LAST if k == HK - 1 else P

                    def down(k):
                        return k * D if k < 8 else W_DOWN + (k - 8) * D
                    ins = cut_product([(ps[:, 0:D], 0)], [[HT[0:rows(k), t % 2, a, k, :] for a in range(2)] for k in range(HK)],
                                      lambda k, b, c: ws[0:rows(k), b, down(k):down(k) + D])
                ins.then_inc(pe_done, 1)

        @block.scalar
        def _(act):
            for step in SCHEDULE:
                kind, n = step[0], NTH[step]
                ps = psum(step) if kind in RING_OF else None
                if kind == "split":
                    i = step[1]
                    name, _, cols, first = PIECES[i]
                    if name == "wdown" and first == 0:
                        act.wait_ge(pe_done, PLACE[("proj", NT - 1)][3])
                    act.wait_ge(piece_in[i], 16)
                    dst, src = split_views(i, 0)
                    nc.scalar.activation(dst, src, ACT.Copy, scale=SA if name == "xT" else SW).then_inc(head_cut, 1)
                elif kind == "bias":
                    if n == 1:
                        act.wait_ge(bias_in, 16)
                        act.wait_ge(ready0, 4)
                    w = slice(0, 5 * D) if n == 1 else slice(5 * D, 9 * D)
                    nc.scalar.activation(bias[0:2, w], bias_raw[0:2, w], ACT.Copy, scale=SW).then_inc(bias_head, 1)
                elif kind == "proj":
                    t = step[1]
                    act.wait_ge(pe_done, PLACE[step][3])
                    if t >= 2:
                        act.wait_ge(rot1, t - 1)
                        act.wait_ge(rot2, t - 1)
                    if t >= 4:
                        act.wait_ge(gates, t - 3)
                    nc.scalar.activation(QK0[:, t % 2], ps[:, 0, :], ACT.Copy, scale=UN)
                    nc.scalar.activation(VG[:, t % 4], ps[:, 1, :], ACT.Copy, scale=UN).then_inc(evac0, 1)
                elif kind == "sc":
                    _, t, hf = step
                    act.wait_ge(pe_done, PLACE[step][3])
                    nc.scalar.activation(PT[:, t % 2, hf], ps[:, :, 0:2 * P].rearrange("p s (g q) -> p s g q", g=2),
                                         ACT.Copy).then_inc(sc_copied, 1)
                elif kind == "wsum":
                    i = step[1]
                    if i == 0:
                        act.wait_ge(raw_in, 48)
                        act.wait_ge(ready0, 4)
                    if i < 2:
                        w = slice(i * F0, (i + 1) * F0)
                        ins = nc.scalar.activation(Q12[:, :, w], raw12[:, :, w], ACT.Abs, accum_out=gs[:, i:i + 1])
                    else:
                        nc.scalar.activation(Q3[:, 0:FM - 1, :], raw3[:, 0:FM - 1, :], ACT.Abs, accum_out=gs[:, 2:3])
                        ins = nc.scalar.activation(Q3[0:LAST, FM - 1, :], raw3[0:LAST, FM - 1, :], ACT.Abs,
                                                   accum_out=gs[0:LAST, 3:4])
                    ins.then_inc(sums, 1)
                elif kind == "ret":
                    t = step[1]
                    act.wait_ge(evac0, t + 1)
                    if t >= 2:
                        act.wait_ge(gates, t - 1)
                    nc.scalar.activation(TH[:, t % 2, :], VG[:, t % 4, D:2 * D], ACT.Tanh, scale=0.5).then_inc(tanh0, 1)
                elif kind == "tqk":
                    t = step[1]
                    act.wait_ge(pe_done, PLACE[step][3])
                    ins = nc.scalar.activation(QKT[:, t % 3, :, :].rearrange("p a b -> p (a b)"), ps[:, :], ACT.Copy)
                    ins.then_inc(qkT, 1)
                elif kind == "ty":
                    act.wait_ge(pe_done, PLACE[step][3])
                    nc.scalar.activation(YT[:, 0, :], ps[:, 0:D], ACT.Copy, scale=SA * (1.0 if step[1] else 0.5)).then_inc(y_head, 1)
                elif kind == "tx":
                    t = step[2]
                    act.wait_ge(pe_done, PLACE[step][3])
                    nc.scalar.activation(XT[:, 0, :, t * P:(t + 1) * P], ps[:, 0:D].rearrange("p (k t) -> p k t", k=KD),
                                         ACT.Copy, scale=SA).then_inc(x_head[step[1]], 1)
                elif kind == "up":
                    m = step[2]
                    rows = P if m < FM - 1 else LAST
                    act.wait_ge(pe_done, PLACE[step][3])
                    if n > 2:
                        act.wait_ge(hidden, n - 2)
                    nc.scalar.activation(THF[0:rows, n % 2, :], ps[0:rows, 0, :], ACT.Tanh, scale=0.5 / SA).then_inc(up_tanh, 1)
                elif kind == "cut":
                    m = step[2]
                    rows = P if m < FM - 1 else LAST
                    act.wait_ge(hidden, n)
                    if step == ("cut", 1, 0):
                        act.wait_ge(pe_done, PLACE[("dn", TB - 1)][3])
                    nc.scalar.activation(HT0[0:rows, 0, m, :], HF[0:rows, n % 2, :], ACT.Copy).then_inc(h_head, 1)
                elif kind == "qk":
                    _, b, i = step
                    act.wait_ge(pe_done, PLACE[step][3])
                    if n == 1:
                        act.wait_ge(st_init, 2)
                    if b:
                        act.wait_ge(pe_done, PLACE[("tm", 0, i)][3])
                        act.wait_ge(pe_done, PLACE[("pv", 0, AH // 4 - 1, TB - 1)][3])
                    q, k, val = (w.rearrange("p (h d) -> p h d", h=AH) for w in (ps[:, 0, 0:D], ps[:, 0, D:2 * D], ps[:, 1, 0:D]))
                    nc.scalar.activation(ST[:, i, 0, :, 0:16], q, ACT.Copy, scale=UN)
                    nc.scalar.activation(ST[:, i, 1, :, 0:16], k, ACT.Copy, scale=4 * UN).then_inc(st_head, 1)
                    nc.scalar.activation(V[:, i, :, 0:16], val, ACT.Copy, scale=UN)
                    act.wait_ge(st_head, n)
                    nc.scalar.activation(ST[:, i, 0, :, 16:32], ST[:, i, 0, :, 0:16], ACT.Copy)
                    nc.scalar.activation(ST[:, i, 1, :, 32:48], ST[:, i, 1, :, 0:16], ACT.Copy).then_inc(qkv_copied, 1)
                elif kind == "tq":
                    i = step[2]
                    act.wait_ge(pe_done, PLACE[step][3])
                    nc.scalar.activation(QT[:, :, i * P:(i + 1) * P],
                                         psum16(step)[:, 0, :].rearrange("p (a b) -> p a b", b=P), ACT.Copy).then_inc(q_up, 1)
                elif kind == "tm":
                    i = step[2]
                    act.wait_ge(pe_done, PLACE[step][3])
                    ins = nc.scalar.activation(QT[:, :, i * P:(i + 1) * P],
                                               psum16(step).rearrange("p (a b) -> p a b", b=P), ACT.Copy)
                    ins.then_inc(q_max, 1)
                elif kind == "se":
                    _, b, g, j, hf = step
                    act.wait_ge(pe_done, PLACE[step][3])
                    w = (TB - j) * P
                    ins = nc.scalar.activation(PE1[:, j % 2, 2 * hf:2 * hf + 2, 0:w], ps[:, :, 0:w], ACT.Exp, scale=1.0 / 16)
                    ins.then_inc(exped, 1)
                elif kind == "pv" and step[3] == TB - 1:
                    act.wait_ge(pe_done, PLACE[step][3])
                    nc.scalar.activation(YU[:, step[2], :], ps[:, :], ACT.Copy).then_inc(yu, 1)
                elif kind == "rc":
                    t = step[1]
                    r = small[:, t % 2, :]
                    act.wait_ge(logits, n)
                    nc.scalar.activation(r[:, 24:32], r[:, 16:24], ACT.Exp, bias=r[:, 9:10], accum_out=r[:, 32:33])
                    nc.scalar.activation(r[:, 33:34], r[:, 8:9], ACT.Tanh, scale=0.5).then_inc(r_exp, 1)
                elif kind == "mu":
                    act.wait_ge(pe_done, PLACE[step][3])
                    if n > 2:
                        act.wait_ge(mu_h, n - 2)
                    nc.scalar.activation(TG[:, n % 2, :], ps[:, 0, 0:MCW], ACT.Tanh, scale=0.5 * UN).then_inc(mu_tanh, 1)
                elif kind == "mt":
                    _, t, part = step
                    act.wait_ge(pe_done, PLACE[step][3])
                    if part < 2:
                        nc.scalar.activation(HT[:, t % 2, 0, 8 * part:8 * part + 8, :].rearrange("p a b -> p (a b)"),
                                             ps[:, :, :].rearrange("p a b -> p (a b)"), ACT.Copy).then_inc(mt_head, 1)
                    else:
                        nc.scalar.activation(HT[0:LAST, t % 2, 0, 16, :], ps[0:LAST, 0:P], ACT.Copy).then_inc(mt_head, 1)

        @block.vector
        def _(dve):
            v = nc.vector
            count = [0]

            def mark(ins):
                count[0] += 1
                ins.then_inc(dve_order, 1)
                return count[0]

            def link(ins):
                dve.wait_ge(dve_order, mark(ins))

            def finished(step):
                dve.wait_ge(pe_done, PLACE[step][3])

            def norm_input(step, ps, scale):
                layer, t = LAYER.get(step[0], step[1]), step[-1]
                n = NTH[("ln", layer, t)]
                r = 2 * (layer % 2) + n % 2
                finished(step)
                if layer == 0:
                    dve.wait_ge(x_in[t // TB], 16)
                v.scalar_tensor_tensor(Z[:, r, :], ps[:, 0:D], scale, X[:, t, :], ALU.mult, ALU.add).then_inc(z_ready[layer], 1)
                dve.wait_ge(z_ready[layer], n)
                link(v.bn_stats(stats[:, r, :], Z[:, r, :]))
                link(v.bn_aggr(mv[:, r, :], stats[:, r, :]))
                v.tensor_scalar(veps[:, r:r + 1], mv[:, r, 1:2], EPS, None, ALU.add).then_inc(ln_var[layer], 1)

            for step in SCHEDULE:
                kind, n = step[0], NTH[step]
                ps = psum(step) if kind in RING_OF else None
                if kind == "split":
                    i = step[1]
                    (head, src), (rest, _) = split_views(i, 0), split_views(i, 1)
                    dve.wait_ge(head_cut, n)
                    v.scalar_tensor_tensor(rest, src, SA if PIECES[i][0] == "xT" else SW, head,
                                           ALU.mult, ALU.subtract).then_inc(rest_cut, 1)
                elif kind == "bias":
                    if n == 1:
                        dve.wait_ge(con_in, 16)
                    dve.wait_ge(bias_head, n)
                    w = slice(0, 5 * D) if n == 1 else slice(5 * D, 9 * D)
                    v.scalar_tensor_tensor(bias[0:2, w], bias_raw[0:2, w], con[0:2, C_REST:C_REST + 1], bias[0:2, w],
                                           ALU.mult, ALU.subtract).then_inc(bias_cut, 1)
                elif kind == "proj":
                    t = step[1]
                    dve.wait_ge(evac0, t + 1)
                    if t < TB:
                        dve.wait_ge(tables, t + 1)
                    qk = QK0[:, t % 2].rearrange("p (s u j) -> p s u j", u=2, j=RD // 2)
                    cos = tab_cos[:, t % TB].unsqueeze(2).to_broadcast([P, 2 * RH, 2, RD // 2])
                    v.tensor_tensor(R1[:, t % 2].rearrange("p (s u j) -> p s u j", u=2, j=RD // 2),
                                    qk, cos, ALU.mult).then_inc(rot1, 1)
                elif kind == "rot":
                    t = step[1]
                    dve.wait_ge(rot1, t + 1)
                    dve.wait_ge(rot2, t + 1)
                    a, b, o = (w[:, t % 2].rearrange("p (s u j) -> p s u j", u=2, j=RD // 2) for w in (R1, R2, ROT))
                    v.tensor_tensor(o[:, :, 0], a[:, :, 0], b[:, :, 0], ALU.subtract)
                    v.tensor_tensor(o[:, :, 1], a[:, :, 1], b[:, :, 1], ALU.add).then_inc(rotated, 1)
                elif kind == "kv":
                    t = step[1]
                    c = t % TB
                    finished(step)
                    if t == 0:
                        dve.wait_ge(block_in, 16)
                    if c == 0:
                        v.tensor_tensor(TS[:, 0], ps[:, 0:D], block_g, ALU.mult).then_inc(state, 1)
                    else:
                        link(v.tensor_tensor(KVM, ps[:, 0:D], block_g, ALU.mult))
                        for g in range(2):
                            w = slice(g * P, (g + 1) * P)
                            ins = v.scalar_tensor_tensor(TS[:, c, w], TS[:, c - 1, w], con[:, C_G128 + g:C_G128 + g + 1],
                                                         KVM[:, w], ALU.mult, ALU.add)
                        ins.then_inc(state, 1)
                    dve.wait_ge(state, n)
                elif kind == "ret":
                    t = step[1]
                    finished(step)
                    sm = gsmall[:, t % 2]
                    heads = ps[:, 0:D].rearrange("p (h d) -> p h d", h=RH)
                    cent = CENT[:, t % 2].rearrange("p (h d) -> p h d", h=RH)
                    link(v.tensor_reduce(sm[:, 0], heads, AX.X, ALU.add))
                    link(v.tensor_scalar(sm[:, 1], sm[:, 0], -1.0 / RD, None, ALU.mult))
                    v.tensor_tensor(cent, heads, sm[:, 1].unsqueeze(2).to_broadcast([P, RH, RD]), ALU.add)\
                        .then_inc(centered, 1)
                    dve.wait_ge(centered, n)
                    link(v.tensor_tensor(SQ, CENT[:, t % 2], CENT[:, t % 2], ALU.mult))
                    link(v.tensor_reduce(sm[:, 2], SQ.rearrange("p (h d) -> p h d", h=RH), AX.X, ALU.add))
                    v.tensor_scalar(sm[:, 2], sm[:, 2], 1.0 / RD, EPS, ALU.mult, ALU.add).then_inc(gvar, 1)
                elif kind == "gn":
                    t = step[1]
                    y = Y[:, NTH[("ty", 0, t)] % 2, :]
                    dve.wait_ge(grstd, n)
                    dve.wait_ge(gates, n)
                    link(v.tensor_tensor(y.rearrange("p (h d) -> p h d", h=RH),
                                         CENT[:, t % 2].rearrange("p (h d) -> p h d", h=RH),
                                         gsmall[:, t % 2, 3].unsqueeze(2).to_broadcast([P, RH, RD]), ALU.mult))
                    link(v.tensor_tensor(y, y, GA[:, t % 2], ALU.mult))
                    v.tensor_tensor(y, y, GC[:, t % 2], ALU.add).then_inc(y_ready, 1)
                elif kind == "ty":
                    finished(step)
                    dve.wait_ge(y_head, n)
                    v.scalar_tensor_tensor(YT[:, 1, :], ps[:, 0:D], SA * (1.0 if step[1] else 0.5), YT[:, 0, :],
                                           ALU.mult, ALU.subtract).then_inc(y_rest, 1)
                elif kind == "wo":
                    norm_input(step, ps, UN)
                elif kind == "dn":
                    norm_input(step, ps, 0.5 / SA)
                elif kind == "md":
                    norm_input(step, ps, UN)
                elif kind == "ln":
                    layer, t = step[1:]
                    r = 2 * (layer % 2) + n % 2
                    dve.wait_ge(ln_rstd[layer], n)
                    v.tensor_scalar(X[:, t, :], Z[:, r, :], mv[:, r, 0:1], rstd[:, r:r + 1],
                                    ALU.subtract, ALU.mult).then_inc(ln_done[layer], 1)
                    dve.wait_ge(ln_done[layer], n)
                elif kind == "tx":
                    t = step[2]
                    finished(step)
                    dve.wait_ge(x_head[step[1]], n)
                    w = slice(t * P, (t + 1) * P)
                    v.scalar_tensor_tensor(XT[:, 1, :, w], ps[:, 0:D].rearrange("p (k t) -> p k t", k=KD), SA,
                                           XT[:, 0, :, w], ALU.mult, ALU.subtract).then_inc(x_rest[step[1]], 1)
                elif kind == "gsum":
                    finished(step)
                    link(v.tensor_scalar(thr[:, 0, 0:3], ps[:, 0:3], 0.5 / (D * F0), 0.5e-8, ALU.mult, ALU.add))
                    link(v.scalar_tensor_tensor(thr[:, 0, 2:3], ps[:, 3:4], 0.5 / (D * F0), thr[:, 0, 2:3], ALU.mult, ALU.add))
                    v.tensor_scalar(thr[:, 1, :], thr[:, 0, :], -1.0, None, ALU.mult).then_inc(thresholds, 1)
                    dve.wait_ge(thresholds, 1)
                elif kind == "quant":
                    i = step[1]
                    if i < 2:
                        parts = [(P, raw12[:, :, i * F0:(i + 1) * F0], Q12[:, :, i * F0:(i + 1) * F0])]
                    else:
                        parts = [(P, raw3[:, 0:FM - 1, :], Q3[:, 0:FM - 1, :]),
                                 (LAST, raw3[0:LAST, FM - 1, :], Q3[0:LAST, FM - 1, :])]
                    for rows, raw, q in parts:
                        link(v.tensor_scalar(q, raw, thr[0:rows, 1, i:i + 1], None, ALU.is_lt))
                        ins = v.scalar_tensor_tensor(q, raw, thr[0:rows, 0, i:i + 1], q, ALU.is_gt, ALU.subtract)
                    ins.then_inc(quant, 1)
                elif kind == "up":
                    m = step[2]
                    rows = P if m < FM - 1 else LAST
                    finished(step)
                    dve.wait_ge(up_tanh, n)
                    if n == 1:
                        dve.wait_ge(quant, 3)
                    if n > 2:
                        dve.wait_ge(h_head, n - 2)
                        dve.wait_ge(h_rest, n - 2)
                    v.scalar_tensor_tensor(HF[0:rows, n % 2, :], THF[0:rows, n % 2, :], 1.0, ps[0:rows, 1, :],
                                           ALU.add, ALU.mult).then_inc(hidden, 1)
                elif kind == "qk":
                    i = step[2]
                    finished(step)
                    if n == 1:
                        v.memset(ST[:, :, :, :, 48:64], 0.0)
                        v.memset(V[:, :, :, 16:32], 0.0).then_inc(st_init, 1)
                        dve.wait_ge(st_init, 1)
                        v.memset(ST[:, :, 1, :, 48:49], 1.0)
                        v.memset(V[:, :, :, 16:17], 1.0).then_inc(st_init, 1)
                    if n > TB:
                        v.memset(ST[:, i, 0, :, 48:49], 0.0)
                    dve.wait_ge(st_head, n)
                    for w, scale, at in ((0, UN, 32), (1, 4 * UN, 16)):
                        ins = v.scalar_tensor_tensor(ST[:, i, w, :, at:at + 16],
                                                     ps[:, 0, w * D:(w + 1) * D].rearrange("p (h d) -> p h d", h=AH), scale,
                                                     ST[:, i, w, :, 0:16], ALU.mult, ALU.subtract)
                    ins.then_inc(st_rest, 1)
                elif kind == "tq":
                    i = step[2]
                    finished(step)
                    v.tensor_copy(KT[:, :, i * P:(i + 1) * P],
                                  psum16(step)[:, 1, :].rearrange("p (a b) -> p a b", b=P)).then_inc(k_up, 1)
                elif kind == "mx":
                    _, b, i, p = step
                    finished(step)
                    v.tensor_reduce(ST[:, i, 0, 2 * p:2 * p + 2, 48], ps[:, :, 0:(i + 1) * P], AX.X, ALU.max,
                                    negate=True).then_inc(maxed, 1)
                elif kind == "ya":
                    _, b, i = step
                    m = NTH[("ty", 2, b * TB + i)]
                    finished(step)
                    heads = ps[:, :].rearrange("p (h d) -> p h d", h=AH)
                    link(v.reciprocal(rden[:, m % 2].unsqueeze(2), heads[:, :, AD:AD + 1]))
                    v.tensor_tensor(Y[:, m % 2].rearrange("p (h d) -> p h d", h=AH), heads[:, :, 0:AD],
                                    rden[:, m % 2].unsqueeze(2).to_broadcast([P, AH, AD]), ALU.mult).then_inc(y_ready, 1)
                elif kind == "rt":
                    t = step[1]
                    r = small[:, t % 2, :]
                    finished(step)
                    v.tensor_scalar(r[:, 0:NR], ps[:, 0:NR], UN, None, ALU.mult).then_inc(logit_read, 1)
                    dve.wait_ge(logit_read, n)
                    link(v.max(r[:, 16:24], r[:, 0:NE]))
                    link(v.max_index(small_i[:, t % 2, :], r[:, 16:24], r[:, 0:NE]))
                    v.tensor_scalar(r[:, 9:10], r[:, 16:17], -1.0, None, ALU.mult).then_inc(logits, 1)
                    link(v.tensor_copy(r[:, 34:36], small_i[:, t % 2, 0:2]))
                elif kind == "rc":
                    t = step[1]
                    r = small[:, t % 2, :]
                    scale = 0.5 * SA * UN * UN
                    iota = con[:, C_IOTA:C_IOTA + NE]
                    dve.wait_ge(r_exp, n)
                    link(v.reciprocal(r[:, 36:37], r[:, 32:33]))
                    link(v.tensor_scalar(r[:, 37:39], r[:, 24:26], r[:, 36:37], scale, ALU.mult, ALU.mult))
                    v.tensor_scalar(r[:, 40:48], iota, r[:, 34:35], r[:, 37:38], ALU.is_equal, ALU.mult)
                    link(v.tensor_scalar(r[:, 48:56], iota, r[:, 35:36], r[:, 38:39], ALU.is_equal, ALU.mult))
                    v.tensor_tensor(r[:, 48:56], r[:, 48:56], r[:, 40:48], ALU.add)
                    link(v.tensor_scalar(r[:, 56:57], r[:, 33:34], 1.0, 0.5 * scale, ALU.add, ALU.mult))
                elif kind == "mu":
                    _, t, c = step
                    finished(step)
                    dve.wait_ge(mu_tanh, n)
                    if n > 2:
                        dve.wait_ge(mu_h, n - 2)
                    link(v.scalar_tensor_tensor(AG[:, n % 2, :], TG[:, n % 2, :], 1.0, ps[:, 0, 0:MCW], ALU.add, ALU.mult))
                    coef_at = [(0, FE, 2 * c), (FE, FE, 2 * c + 1)] if 2 * c < NE else [(0, MCW, NE)]
                    for at, w, e in coef_at:
                        ins = v.scalar_tensor_tensor(H[:, c * MCW + at:c * MCW + at + w], AG[:, n % 2, at:at + w],
                                                     small[:, t % 2, 48 + e:49 + e], ps[:, 1, at:at + w], ALU.mult, ALU.mult)
                    ins.then_inc(mu_h, 1)
                elif kind == "mt":
                    _, t, part = step
                    finished(step)
                    dve.wait_ge(mt_head, n)
                    if part < 2:
                        k = slice(8 * part, 8 * part + 8)
                        v.tensor_tensor(HT[:, t % 2, 1, k, :].rearrange("p a b -> p (a b)"),
                                        ps[:, :, :].rearrange("p a b -> p (a b)"),
                                        HT[:, t % 2, 0, k, :].rearrange("p a b -> p (a b)"), ALU.subtract).then_inc(mt_rest, 1)
                    else:
                        v.tensor_tensor(HT[0:LAST, t % 2, 1, 16, :], ps[0:LAST, 0:P], HT[0:LAST, t % 2, 0, 16, :],
                                        ALU.subtract).then_inc(mt_rest, 1)

        @block.gpsimd
        def _(pool):
            g_ = nc.gpsimd
            count = [0]

            def link(ins):
                count[0] += 1
                ins.then_inc(pool_order, 1)
                pool.wait_ge(pool_order, count[0])

            g_.memset(ones, 1.0).then_inc(ready0, 1)
            g_.memset(gs[:, :], 0.0).then_inc(ready0, 1)
            g_.memset(half[:, :], -0.5).then_inc(ready0, 1)
            g_.memset(bias[:, :], 0.0).then_inc(ready0, 1)
            pool.wait_ge(ready0, 4)
            for step in SCHEDULE:
                kind, n = step[0], NTH[step]
                if kind == "proj":
                    t = step[1]
                    if t == 0:
                        pool.wait_ge(con_in, 16)
                    if t < TB:
                        dec = con[:, C_DEC:C_DEC + 2 * RH].unsqueeze(2).to_broadcast([P, 2 * RH, RD // 2])
                        for tab, at in ((tab_cos, C_COS), (tab_sin, C_SIN)):
                            at += t * RD // 2
                            ins = g_.tensor_tensor(tab[:, t], con[:, at:at + RD // 2].unsqueeze(1).to_broadcast([P, 2 * RH, RD // 2]),
                                                   dec, ALU.mult)
                        ins.then_inc(tables, 1)
                        pool.wait_ge(tables, t + 1)
                    if t >= 2:
                        pool.wait_ge(rotated, t - 1)
                    pool.wait_ge(evac0, t + 1)
                    qk = QK0[:, t % 2].rearrange("p (s u j) -> p s u j", u=2, j=RD // 2)
                    o = R2[:, t % 2].rearrange("p (s u j) -> p s u j", u=2, j=RD // 2)
                    g_.tensor_tensor(o[:, :, 0], qk[:, :, 1], tab_sin[:, t % TB], ALU.mult)
                    g_.tensor_tensor(o[:, :, 1], qk[:, :, 0], tab_sin[:, t % TB], ALU.mult).then_inc(rot2, 1)
                elif kind == "sc":
                    _, t, hf = step
                    pool.wait_ge(sc_copied, n)
                    part = PT[:, t % 2, hf].rearrange("p s g q -> p (s g) q")
                    g_.affine_select(out=part, in_=part, compare_op=ALU.is_ge, fill=0.0, base=0,
                                     pattern=[[0, 4], [1, P]], channel_multiplier=-1).then_inc(pT, 1)
                elif kind == "ret":
                    t = step[1]
                    if t == 0:
                        pool.wait_ge(gnorm_in, 16)
                    pool.wait_ge(tanh0, t + 1)
                    if t >= 2:
                        pool.wait_ge(y_ready, NTH[("ty", 0, t - 2)])
                    gate = VG[:, t % 4, D:2 * D]
                    link(g_.tensor_tensor(GC[:, t % 2], TH[:, t % 2], gate, ALU.mult))
                    link(g_.tensor_tensor(GC[:, t % 2], GC[:, t % 2], gate, ALU.add))
                    link(g_.tensor_tensor(GA[:, t % 2], GC[:, t % 2], gnorm[:, 0:D], ALU.mult))
                    g_.tensor_tensor(GC[:, t % 2], GC[:, t % 2], gnorm[:, D:2 * D], ALU.mult).then_inc(gates, 1)
                    pool.wait_ge(gvar, n)
                    g_.tensor_tensor(gsmall[:, t % 2, 3], gsmall[:, t % 2, 2], half[:, 0:RH], ALU.pow).then_inc(grstd, 1)
                elif kind in ("wo", "dn", "md"):
                    layer = LAYER.get(kind, step[1])
                    m = NTH[("ln", layer, step[-1])]
                    r = 2 * (layer % 2) + m % 2
                    pool.wait_ge(ln_var[layer], m)
                    g_.tensor_tensor(rstd[:, r:r + 1], veps[:, r:r + 1], half[:, 0:1], ALU.pow).then_inc(ln_rstd[layer], 1)
                elif kind == "cut":
                    m = step[2]
                    rows = P if m < FM - 1 else LAST
                    pool.wait_ge(h_head, n)
                    g_.tensor_tensor(HT0[0:rows, 1, m, :], HF[0:rows, n % 2, :], HT0[0:rows, 0, m, :],
                                     ALU.subtract).then_inc(h_rest, 1)
                elif kind == "se":
                    _, b, g, j, hf = step
                    pool.wait_ge(exped, n)
                    part = PE1[:, j % 2, 2 * hf:2 * hf + 2, 0:P]
                    g_.affine_select(out=part, in_=part, compare_op=ALU.is_ge, fill=0.0, base=0,
                                     pattern=[[0, 2], [1, P]], channel_multiplier=-1).then_inc(causal, 1)


def constants():
    gammas = (1.0 - np.exp(np.linspace(np.log(1 / 32), np.log(1 / 64), RH))).astype(np.float32).astype(np.float64)
    con = np.zeros((P, C_TOT))
    part = np.arange(P)
    block = np.zeros((P, D))
    con[:, C_ID:C_ID + P] = np.eye(P)
    for g in range(2):
        own = gammas[4 * g + part // RD] ** P
        block[:, g * P:(g + 1) * P] = own[:, None] * (part[:, None] // RD == part[None, :] // RD)
        con[:, C_G128 + g] = own
    thetas = (1.0 / np.float32(10000.0) ** np.linspace(0.0, 1.0, RD // 2, dtype=np.float32)).astype(np.float32)
    for c in range(TB):
        angle = ((c * P + part).astype(np.float32)[:, None] * thetas[None, :]).astype(np.float32).astype(np.float64)
        con[:, C_COS + c * RD // 2:C_COS + (c + 1) * RD // 2] = np.cos(angle)
        con[:, C_SIN + c * RD // 2:C_SIN + (c + 1) * RD // 2] = np.sin(angle)
    con[:, C_DEC:C_DEC + RH] = gammas[None, :] ** part[:, None]
    con[:, C_DEC + RH:C_DEC + 2 * RH] = gammas[None, :] ** -part[:, None].astype(np.float64) / np.sqrt(RD)
    con[:, C_IOTA:C_IOTA + NE] = np.arange(NE)
    con[1:, C_REST] = SW
    con16 = np.zeros((P, 3 * P))
    con16[0, 2 * P:] = -SA
    con16[1, 2 * P:] = SA
    con16[:, 0:P] = np.eye(P)
    con16[:, P:2 * P] = np.where(part[None, :] > part[:, None], -60000.0, 0.0)
    return con.astype(np.float32), con16.astype(np.float16), block.astype(np.float32)


def tiled(w):
    k = w.shape[0] // P
    return np.ascontiguousarray(w.reshape(k, P, -1).transpose(1, 0, 2).reshape(P, -1))


def layout(i):
    turn = np.concatenate([np.concatenate([np.arange(0, RD, 2), np.arange(1, RD, 2)]) + h * RD for h in range(RH)])
    x = i["L0_attn_x"].reshape(NT * P, D)
    a = {"xT": tiled(x.T).reshape(P, KD, NB, TB * P).transpose(0, 2, 1, 3).reshape(P, -1), "x": np.ascontiguousarray(x)}
    a["wqkvg"] = tiled(np.concatenate([i["L0_attn_w_q"][:, turn], i["L0_attn_w_k"][:, turn], i["L0_attn_w_v"],
                                       i["L0_attn_w_g"]], 1))
    a["wo"] = np.concatenate([tiled(i["L0_attn_w_o"]), tiled(i["L1_attn_Wo"])], 1)
    a["wqkv1"] = tiled(np.concatenate([i[f"L1_attn_W{c}"].transpose(1, 0, 2).reshape(D, D) for c in "qkv"], 1))
    gate = np.concatenate([i["L1_ffn_We_gate_up"][e, :, :FE] for e in range(NE)] + [i["L1_ffn_Ws_gate_up"][:, :FS]], 1)
    up = np.concatenate([i["L1_ffn_We_gate_up"][e, :, FE:] for e in range(NE)] + [i["L1_ffn_Ws_gate_up"][:, FS:]], 1)
    a["wup"] = tiled(np.stack([gate.reshape(D, MC, MCW), up.reshape(D, MC, MCW)], 2).reshape(D, -1))
    down = np.concatenate([i["L1_ffn_We_down"].reshape(NE * FE, D), i["L1_ffn_Ws_down"]], 0)
    a["wdown"] = tiled(down[:(HK - 1) * P])
    last = np.concatenate([down[(HK - 1) * P:], np.zeros((P - LAST, D), np.float32)], 0)
    a["wtail"] = np.concatenate([last, tiled(np.concatenate([i["L1_ffn_W_router"].T, i["L1_ffn_W_sgate"].T], 1))], 1)
    a["w12"] = np.concatenate([i["L0_ffn_w1"].T, i["L0_ffn_w2"].T], 1)
    a["w3"] = np.ascontiguousarray(i["L0_ffn_w3"].T)
    a["bias_rows"] = np.concatenate([i["L0_attn_b_q"][turn], i["L0_attn_b_k"][turn], i["L0_attn_b_v"], i["L0_attn_b_g"],
                                     i["L0_attn_b_o"], i["L1_attn_bq"].reshape(-1), i["L1_attn_bk"].reshape(-1),
                                     i["L1_attn_bv"].reshape(-1), i["L1_attn_bo"]])
    a["gnorm_rows"] = np.concatenate([i["L0_attn_gn_weight"], i["L0_attn_gn_bias"]])
    a["consts"], a["consts16"], a["block_decay"] = constants()
    return a


def kernel(**inputs):
    import concourse.bacc as _bacc
    from concourse.bass_utils import run_bass_kernel_spmd as _run

    nc = _bacc.Bacc("TRN2", target_bir_lowering=False, num_devices=1)
    arrays, args = {}, []
    for name, a in layout({k: np.asarray(v) for k, v in inputs.items()}).items():
        a = np.ascontiguousarray(a)
        arrays[f"in_{name}"] = a
        args.append(nc.dram_tensor(f"in_{name}", a.shape, mybir.dt.from_np(a.dtype), kind="ExternalInput").ap())
    out = nc.dram_tensor("out", (NT * P, D), mybir.dt.float32, kind="ExternalOutput").ap()
    build_two_layers(nc, *args, out)
    r = _run(nc, [arrays], core_ids=[0])
    return r.results[0]["out"].reshape(NB, TB * P, D)
```

```python
import concourse.bass as bass
from concourse import mybir
from contextlib import ExitStack
import numpy as np

P = 128
D = 256
KD = D // P
NT = 8
NB = 2
TB = NT // NB
RH, RD = 8, 32
AH, AD = 16, 16
F0 = 704
FM = 6
NE, FE, FS = 8, 176, 704
HID = NE * FE + FS
MC, MCW = 6, 352
HK = (HID + P - 1) // P
LAST = F0 % P
EPS = 1e-5


def mx_heads(i):
    return (8, 4, 2, 2)[i]


def se_heads(j):
    return 2 if j < 2 else 4



SA = 16.0
SW = 64.0
UN = 1.0 / (SA * SW)

W_QKVG = 0
W_O0 = W_QKVG + KD * 4 * D
W_O1 = W_O0 + KD * D
W_QKV1 = W_O1 + KD * D
W_UP = W_QKV1 + KD * 3 * D
W_DOWN = W_UP + KD * 2 * HID
W_TAIL = W_DOWN + (HK - 9) * D
W_ROUT = W_TAIL + D
NR = NE + 1
W_TOT = W_ROUT + KD * NR
STAGE = 1024
NSTAGE = 3


C_ID = 0
C_G128 = C_ID + P
C_REST = C_G128 + KD
C_COS = C_REST + 1
C_SIN = C_COS + TB * RD // 2
C_DEC = C_SIN + TB * RD // 2
C_IOTA = C_DEC + 2 * RH
C_TOT = C_IOTA + NE


def pieces():
    out = [("xT", 0, KD * TB * P, 0), ("wqkvg", 0, 4 * D, W_QKVG), ("wqkvg", 4 * D, 4 * D, W_QKVG + 4 * D),
           ("xT", KD * TB * P, KD * TB * P, TB * P)]
    rest = [("wo", W_O0, 2 * KD * D, 1024), ("wqkv1", W_QKV1, KD * 3 * D, 768), ("wup", W_UP, KD * 2 * HID, STAGE),
            ("wdown", None, (HK - 1) * D, 1024), ("wtail", W_TAIL, D + KD * NR, STAGE)]
    for name, first, n, step in rest:
        for a in range(0, n, step):
            at = first + a if name != "wdown" else a if a < 8 * D else W_DOWN + a - 8 * D
            out.append((name, a, min(step, n - a), at))
    return out


PIECES = pieces()


COST = {
    "split": "A1.07 D1.49", "bias": "A1.23 D1.39", "wsum": "A2.70", "gsum": "T0.07 D1.07", "quant": "D1.50",
    "proj": "T3.18 A1.00 d0.73 p1.76", "rot": "D0.94", "tqk": "T1.17 A0.50", "sc": "T0.90 A0.50 p0.60",
    "kv": "T0.49 D1.77", "ret": "T1.60 A0.30 D0.95 d0.80 p4.40", "gn": "D2.35", "ty": "T0.18 A0.30 D0.40",
    "wo": "T0.74 D0.72 d0.66 p0.70", "ln": "D0.29", "tx": "T0.20 A0.30 D0.46", "up": "T1.70 A0.60 D0.67",
    "cut": "A0.50 P2.26", "dn": "T1.09 D0.44 d0.66 p0.79", "qk": "T3.01 A1.79 D1.08", "tq": "T0.90 A1.00 D1.76",
    "mx": "T0.55 D0.96", "tm": "T0.55 A1.76", "se": "T0.31 A0.80 p0.60", "pv": "T1.10 A0.18", "ya": "T0.54 D0.60",
    "rt": "T0.41 D0.25 d0.75", "rc": "A0.42 D1.30", "mu": "T1.80 A0.31 D1.22", "mt": "T1.01 A1.20 D1.10",
    "md": "T3.68 D0.44 d0.74 p0.59"
}
HOP = 0.152
CROSS = 0.929
LATE = 11
SLACK = 0.789
NUDGE = {
    ("sc", 3, 0): 10.1, ("mu", 4, 4): -17.9, ("mx", 0, 2, 4): 0.7, ("ln", 3, 1): 68.6, ("split", 2): -75.4,
    ("mu", 2, 3): -54.5, ("ln", 1, 7): 38.7, ("pv", 1, 0, 1): 11.0, ("mt", 4, 0): 37.9, ("ln", 1, 5): -9.3,
    ("mu", 5, 3): 17.1
}
URGE = {
    "cuta": 18.4, "cutb": 32.7, "dna": -2.0, "dnb": 19.8, "gna": 22.1, "gnb": -2.3, "gsum": -1.1, "kva": 43.1,
    "kvb": -1.5, "ln0b": -2.0, "ln1b": -52.0, "ln2a": -25.1, "ln2b": 11.4, "ln3a": -33.7, "ln3b": -6.7, "mda": 14.4,
    "mdb": 14.0, "mta": -27.2, "mtb": -21.5, "mxb": 1.3, "projb": -2.4, "qka": -11.2, "qkb": -28.0, "quant": 1.5,
    "rca": -17.9, "rcb": -45.8, "reta": -29.7, "retb": -17.8, "rota": 2.5, "rotb": 2.5, "rta": -5.5, "rtb": -1.9,
    "sea": 10.7, "split": 37.8, "tqa": -31.1, "tqb": -6.3, "tqka": -22.2, "tx0a": -10.1, "tx0b": -9.5, "tx1a": -9.5,
    "tx2b": -17.8, "ty0b": -0.2, "ty2a": -7.8, "ty2b": -20.0, "upb": -37.5, "wo0a": -4.7, "wo2a": -29.8, "wo2b": 0.6,
    "wsum": -2.6
}


def dependences():
    need = {}

    def add(step, *after):
        need[step] = [x for x in after if x]

    def at(condition, step):
        return step if condition else None

    for i, (name, _, _, first) in enumerate(PIECES):
        add(("split", i), at(i, ("split", i - 1)), at(i > LATE, pv_at(i - LATE - 1) if i - LATE - 1 < 16 else None))
    add(("bias", 0), ("split", 1))
    add(("bias", 1), ("bias", 0), ("split", 4))
    for i in range(3):
        add(("wsum", i), ("split", 4), at(i, ("wsum", i - 1)))
        add(("quant", i), ("gsum",))
    add(("gsum",), ("wsum", 2))
    for t in range(NT):
        b, i = divmod(t, TB)
        add(("proj", t), ("split", 3 if b else 2), ("bias", 0), at(t > 1, ("rot", t - 2)), at(t > 3, ("ret", t - 4)),
            at(t > 3 and i < TB - 1, ("kv", t - 4)))
        add(("rot", t), ("proj", t), at(t > 1, ("tqk", t - 2)), at(t > 1 and (t - 2) % TB < TB - 1, ("kv", t - 2)))
        add(("tqk", t), ("rot", t), at(t > 2, ("ret", t - 3)))
        for hf in range(2):
            add(("sc", t, hf), ("tqk", t), at(hf, ("sc", t, 0)), at(t > 1, ("ret", t - 2)))
        if i < TB - 1:
            add(("kv", t), ("rot", t), at(i, ("kv", t - 1)), at(t >= TB, ("ret", TB - 1)))
        add(("ret", t), ("sc", t, 0), ("sc", t, 1), at(i, ("kv", t - 1)), at(t > 1, ("gn", t - 2)))
        add(("gn", t), ("ret", t), at(t > 1, ("ty", 0, t - 2)))
    for layer, mixed in ((0, "gn"), (2, "ya")):
        for t in range(NT):
            b, i = divmod(t, TB)
            if layer:
                add(("ya", b, i), ("pv", b, AH // 4 - 1, TB - 1), at(t > 1, ("ty", 2, t - 2)))
            last = ("wo", layer, t - 1) if t else at(layer, ("wo", 0, NT - 1))
            add(("ty", layer, t), (mixed, b, i) if layer else (mixed, t), last)
            add(("wo", layer, t), ("ty", layer, t), ("split", 4), at(t > 1, ("ln", layer, t - 2)))
    for layer, of in enumerate(("wo", "dn", "wo", "md")):
        for t in range(NT):
            add(("ln", layer, t), (of, layer, t) if of == "wo" else (of, t))
            if layer < 3:
                add(("tx", layer, t), ("ln", layer, t))
    for b in range(NB):
        tiles = range(b * TB, b * TB + TB)
        for m in range(FM):
            add(("up", b, m), *(("tx", 0, t) for t in tiles), ("quant", 2), at(m > 1, ("cut", b, m - 2)),
                at(b and m < 2, ("cut", 0, FM - 2 + m)))
            add(("cut", b, m), ("up", b, m), at(b, ("dn", TB - 1)))
        for t in tiles:
            i = t % TB
            add(("dn", t), ("cut", b, FM - 1), at(t > 1, ("ln", 1, t - 2)))
            add(("qk", b, i), ("tx", 1, t), ("split", 6), ("bias", 1), ("wo", 0, NT - 1), at(b, ("tm", 0, i)))
            add(("tq", b, i), ("qk", b, i), at(b, ("se", 0, AH // 4 - 1, TB - 1, 0)))
            for h in range(0, AH, mx_heads(i)):
                add(("mx", b, i, h), ("tq", b, i))
            add(("tm", b, i), ("mx", b, i, AH - mx_heads(i)))
        for g in range(AH // 4):
            for j in range(TB):
                n = (b * AH // 4 + g) * TB + j
                for s in range(0, 4, se_heads(j)):
                    add(("se", b, g, j, s), ("tm", b, TB - 1), at(n > 1, pv_at(n - 2)))
                add(("pv", b, g, j), ("se", b, g, j, 4 - se_heads(j)))
    for t in range(NT):
        add(("rt", t), ("tx", 2, t), ("split", len(PIECES) - 1), at(t > 1, ("mu", t - 2, MC - 1)))
        add(("rc", t), ("rt", t))
        for c in range(MC):
            add(("mu", t, c), ("rc", t), ("dn", NT - 1), at(t, ("mt", t - 1, 0)), at(t and c > 1, ("mt", t - 1, 1)),
                at(t and c > 2, ("mt", t - 1, 2)))
        for part, c in ((0, 2), (1, MC - 1), (2, MC - 1)):
            add(("mt", t, part), ("mu", t, c), at(t > 1, ("md", t - 2)))
        add(("md", t), ("mt", t, 2), at(t > 1, ("ln", 3, t - 2)))
    return need


def pv_at(n):
    return ("pv", n // (AH // 4 * TB), n // TB % (AH // 4), n % TB)


def engine_times(step):
    out = [(w[0], float(w[1:])) for w in COST[step[0]].split()]
    part = {"mx": lambda: mx_heads(step[2]) * (step[2] + 1) / 6, "se": lambda: se_heads(step[3]) * (TB - step[3]) / 6.4,
            "pv": lambda: (TB - step[3]) * 0.35}.get(step[0])
    if part:
        out = [(e, w * part()) for e, w in out]
    return out


def name_of(step):
    kind = step[0]
    if kind in ("split", "bias", "wsum", "gsum", "quant"):
        return kind
    if kind in ("ty", "wo", "ln", "tx"):
        return kind + str(step[1]) + "ab"[step[2] // TB]
    return kind + "ab"[step[1] if kind in ("up", "cut", "qk", "tq", "mx", "tm", "se", "pv", "ya") else step[1] // TB]


def schedule():
    need = dependences()
    after = {step: [] for step in need}
    last_of_kind = {}
    for step in need:
        key = step[:2] if step[0] in ("ln", "tx") else step[0]
        if key in last_of_kind:
            need[step].append(last_of_kind[key])
        last_of_kind[key] = step
        for x in need[step]:
            after[x].append(step)
    ordered = {}
    while len(ordered) < len(need):
        ordered.update({step: True for step in need if step not in ordered and all(x in ordered for x in need[step])})
    span = {}
    for step in reversed(ordered):
        span[step] = sum(w for _, w in engine_times(step)) + max((span[x] for x in after[step]), default=0)
    order = []
    free = dict.fromkeys("TADP", 0.0)
    tiles = {("A", i): [i - 9, 0.0] for i in range(RING_A)}
    tiles.update({("B", i): [i - 9, 0.0] for i in range(RING_B)})
    kept = None
    end, tile_of = {}, {}
    landed = [4.1 + 1.6 * i + (1.5 if i > 2 else 0) for i in range(5)]
    left = {step: len(x) for step, x in need.items()}
    ready = [step for step in need if not left[step]]
    while ready:
        best = []
        for step in ready:
            times = engine_times(step)
            start = max([end[x] - (2.0 if step[0] == "md" and x[0] == "mt" else 0.0) for x in need[step]]
                        + [free[times[0][0]]])
            if step[0] == "split" and step[1] < len(landed):
                start = max(start, landed[step[1]])
            tile = None
            if step[0] in RING_OF:
                ring = "B" if step[0] == "mt" and step[2] == 2 else RING_OF[step[0]]
                if step[0] == "pv" and step[3]:
                    tile = kept
                else:
                    fit = [x for x in tiles if x != kept and ring in (x[0], "B")]
                    tile = min(fit, key=lambda x: (max(start, tiles[x][1]) + (CROSS if x[0] != ring else 0.0), tiles[x][0]))
                    start = max(start, tiles[tile][1])
            best.append((start, step, tile))
        first = min(x[0] for x in best)
        start, step, tile = max((x for x in best if x[0] <= first + SLACK), key=lambda x: (
            span[x[1]] + URGE.get(name_of(x[1]), 0.0) + NUDGE.get(x[1], 0.0), -x[0]))
        ready.remove(step)
        now = start
        for e, w in engine_times(step):
            now = max(now, free[e.upper()]) + w
            free[e.upper()] = now
            now += HOP
            if e.isupper():
                read_out = now
        end[step] = now
        if tile:
            tiles[tile] = [len(order), read_out]
            tile_of[step] = tile
            if step[0] == "pv":
                kept = tile if step[3] < TB - 1 else None
        order.append(step)
        for x in after[step]:
            left[x] -= 1
            if not left[x]:
                ready.append(x)
    assert len(order) == len(need)
    return order, tile_of


RING_A, RING_B = 3, 2
RING_OF = {"proj": "A", "tqk": "B", "sc": "A", "kv": "B", "ret": "B", "ty": "B", "wo": "B", "tx": "B",
           "gsum": "B", "up": "A", "dn": "B", "qk": "A", "tq": "A", "mx": "A", "tm": "B", "se": "A",
           "pv": "B", "ya": "B", "rt": "B", "mu": "A", "mt": "A", "md": "B"}

SCHEDULE, TILE_OF = schedule()


def occurrences():
    seen, out = {}, {}
    for step in SCHEDULE:
        key = step[:2] if step[0] in ("ln", "tx") else step[0]
        seen[key] = seen.get(key, 0) + 1
        out[step] = seen[key]
    return out


NTH = occurrences()
LAYER = {"dn": 1, "md": 3}


def psum_places():
    user, done, out = {}, 0, {}
    for step in SCHEDULE:
        if step[0] not in RING_OF:
            continue
        done += 1
        tile, before = TILE_OF[step], None
        if step[0] != "pv" or step[3] == 0:
            before = user.get(tile)
            user[tile] = step
        out[step] = (*tile, before, done)
    return out


PLACE = psum_places()


def build_two_layers(nc: bass.Bass, xT, x, wqkvg, wo, wqkv1, wup, wdown, wtail, w12, w3, bias_rows, gnorm_rows,
                     consts, consts16, block_decay, out):
    f32, f16, u32 = mybir.dt.float32, mybir.dt.float16, mybir.dt.uint32
    ALU, ACT, AX = mybir.AluOpType, mybir.ActivationFunctionType, mybir.AxisListType
    source = {"xT": xT, "wqkvg": wqkvg, "wo": wo, "wqkv1": wqkv1, "wup": wup, "wdown": wdown, "wtail": wtail}

    with ExitStack() as ctx:
        def sb(name, shape, dt=f32):
            return ctx.enter_context(nc.sbuf_tensor(name, shape, dt))

        def sem(name):
            return ctx.enter_context(nc.semaphore(name))

        ws = sb("cut_weights", [P, 2, W_TOT], f16)
        stage = sb("stage", [P, NSTAGE, STAGE])
        X = sb("residual", [P, NT, D])
        XT = sb("x_transposed", [P, 2, KD, NT * P], f16)
        con = sb("constants", [P, C_TOT])
        con16 = sb("constants16", [P, 3 * P], f16)
        bias = sb("bias_rows", [P, 9 * D], f16)
        Y = sb("y", [P, 2, D])
        YT = sb("y_transposed", [P, 2, D], f16)
        Z = sb("z", [P, 4, D])
        stats = sb("ln_stats", [P, 4, 6])
        mv = sb("ln_mean_var", [P, 4, 2])
        veps = sb("ln_var_eps", [P, 4])
        rstd = sb("ln_rstd", [P, 4])
        half = sb("minus_half", [P, RH])
        gs = sb("weight_sums", [P, 4])
        thr = sb("thresholds", [P, 3])
        small = sb("router", [P, 2, 64])
        small_i = sb("router_index", [P, 2, 8], u32)

        arena1 = sb("arena_mixers", [P, 18480])
        arena2 = sb("arena_ffn", [P, 7872])

        class Carve:
            def __init__(self, arena):
                self.arena, self.at = arena, 0

            def __call__(self, dims, dt=f32):
                n = int(np.prod(dims)) // (2 if dt == f16 else 1)
                view = self.arena[:, self.at:self.at + n]
                self.at += n
                assert self.at <= self.arena.shape[1], self.at
                if dt == f16:
                    view = view.bitcast(f16)
                if len(dims) == 1:
                    return view
                names = "abcdef"[:len(dims)]
                return view.rearrange(f"p ({' '.join(names)}) -> p {' '.join(names)}",
                                      **{c: d for c, d in zip(names, dims)})

        cut = Carve(arena1)
        bias_raw = cut([9 * D])
        gnorm = cut([2 * D])
        tab_cos = cut([TB, 2 * RH, RD // 2])
        tab_sin = cut([TB, 2 * RH, RD // 2])
        QK0 = cut([2, 2 * D])
        VG = cut([4, 2 * D])
        ROT = cut([2, 2 * D])
        R1 = cut([2, 2 * D])
        R2 = cut([2, 2 * D])
        QKT = cut([3, 4, P])
        PT = cut([2, 2, 2, 2, P])
        TS = cut([TB - 1, D])
        block_g = cut([D])
        ones = cut([P])
        KVM = cut([D])
        CENT = cut([2, D])
        SQ = cut([D])
        GA = cut([2, D])
        GC = cut([2, D])
        TH = cut([2, D])
        gsmall = cut([2, 4, RH])
        cut = Carve(arena1)
        ST = cut([TB, 2, AH, 64], f16)
        QT = cut([AH // 2, TB * P], f16)
        KT = cut([AH // 2, TB * P], f16)
        V = cut([NT, AH, 32])
        PE1 = cut([2, 4, TB * P])
        YU = cut([AH // 4, TB * P])
        rden = cut([2, AH])
        cut = Carve(arena2)
        Q12 = cut([KD, 2 * F0], f16)
        Q3 = cut([FM, D], f16)
        work_at = cut.at
        raw12 = cut([KD, 2 * F0])
        raw3 = cut([FM, D])
        cut.at = work_at
        HT0 = cut([2, FM, TB * P], f16)
        HF = cut([2, TB * P])
        THF = cut([2, TB * P])
        cut = Carve(arena2)
        H = cut([HID])
        HT = cut([2, 2, HK, P], f16)
        TG = cut([2, MCW])
        AG = cut([2, MCW])

        psA = [ctx.enter_context(nc.psum_tensor(f"psum_a{i}", [P, 2, 512], f32)) for i in range(RING_A)]
        psB = [ctx.enter_context(nc.psum_tensor(f"psum_b{i}", [P, 512], f32)) for i in range(RING_B)]

        def psum(step):
            ring, at, _, _ = PLACE[step]
            if ring == "B":
                return psB[at]
            return psA[at][:, 0, :] if RING_OF[step[0]] == "B" or (step[0] == "mt" and step[2] == 2) else psA[at]

        def by_row_tile(ps, heads):
            return ps[:, :, :].rearrange("p s (h k) -> p s h k", h=heads // 2)

        def psum16(step):
            ring, at, _, _ = PLACE[step]
            if ring == "B":
                return psB[at][:, :].bitcast(f16)
            return psA[at][:, 0, :].bitcast(f16) if RING_OF[step[0]] == "B" else psA[at][:, :, :].bitcast(f16)

        pe_done = sem("pe_done")
        piece_in = [sem(f"piece_in{i}") for i in range(len(PIECES))]
        head_cut, rest_cut = sem("head_cut"), sem("rest_cut")
        con_in, con16_in, bias_in, gnorm_in = (sem(n) for n in ("con_in", "con16_in", "bias_in", "gnorm_in"))
        x_in = [sem(f"x_in{b}") for b in range(NB)]
        raw_in = sem("raw_in")
        tables, ready0 = sem("tables_ready"), sem("memsets_done")
        bias_head, bias_cut = sem("bias_heads"), sem("bias_cut")
        block_in = sem("block_in")
        evac0, rot1, rot2, rotated = sem("qkvg_copied"), sem("rot_first_term"), sem("rot_second_term"), sem("rotated")
        sc_copied = sem("scores_copied")
        qkT, pT, state = sem("qk_transposed"), sem("masked_scores"), sem("state_ready")
        tanh0, gates, gvar, grstd = sem("gate_tanh"), sem("gates_ready"), sem("gn_var"), sem("gn_rstd")
        y_ready, y_head, y_rest = sem("y_ready"), sem("y_head"), sem("y_rest")
        ln_var, ln_rstd, ln_done, z_ready, x_head, x_rest = (
            [sem(f"{what}{layer}") for layer in range(4)]
            for what in ("ln_var", "ln_rstd", "ln_done", "z_ready", "x_head", "x_rest"))
        sums, quant = sem("weight_sums_ready"), sem("quantized")
        up_tanh, hidden, h_head, h_rest = sem("up_tanh"), sem("hidden"), sem("h_head"), sem("h_rest")
        st_head, st_rest, qkv_copied = sem("stack_heads"), sem("stack_rests"), sem("qkv_copied")
        centered = sem("centered")
        thresholds, logit_read = sem("thresholds_ready"), sem("logits_read")
        q_up, k_up = sem("q_stack_transposed"), sem("k_stack_transposed")
        maxed, q_max = sem("row_max"), sem("q_max_transposed")
        exped, causal, yu = sem("exp_done"), sem("causal_done"), sem("pv_copied")
        v_init = sem("v_columns_set")
        logits, r_exp = sem("logits"), sem("router_exp")
        mu_tanh, mu_h, mt_head, mt_rest = sem("mu_tanh"), sem("mu_hidden"), sem("mt_head"), sem("mt_rest")
        dve_order, pool_order, out_done = sem("dve_order"), sem("pool_order"), sem("out_done")

        ident = con[:, C_ID:C_ID + P]
        ident16 = con16[:, 0:P]
        below16 = con16[:, P:2 * P]
        pick16 = con16[:, 2 * P:3 * P]

        def split_views(i, a):
            name, _, cols, first = PIECES[i]
            piece = stage[:, i % NSTAGE, 0:cols]
            if name == "xT":
                return XT[:, a, :, first:first + TB * P], piece.rearrange("p (k t) -> p k t", k=KD)
            return ws[:, a, first:first + cols], piece

        block = ctx.enter_context(nc.Block())

        @block.sync
        def _(sp):
            def load(i):
                name, a, n, _ = PIECES[i]
                if i >= NSTAGE:
                    sp.wait_ge(rest_cut, NTH[("split", i - NSTAGE)])
                sp.dma_start(stage[:, i % NSTAGE, 0:n], source[name][:, a:a + n]).then_inc(piece_in[i], 16)

            load(0)
            load(1)
            sp.dma_start(bias_raw[0:2, :], bias_rows.partition_broadcast(2)).then_inc(bias_in, 16)
            load(2)
            sp.dma_start(con[:, :], consts).then_inc(con_in, 16)
            sp.dma_start(con16[:, :], consts16).then_inc(con16_in, 16)
            sp.dma_start(gnorm, gnorm_rows.partition_broadcast(P)).then_inc(gnorm_in, 16)
            load(3)
            sp.dma_start(block_g, block_decay).then_inc(block_in, 16)
            sp.dma_start(X[:, 0:TB, :], x[0:TB * P, :].rearrange("(t p) d -> p t d", p=P)).then_inc(x_in[0], 16)
            load(4)
            sp.dma_start(raw12, w12.rearrange("(k p) n -> p k n", p=P)).then_inc(raw_in, 16)
            sp.dma_start(raw3[:, 0:FM - 1, :], w3[0:(FM - 1) * P, :].rearrange("(k p) n -> p k n", p=P)).then_inc(raw_in, 16)
            sp.dma_start(raw3[0:LAST, FM - 1, :], w3[(FM - 1) * P:F0, :]).then_inc(raw_in, 16)
            sp.dma_start(X[:, TB:NT, :], x[TB * P:NT * P, :].rearrange("(t p) d -> p t d", p=P)).then_inc(x_in[1], 16)
            for i in range(5, len(PIECES)):
                load(i)
            for t in range(NT):
                sp.wait_ge(ln_done[3], NTH[("ln", 3, t)])
                sp.dma_start(out[t * P:(t + 1) * P, :], X[:, t, :]).then_inc(out_done, 16)
            sp.wait_ge(out_done, 16 * NT)

        @block.tensor
        def _(pe):
            mm = nc.tensor.matmul

            reader = {"proj": evac0, "tqk": qkT, "sc": sc_copied, "kv": state, "ret": centered, "ty": y_rest,
                      "gsum": thresholds, "up": hidden, "mx": maxed, "tm": q_max, "se": exped,
                      "ya": y_ready, "rt": logit_read, "mu": mu_h, "mt": mt_rest}

            def claim(step):
                last = PLACE[step][2]
                if last is None:
                    return
                if last[0] == "tq":
                    pe.wait_ge(q_up, NTH[last])
                    pe.wait_ge(k_up, NTH[last])
                elif last[0] == "qk":
                    pe.wait_ge(st_rest, NTH[last])
                    pe.wait_ge(qkv_copied, NTH[last])
                elif last[0] == "pv":
                    pe.wait_ge(yu, NTH[("pv", last[1], last[2], TB - 1)] // TB)
                elif last[0] in ("wo", "dn", "md"):
                    layer = LAYER.get(last[0], last[1])
                    pe.wait_ge(z_ready[layer], NTH[("ln", layer, last[-1])])
                elif last[0] == "tx":
                    pe.wait_ge(x_rest[last[1]], NTH[last])
                elif last[0] == "ya":
                    pe.wait_ge(y_ready, NTH[("ty", 2, last[1] * TB + last[2])])
                else:
                    pe.wait_ge(reader[last[0]], NTH[last])

            def cut_product(out_of, lhs, rhs, bias_at=None, ready=None):
                n = len(lhs)
                ins = None
                for k in range(n):
                    if ready:
                        ready(k)
                    for a, b in ((0, 0), (0, 1), (1, 0)):
                        for dst, col in out_of:
                            ins = mm(dst, lhs[k][a], rhs(k, b, col), start=(k == 0 and a == 0 and b == 0),
                                     stop=(bias_at is None and k == n - 1 and a == 1))
                if bias_at is not None:
                    if ready:
                        ready(n)
                    for dst, col in out_of:
                        at = bias_at + col
                        ins = mm(dst, pick16, bias[:, at:at + dst.shape[-1]], start=False, stop=True)
                return ins

            def x_tiles(t):
                return [[XT[:, a, k, t * P:(t + 1) * P] for a in range(2)] for k in range(KD)]

            for step in SCHEDULE:
                kind = step[0]
                if kind not in RING_OF:
                    continue
                ps = psum(step)
                if kind == "proj":
                    t = step[1]
                    if t == 0:
                        pe.wait_ge(rest_cut, NTH[("split", 0)])
                    if t == TB:
                        pe.wait_ge(rest_cut, NTH[("split", 3)])
                    claim(step)
                    w = ws[:, :, W_QKVG:W_O0].rearrange("p a (k n) -> p a k n", k=KD)

                    def weights(k):
                        if k < KD:
                            pe.wait_ge(rest_cut, NTH[("split", 1 + k)])
                        else:
                            pe.wait_ge(bias_cut, 1)
                            pe.wait_ge(con16_in, 16)
                    ins = cut_product([(ps[:, 0, :], 0), (ps[:, 1, :], 512)], x_tiles(t),
                                      lambda k, b, c: w[:, b, k, c:c + 512], 0, None if t else weights)
                elif kind == "tqk":
                    t = step[1]
                    pe.wait_ge(rotated, t + 1)
                    claim(step)
                    for j in range(4):
                        ins = nc.tensor.transpose(ps[:, j * P:(j + 1) * P], ROT[:, t % 2, j * P:(j + 1) * P], ident)
                elif kind == "sc":
                    _, t, hf = step
                    pe.wait_ge(qkT, t + 1)
                    claim(step)
                    for g in range(2):
                        for s in range(2):
                            r = 32 * (2 * hf + s)
                            ins = mm(ps[:, s, g * P:(g + 1) * P], QKT[r:r + 32, t % 3, 2 + g, :],
                                     QKT[r:r + 32, t % 3, g, :], start=True, stop=True)
                elif kind == "kv":
                    t = step[1]
                    pe.wait_ge(rotated, t + 1)
                    claim(step)
                    for g in range(2):
                        ins = mm(ps[:, g * P:(g + 1) * P], ROT[:, t % 2, D + g * P:D + (g + 1) * P],
                                 VG[:, t % 4, g * P:(g + 1) * P], start=True, stop=True)
                elif kind == "ret":
                    t = step[1]
                    c = t % TB
                    pe.wait_ge(pT, NTH[("sc", t, 1)])
                    if c:
                        pe.wait_ge(state, NTH[("kv", t - 1)])
                    claim(step)
                    if t == 0:
                        pe.wait_ge(con_in, 16)
                    if c:
                        for g in range(2):
                            mm(ps[:, g * P:(g + 1) * P], QKT[:, t % 3, g, :], TS[:, c - 1, g * P:(g + 1) * P],
                               start=(g == 0), stop=False, skip_group_check=True)
                    for h in range(RH):
                        g, s = divmod(h, 4)
                        ins = mm(ps[:, h * RD:(h + 1) * RD], PT[:, t % 2, s // 2, s % 2, g, :],
                                 VG[:, t % 4, h * RD:(h + 1) * RD],
                                 start=(h == 0 and not c), stop=(h == RH - 1), skip_group_check=True)
                elif kind == "ty":
                    pe.wait_ge(y_ready, NTH[step])
                    claim(step)
                    for k in range(KD):
                        ins = nc.tensor.transpose(ps[:, k * P:(k + 1) * P], Y[:, NTH[step] % 2, k * P:(k + 1) * P], ident)
                elif kind == "wo":
                    _, layer, t = step
                    pe.wait_ge(y_rest, NTH[step])
                    if layer == 0 and t == 0:
                        pe.wait_ge(rest_cut, NTH[("split", 4)])
                    claim(step)
                    first = W_O1 if layer else W_O0
                    w = ws[:, :, first:first + KD * D].rearrange("p a (k n) -> p a k n", k=KD)
                    ins = cut_product([(ps[:, 0:D], 0)], [[YT[:, a, k * P:(k + 1) * P] for a in range(2)] for k in range(KD)],
                                      lambda k, b, c: w[:, b, k, :], (8 if layer else 4) * D)
                elif kind == "tx":
                    _, layer, t = step
                    pe.wait_ge(ln_done[layer], NTH[("ln", layer, t)])
                    claim(step)
                    for k in range(KD):
                        ins = nc.tensor.transpose(ps[:, k * P:(k + 1) * P], X[:, t, k * P:(k + 1) * P], ident)
                elif kind == "gsum":
                    pe.wait_ge(sums, 3)
                    claim(step)
                    ins = mm(ps[:, 0:4], ones, gs[:, :], start=True, stop=True)
                elif kind == "up":
                    _, n, m = step
                    rows = P if m < FM - 1 else LAST
                    if m == 0:
                        pe.wait_ge(x_rest[0], NTH[("tx", 0, TB * n + TB - 1)])
                        pe.wait_ge(quant, 3)
                    claim(step)
                    for k in range(KD):
                        for gu in range(2):
                            w = Q12[:, k, gu * F0 + m * P:gu * F0 + m * P + rows]
                            for a in range(2):
                                ins = mm(ps[0:rows, gu, :], w, XT[:, a, k, n * TB * P:(n + 1) * TB * P],
                                         start=(k == 0 and a == 0), stop=(k == KD - 1 and a == 1))
                elif kind == "dn":
                    t = step[1]
                    claim(step)
                    c = (t % TB) * P
                    for m in range(FM):
                        rows = P if m < FM - 1 else LAST
                        if t % TB == 0:
                            pe.wait_ge(h_rest, NTH[("cut", t // TB, m)])
                            pe.wait_ge(h_head, NTH[("cut", t // TB, m)])
                        for a in range(2):
                            ins = mm(ps[:, 0:D], HT0[0:rows, a, m, c:c + P], Q3[0:rows, m, :],
                                     start=(m == 0 and a == 0), stop=(m == FM - 1 and a == 1))
                elif kind == "qk":
                    _, b, i = step
                    t = b * TB + i
                    pe.wait_ge(x_rest[1], NTH[("tx", 1, t)])
                    claim(step)
                    if (b, i) == (0, 0):
                        pe.wait_ge(rest_cut, NTH[("split", 6)])
                        pe.wait_ge(bias_cut, 2)
                    w = ws[:, :, W_QKV1:W_UP].rearrange("p a (k n) -> p a k n", k=KD)
                    ins = cut_product([(ps[:, 0, :], 0), (ps[:, 1, 0:D], 512)], x_tiles(t),
                                      lambda k, b_, c: w[:, b_, k, c:c + (D if c else 512)], 5 * D)
                elif kind == "tq":
                    _, b, i = step
                    pe.wait_ge(st_rest, NTH[("qk", b, i)])
                    pe.wait_ge(qkv_copied, NTH[("qk", b, i)])
                    claim(step)
                    p16 = psum16(step)
                    for w in range(2):
                        for p in range(AH // 2):
                            ins = nc.tensor.transpose(p16[:, w, p * P:(p + 1) * P],
                                                      ST[:, i, w, 2 * p:2 * p + 2, :], ident16)
                elif kind == "mx":
                    _, b, i, h0 = step
                    if h0 == 0:
                        pe.wait_ge(q_up, NTH[("tq", b, i)])
                        pe.wait_ge(k_up, NTH[("tq", b, i)])
                    claim(step)
                    out_of = by_row_tile(ps, mx_heads(i))
                    for h in range(mx_heads(i)):
                        mm(out_of[:, h % 2, h // 2, i * P:(i + 1) * P], ident16, below16, start=True, stop=True)
                    for h in range(mx_heads(i)):
                        p, r = (h0 + h) // 2, 64 * (h % 2)
                        ins = mm(out_of[:, h % 2, h // 2, 0:(i + 1) * P], QT[r:r + 64, p, i * P:(i + 1) * P],
                                 KT[r:r + 64, p, 0:(i + 1) * P], start=False, stop=True, skip_group_check=True)
                elif kind == "tm":
                    _, b, i = step
                    pe.wait_ge(maxed, NTH[("mx", b, i, AH - mx_heads(i))])
                    claim(step)
                    p16 = psum16(step)
                    for p in range(AH // 2):
                        ins = nc.tensor.transpose(p16[:, p * P:(p + 1) * P], ST[:, i, 0, 2 * p:2 * p + 2, :], ident16)
                elif kind == "se":
                    _, b, g, j, s0 = step
                    pe.wait_ge(q_max, NTH[("tm", b, TB - 1)])
                    claim(step)
                    out_of = by_row_tile(ps, se_heads(j))
                    for h in range(se_heads(j)):
                        p, r = 2 * g + (s0 + h) // 2, 64 * (h % 2)
                        ins = mm(out_of[:, h % 2, h // 2, 0:(TB - j) * P], KT[r:r + 64, p, j * P:(j + 1) * P],
                                 QT[r:r + 64, p, j * P:TB * P], start=True, stop=True)
                elif kind == "pv":
                    _, b, g, j = step
                    pe.wait_ge(causal, NTH[("se", b, g, j, 4 - se_heads(j))])
                    if step == ("pv", 0, 0, 0):
                        pe.wait_ge(v_init, 1)
                    if j == 0:
                        claim(step)
                    for s in range(4):
                        ins = mm(ps[32 * s:32 * s + 32, j * P:TB * P], V[:, b * TB + j, 4 * g + s, :],
                                 PE1[:, j % 2, s, 0:(TB - j) * P], start=(j == 0), stop=(j == TB - 1))
                elif kind == "ya":
                    _, b, i = step
                    pe.wait_ge(yu, NTH[("pv", b, AH // 4 - 1, TB - 1)] // TB)
                    claim(step)
                    for g in range(AH // 4):
                        ins = nc.tensor.transpose(ps[:, g * P:(g + 1) * P], YU[:, g, i * P:(i + 1) * P], ident)
                elif kind == "rt":
                    t = step[1]
                    pe.wait_ge(x_rest[2], NTH[("tx", 2, t)])
                    pe.wait_ge(rest_cut, len(PIECES))
                    claim(step)
                    w = ws[:, :, W_ROUT:W_TOT].rearrange("p a (k n) -> p a k n", k=KD)
                    ins = cut_product([(ps[:, 0:NR], 0)], x_tiles(t), lambda k, b, c: w[:, b, k, :])
                elif kind == "mu":
                    _, t, c = step
                    claim(step)
                    w = ws[:, :, W_UP:W_DOWN].rearrange("p a (k c u n) -> p a k c u n", k=KD, c=MC, u=2)
                    ins = cut_product([(ps[:, 0, 0:MCW], 0), (ps[:, 1, 0:MCW], 1)], x_tiles(t),
                                      lambda k, b, u: w[:, b, k, c, u, :])
                elif kind == "mt":
                    _, t, part = step
                    if part == 0:
                        pe.wait_ge(mu_h, NTH[("mu", t, 2)])
                        claim(step)
                        for k in range(8):
                            ins = nc.tensor.transpose(ps[:, k // 4, (k % 4) * P:(k % 4 + 1) * P], H[:, k * P:(k + 1) * P], ident)
                    elif part == 1:
                        pe.wait_ge(mu_h, NTH[("mu", t, MC - 1)])
                        claim(step)
                        for k in range(8):
                            ins = nc.tensor.transpose(ps[:, k // 4, (k % 4) * P:(k % 4 + 1) * P],
                                                      H[:, (8 + k) * P:(9 + k) * P], ident)
                    else:
                        claim(step)
                        ins = nc.tensor.transpose(ps[0:LAST, 0:P], H[:, 16 * P:HID], ident)
                elif kind == "md":
                    t = step[1]
                    claim(step)

                    def rows(k):
                        return LAST if k == HK - 1 else P

                    def hidden_rows(k):
                        if k % 8 == 0:
                            pe.wait_ge(mt_rest, NTH[("mt", t, k // 8)])

                    def down(k):
                        return k * D if k < 8 else W_DOWN + (k - 8) * D
                    ins = cut_product([(ps[:, 0:D], 0)], [[HT[0:rows(k), t % 2, a, k, :] for a in range(2)] for k in range(HK)],
                                      lambda k, b, c: ws[0:rows(k), b, down(k):down(k) + D], None, hidden_rows)
                ins.then_inc(pe_done, 1)

        @block.scalar
        def _(act):
            for step in SCHEDULE:
                kind, n = step[0], NTH[step]
                ps = psum(step) if kind in RING_OF else None
                if kind == "split":
                    i = step[1]
                    name, _, cols, first = PIECES[i]
                    if name == "wdown" and first == 0:
                        act.wait_ge(pe_done, PLACE[("proj", NT - 1)][3])
                    act.wait_ge(piece_in[i], 16)
                    dst, src = split_views(i, 0)
                    nc.scalar.activation(dst, src, ACT.Copy, scale=SA if name == "xT" else SW).then_inc(head_cut, 1)
                elif kind == "bias":
                    if n == 1:
                        act.wait_ge(bias_in, 16)
                        act.wait_ge(ready0, 4)
                    w = slice(0, 5 * D) if n == 1 else slice(5 * D, 9 * D)
                    nc.scalar.activation(bias[0:2, w], bias_raw[0:2, w], ACT.Copy, scale=SW).then_inc(bias_head, 1)
                elif kind == "proj":
                    t = step[1]
                    act.wait_ge(pe_done, PLACE[step][3])
                    if t >= 2:
                        act.wait_ge(rot1, t - 1)
                        act.wait_ge(rot2, t - 1)
                    if t >= 4:
                        act.wait_ge(gates, t - 3)
                    nc.scalar.activation(QK0[:, t % 2], ps[:, 0, :], ACT.Copy, scale=UN)
                    nc.scalar.activation(VG[:, t % 4], ps[:, 1, :], ACT.Copy, scale=UN).then_inc(evac0, 1)
                elif kind == "sc":
                    _, t, hf = step
                    act.wait_ge(pe_done, PLACE[step][3])
                    nc.scalar.activation(PT[:, t % 2, hf], ps[:, :, 0:2 * P].rearrange("p s (g q) -> p s g q", g=2),
                                         ACT.Copy).then_inc(sc_copied, 1)
                elif kind == "wsum":
                    i = step[1]
                    if i == 0:
                        act.wait_ge(raw_in, 48)
                        act.wait_ge(ready0, 4)
                    if i < 2:
                        w = slice(i * F0, (i + 1) * F0)
                        parts = [(Q12[:, :, w], raw12[:, :, w], gs[:, i:i + 1])]
                    else:
                        parts = [(Q3[:, 0:FM - 1, :], raw3[:, 0:FM - 1, :], gs[:, 2:3]),
                                 (Q3[0:LAST, FM - 1, :], raw3[0:LAST, FM - 1, :], gs[0:LAST, 3:4])]
                    for sign, raw, total in parts:
                        nc.scalar.activation(sign, raw, ACT.Sign)
                        ins = nc.scalar.activation(raw, raw, ACT.Abs, accum_out=total)
                    ins.then_inc(sums, 1)
                elif kind == "ret":
                    t = step[1]
                    act.wait_ge(evac0, t + 1)
                    if t >= 2:
                        act.wait_ge(gates, t - 1)
                    nc.scalar.activation(TH[:, t % 2, :], VG[:, t % 4, D:2 * D], ACT.Tanh, scale=0.5).then_inc(tanh0, 1)
                elif kind == "tqk":
                    t = step[1]
                    act.wait_ge(pe_done, PLACE[step][3])
                    ins = nc.scalar.activation(QKT[:, t % 3, :, :].rearrange("p a b -> p (a b)"), ps[:, :], ACT.Copy)
                    ins.then_inc(qkT, 1)
                elif kind == "ty":
                    act.wait_ge(pe_done, PLACE[step][3])
                    nc.scalar.activation(YT[:, 0, :], ps[:, 0:D], ACT.Copy, scale=SA * (1.0 if step[1] else 0.5)).then_inc(y_head, 1)
                elif kind == "tx":
                    t = step[2]
                    act.wait_ge(pe_done, PLACE[step][3])
                    nc.scalar.activation(XT[:, 0, :, t * P:(t + 1) * P], ps[:, 0:D].rearrange("p (k t) -> p k t", k=KD),
                                         ACT.Copy, scale=SA).then_inc(x_head[step[1]], 1)
                elif kind == "up":
                    m = step[2]
                    rows = P if m < FM - 1 else LAST
                    act.wait_ge(pe_done, PLACE[step][3])
                    if n > 2:
                        act.wait_ge(hidden, n - 2)
                    nc.scalar.activation(THF[0:rows, n % 2, :], ps[0:rows, 0, :], ACT.Tanh, scale=0.5 / SA).then_inc(up_tanh, 1)
                elif kind == "cut":
                    m = step[2]
                    rows = P if m < FM - 1 else LAST
                    act.wait_ge(hidden, n)
                    if step == ("cut", 1, 0):
                        act.wait_ge(pe_done, PLACE[("dn", TB - 1)][3])
                    nc.scalar.activation(HT0[0:rows, 0, m, :], HF[0:rows, n % 2, :], ACT.Copy).then_inc(h_head, 1)
                elif kind == "qk":
                    _, b, i = step
                    act.wait_ge(pe_done, PLACE[step][3])
                    if b:
                        act.wait_ge(pe_done, PLACE[("tm", 0, i)][3])
                    q, k, val = (w.rearrange("p (h d) -> p h d", h=AH) for w in (ps[:, 0, 0:D], ps[:, 0, D:2 * D], ps[:, 1, 0:D]))
                    nc.scalar.activation(ST[:, i, 0, :, 0:16], q, ACT.Copy, scale=UN)
                    nc.scalar.activation(ST[:, i, 1, :, 0:16], k, ACT.Copy, scale=4 * UN).then_inc(st_head, 1)
                    nc.scalar.activation(V[:, b * TB + i, :, 0:16], val, ACT.Copy, scale=UN)
                    act.wait_ge(st_head, n)
                    nc.scalar.activation(ST[:, i, 0, :, 16:32], ST[:, i, 0, :, 0:16], ACT.Copy)
                    nc.scalar.activation(ST[:, i, 1, :, 32:48], ST[:, i, 1, :, 0:16], ACT.Copy).then_inc(qkv_copied, 1)
                elif kind == "tq":
                    i = step[2]
                    act.wait_ge(pe_done, PLACE[step][3])
                    nc.scalar.activation(QT[:, :, i * P:(i + 1) * P],
                                         psum16(step)[:, 0, :].rearrange("p (a b) -> p a b", b=P), ACT.Copy).then_inc(q_up, 1)
                elif kind == "tm":
                    i = step[2]
                    act.wait_ge(pe_done, PLACE[step][3])
                    ins = nc.scalar.activation(QT[:, :, i * P:(i + 1) * P],
                                               psum16(step).rearrange("p (a b) -> p a b", b=P), ACT.Copy)
                    ins.then_inc(q_max, 1)
                elif kind == "se":
                    _, b, g, j, s0 = step
                    act.wait_ge(pe_done, PLACE[step][3])
                    w = (TB - j) * P
                    heads = PE1[:, j % 2, s0:s0 + se_heads(j), 0:w].rearrange("p (h s) k -> p s h k", s=2)
                    ins = nc.scalar.activation(heads, by_row_tile(ps, se_heads(j))[:, :, :, 0:w], ACT.Exp, scale=1.0 / 16)
                    ins.then_inc(exped, 1)
                elif kind == "pv" and step[3] == TB - 1:
                    act.wait_ge(pe_done, PLACE[step][3])
                    nc.scalar.activation(YU[:, step[2], :], ps[:, :], ACT.Copy).then_inc(yu, 1)
                elif kind == "rc":
                    t = step[1]
                    r = small[:, t % 2, :]
                    act.wait_ge(logits, n)
                    nc.scalar.activation(r[:, 24:32], r[:, 16:24], ACT.Exp, bias=r[:, 9:10], accum_out=r[:, 32:33])
                    nc.scalar.activation(r[:, 33:34], r[:, 8:9], ACT.Tanh, scale=0.5).then_inc(r_exp, 1)
                elif kind == "mu":
                    act.wait_ge(pe_done, PLACE[step][3])
                    if n > 2:
                        act.wait_ge(mu_h, n - 2)
                    nc.scalar.activation(TG[:, n % 2, :], ps[:, 0, 0:MCW], ACT.Tanh, scale=0.5 * UN).then_inc(mu_tanh, 1)
                elif kind == "mt":
                    _, t, part = step
                    act.wait_ge(pe_done, PLACE[step][3])
                    if part < 2:
                        nc.scalar.activation(HT[:, t % 2, 0, 8 * part:8 * part + 8, :].rearrange("p a b -> p (a b)"),
                                             ps[:, :, :].rearrange("p a b -> p (a b)"), ACT.Copy).then_inc(mt_head, 1)
                    else:
                        nc.scalar.activation(HT[0:LAST, t % 2, 0, 16, :], ps[0:LAST, 0:P], ACT.Copy).then_inc(mt_head, 1)

        @block.vector
        def _(dve):
            v = nc.vector
            count = [0]

            def mark(ins):
                count[0] += 1
                ins.then_inc(dve_order, 1)
                return count[0]

            def link(ins):
                dve.wait_ge(dve_order, mark(ins))

            def finished(step):
                dve.wait_ge(pe_done, PLACE[step][3])

            def norm_input(step, ps, scale):
                layer, t = LAYER.get(step[0], step[1]), step[-1]
                n = NTH[("ln", layer, t)]
                r = 2 * (layer % 2) + n % 2
                finished(step)
                if layer == 0:
                    dve.wait_ge(x_in[t // TB], 16)
                v.scalar_tensor_tensor(Z[:, r, :], ps[:, 0:D], scale, X[:, t, :], ALU.mult, ALU.add).then_inc(z_ready[layer], 1)
                dve.wait_ge(z_ready[layer], n)
                link(v.bn_stats(stats[:, r, :], Z[:, r, :]))
                link(v.bn_aggr(mv[:, r, :], stats[:, r, :]))
                v.tensor_scalar(veps[:, r:r + 1], mv[:, r, 1:2], EPS, None, ALU.add).then_inc(ln_var[layer], 1)

            for step in SCHEDULE:
                kind, n = step[0], NTH[step]
                ps = psum(step) if kind in RING_OF else None
                if kind == "split":
                    i = step[1]
                    (head, src), (rest, _) = split_views(i, 0), split_views(i, 1)
                    dve.wait_ge(head_cut, n)
                    v.scalar_tensor_tensor(rest, src, SA if PIECES[i][0] == "xT" else SW, head,
                                           ALU.mult, ALU.subtract).then_inc(rest_cut, 1)
                elif kind == "bias":
                    if n == 1:
                        dve.wait_ge(con_in, 16)
                    dve.wait_ge(bias_head, n)
                    w = slice(0, 5 * D) if n == 1 else slice(5 * D, 9 * D)
                    v.scalar_tensor_tensor(bias[0:2, w], bias_raw[0:2, w], con[0:2, C_REST:C_REST + 1], bias[0:2, w],
                                           ALU.mult, ALU.subtract).then_inc(bias_cut, 1)
                elif kind == "proj":
                    t = step[1]
                    dve.wait_ge(evac0, t + 1)
                    if t < TB:
                        dve.wait_ge(tables, t + 1)
                    qk = QK0[:, t % 2].rearrange("p (s u j) -> p s u j", u=2, j=RD // 2)
                    cos = tab_cos[:, t % TB].unsqueeze(2).to_broadcast([P, 2 * RH, 2, RD // 2])
                    v.tensor_tensor(R1[:, t % 2].rearrange("p (s u j) -> p s u j", u=2, j=RD // 2),
                                    qk, cos, ALU.mult).then_inc(rot1, 1)
                elif kind == "rot":
                    t = step[1]
                    dve.wait_ge(rot1, t + 1)
                    dve.wait_ge(rot2, t + 1)
                    a, b, o = (w[:, t % 2].rearrange("p (s u j) -> p s u j", u=2, j=RD // 2) for w in (R1, R2, ROT))
                    v.tensor_tensor(o[:, :, 0], a[:, :, 0], b[:, :, 0], ALU.subtract)
                    v.tensor_tensor(o[:, :, 1], a[:, :, 1], b[:, :, 1], ALU.add).then_inc(rotated, 1)
                elif kind == "kv":
                    t = step[1]
                    c = t % TB
                    finished(step)
                    if t == 0:
                        dve.wait_ge(block_in, 16)
                    if c == 0:
                        v.tensor_tensor(TS[:, 0], ps[:, 0:D], block_g, ALU.mult).then_inc(state, 1)
                    else:
                        link(v.tensor_tensor(KVM, ps[:, 0:D], block_g, ALU.mult))
                        for g in range(2):
                            w = slice(g * P, (g + 1) * P)
                            ins = v.scalar_tensor_tensor(TS[:, c, w], TS[:, c - 1, w], con[:, C_G128 + g:C_G128 + g + 1],
                                                         KVM[:, w], ALU.mult, ALU.add)
                        ins.then_inc(state, 1)
                    dve.wait_ge(state, n)
                elif kind == "ret":
                    t = step[1]
                    finished(step)
                    sm = gsmall[:, t % 2]
                    heads = ps[:, 0:D].rearrange("p (h d) -> p h d", h=RH)
                    cent = CENT[:, t % 2].rearrange("p (h d) -> p h d", h=RH)
                    link(v.tensor_reduce(sm[:, 0], heads, AX.X, ALU.add))
                    link(v.tensor_scalar(sm[:, 1], sm[:, 0], -1.0 / RD, None, ALU.mult))
                    v.tensor_tensor(cent, heads, sm[:, 1].unsqueeze(2).to_broadcast([P, RH, RD]), ALU.add)\
                        .then_inc(centered, 1)
                    dve.wait_ge(centered, n)
                    link(v.tensor_tensor(SQ, CENT[:, t % 2], CENT[:, t % 2], ALU.mult))
                    link(v.tensor_reduce(sm[:, 2], SQ.rearrange("p (h d) -> p h d", h=RH), AX.X, ALU.add))
                    v.tensor_scalar(sm[:, 2], sm[:, 2], 1.0 / RD, EPS, ALU.mult, ALU.add).then_inc(gvar, 1)
                elif kind == "gn":
                    t = step[1]
                    y = Y[:, NTH[("ty", 0, t)] % 2, :]
                    dve.wait_ge(grstd, n)
                    dve.wait_ge(gates, n)
                    link(v.tensor_tensor(y.rearrange("p (h d) -> p h d", h=RH),
                                         CENT[:, t % 2].rearrange("p (h d) -> p h d", h=RH),
                                         gsmall[:, t % 2, 3].unsqueeze(2).to_broadcast([P, RH, RD]), ALU.mult))
                    link(v.tensor_tensor(y, y, GA[:, t % 2], ALU.mult))
                    v.tensor_tensor(y, y, GC[:, t % 2], ALU.add).then_inc(y_ready, 1)
                elif kind == "ty":
                    finished(step)
                    dve.wait_ge(y_head, n)
                    v.scalar_tensor_tensor(YT[:, 1, :], ps[:, 0:D], SA * (1.0 if step[1] else 0.5), YT[:, 0, :],
                                           ALU.mult, ALU.subtract).then_inc(y_rest, 1)
                elif kind == "wo":
                    norm_input(step, ps, UN)
                elif kind == "dn":
                    norm_input(step, ps, 0.5 / SA)
                elif kind == "md":
                    norm_input(step, ps, UN)
                elif kind == "ln":
                    layer, t = step[1:]
                    r = 2 * (layer % 2) + n % 2
                    dve.wait_ge(ln_rstd[layer], n)
                    v.tensor_scalar(X[:, t, :], Z[:, r, :], mv[:, r, 0:1], rstd[:, r:r + 1],
                                    ALU.subtract, ALU.mult).then_inc(ln_done[layer], 1)
                    dve.wait_ge(ln_done[layer], n)
                elif kind == "tx":
                    t = step[2]
                    finished(step)
                    dve.wait_ge(x_head[step[1]], n)
                    w = slice(t * P, (t + 1) * P)
                    v.scalar_tensor_tensor(XT[:, 1, :, w], ps[:, 0:D].rearrange("p (k t) -> p k t", k=KD), SA,
                                           XT[:, 0, :, w], ALU.mult, ALU.subtract).then_inc(x_rest[step[1]], 1)
                elif kind == "gsum":
                    finished(step)
                    link(v.tensor_scalar(thr[:, :], ps[:, 0:3], 0.5 / (D * F0), 0.5e-8, ALU.mult, ALU.add))
                    v.scalar_tensor_tensor(thr[:, 2:3], ps[:, 3:4], 0.5 / (D * F0), thr[:, 2:3], ALU.mult, ALU.add)\
                        .then_inc(thresholds, 1)
                    dve.wait_ge(thresholds, 1)
                elif kind == "quant":
                    i = step[1]
                    if i < 2:
                        parts = [(P, raw12[:, :, i * F0:(i + 1) * F0], Q12[:, :, i * F0:(i + 1) * F0])]
                    else:
                        parts = [(P, raw3[:, 0:FM - 1, :], Q3[:, 0:FM - 1, :]),
                                 (LAST, raw3[0:LAST, FM - 1, :], Q3[0:LAST, FM - 1, :])]
                    for rows, raw, q in parts:
                        ins = v.scalar_tensor_tensor(q, raw, thr[0:rows, i:i + 1], q, ALU.is_gt, ALU.mult)
                    ins.then_inc(quant, 1)
                elif kind == "up":
                    m = step[2]
                    rows = P if m < FM - 1 else LAST
                    finished(step)
                    dve.wait_ge(up_tanh, n)
                    if n == 1:
                        dve.wait_ge(quant, 3)
                    if n > 2:
                        dve.wait_ge(h_head, n - 2)
                        dve.wait_ge(h_rest, n - 2)
                    v.scalar_tensor_tensor(HF[0:rows, n % 2, :], THF[0:rows, n % 2, :], 1.0, ps[0:rows, 1, :],
                                           ALU.add, ALU.mult).then_inc(hidden, 1)
                elif kind == "qk":
                    i = step[2]
                    if n == 1:
                        dve.wait_ge(pe_done, PLACE[("wo", 0, NT - 1)][3])
                        link(v.memset(ST[:, :, :, :, 48:64], 0.0))
                        v.memset(ST[:, :, 1, :, 48:49], 1.0)
                    finished(step)
                    if n > TB:
                        v.memset(ST[:, i, 0, :, 48:49], 0.0)
                    dve.wait_ge(st_head, n)
                    for w, scale, at in ((0, UN, 32), (1, 4 * UN, 16)):
                        ins = v.scalar_tensor_tensor(ST[:, i, w, :, at:at + 16],
                                                     ps[:, 0, w * D:(w + 1) * D].rearrange("p (h d) -> p h d", h=AH), scale,
                                                     ST[:, i, w, :, 0:16], ALU.mult, ALU.subtract)
                    ins.then_inc(st_rest, 1)
                elif kind == "tq":
                    i = step[2]
                    finished(step)
                    v.tensor_copy(KT[:, :, i * P:(i + 1) * P],
                                  psum16(step)[:, 1, :].rearrange("p (a b) -> p a b", b=P)).then_inc(k_up, 1)
                elif kind == "mx":
                    _, b, i, h0 = step
                    finished(step)
                    n_h = mx_heads(i)
                    v.tensor_reduce(ST[:, i, 0, h0:h0 + n_h, 48].rearrange("p (h s) -> p s h", s=2),
                                    by_row_tile(ps, n_h)[:, :, :, 0:(i + 1) * P], AX.X, ALU.max,
                                    negate=True).then_inc(maxed, 1)
                elif kind == "ya":
                    _, b, i = step
                    m = NTH[("ty", 2, b * TB + i)]
                    finished(step)
                    heads = ps[:, :].rearrange("p (h d) -> p h d", h=AH)
                    link(v.reciprocal(rden[:, m % 2].unsqueeze(2), heads[:, :, AD:AD + 1]))
                    v.tensor_tensor(Y[:, m % 2].rearrange("p (h d) -> p h d", h=AH), heads[:, :, 0:AD],
                                    rden[:, m % 2].unsqueeze(2).to_broadcast([P, AH, AD]), ALU.mult).then_inc(y_ready, 1)
                elif kind == "rt":
                    t = step[1]
                    r = small[:, t % 2, :]
                    finished(step)
                    v.tensor_scalar(r[:, 0:NR], ps[:, 0:NR], UN, None, ALU.mult).then_inc(logit_read, 1)
                    dve.wait_ge(logit_read, n)
                    link(v.max(r[:, 16:24], r[:, 0:NE]))
                    link(v.max_index(small_i[:, t % 2, :], r[:, 16:24], r[:, 0:NE]))
                    v.tensor_scalar(r[:, 9:10], r[:, 16:17], -1.0, None, ALU.mult).then_inc(logits, 1)
                    link(v.tensor_copy(r[:, 34:36], small_i[:, t % 2, 0:2]))
                elif kind == "rc":
                    t = step[1]
                    r = small[:, t % 2, :]
                    scale = 0.5 * SA * UN * UN
                    iota = con[:, C_IOTA:C_IOTA + NE]
                    dve.wait_ge(r_exp, n)
                    link(v.reciprocal(r[:, 36:37], r[:, 32:33]))
                    link(v.tensor_scalar(r[:, 37:39], r[:, 24:26], r[:, 36:37], scale, ALU.mult, ALU.mult))
                    v.tensor_scalar(r[:, 40:48], iota, r[:, 34:35], r[:, 37:38], ALU.is_equal, ALU.mult)
                    link(v.tensor_scalar(r[:, 48:56], iota, r[:, 35:36], r[:, 38:39], ALU.is_equal, ALU.mult))
                    v.tensor_tensor(r[:, 48:56], r[:, 48:56], r[:, 40:48], ALU.add)
                    link(v.tensor_scalar(r[:, 56:57], r[:, 33:34], 1.0, 0.5 * scale, ALU.add, ALU.mult))
                elif kind == "mu":
                    _, t, c = step
                    finished(step)
                    dve.wait_ge(mu_tanh, n)
                    if n > 2:
                        dve.wait_ge(mu_h, n - 2)
                    link(v.scalar_tensor_tensor(AG[:, n % 2, :], TG[:, n % 2, :], 1.0, ps[:, 0, 0:MCW], ALU.add, ALU.mult))
                    coef_at = [(0, FE, 2 * c), (FE, FE, 2 * c + 1)] if 2 * c < NE else [(0, MCW, NE)]
                    for at, w, e in coef_at:
                        ins = v.scalar_tensor_tensor(H[:, c * MCW + at:c * MCW + at + w], AG[:, n % 2, at:at + w],
                                                     small[:, t % 2, 48 + e:49 + e], ps[:, 1, at:at + w], ALU.mult, ALU.mult)
                    ins.then_inc(mu_h, 1)
                elif kind == "mt":
                    _, t, part = step
                    finished(step)
                    dve.wait_ge(mt_head, n)
                    if part < 2:
                        k = slice(8 * part, 8 * part + 8)
                        v.tensor_tensor(HT[:, t % 2, 1, k, :].rearrange("p a b -> p (a b)"),
                                        ps[:, :, :].rearrange("p a b -> p (a b)"),
                                        HT[:, t % 2, 0, k, :].rearrange("p a b -> p (a b)"), ALU.subtract).then_inc(mt_rest, 1)
                    else:
                        v.tensor_tensor(HT[0:LAST, t % 2, 1, 16, :], ps[0:LAST, 0:P], HT[0:LAST, t % 2, 0, 16, :],
                                        ALU.subtract).then_inc(mt_rest, 1)

        @block.gpsimd
        def _(pool):
            g_ = nc.gpsimd
            count = [0]

            def link(ins):
                count[0] += 1
                ins.then_inc(pool_order, 1)
                pool.wait_ge(pool_order, count[0])

            g_.memset(ones, 1.0).then_inc(ready0, 1)
            g_.memset(gs[:, :], 0.0).then_inc(ready0, 1)
            g_.memset(half[:, :], -0.5).then_inc(ready0, 1)
            g_.memset(bias[:, :], 0.0).then_inc(ready0, 1)
            pool.wait_ge(ready0, 4)
            for step in SCHEDULE:
                kind, n = step[0], NTH[step]
                if kind == "proj":
                    t = step[1]
                    if t == 0:
                        pool.wait_ge(con_in, 16)
                    if t < TB:
                        dec = con[:, C_DEC:C_DEC + 2 * RH].unsqueeze(2).to_broadcast([P, 2 * RH, RD // 2])
                        for tab, at in ((tab_cos, C_COS), (tab_sin, C_SIN)):
                            at += t * RD // 2
                            ins = g_.tensor_tensor(tab[:, t], con[:, at:at + RD // 2].unsqueeze(1).to_broadcast([P, 2 * RH, RD // 2]),
                                                   dec, ALU.mult)
                        ins.then_inc(tables, 1)
                        pool.wait_ge(tables, t + 1)
                    if t >= 2:
                        pool.wait_ge(rotated, t - 1)
                    pool.wait_ge(evac0, t + 1)
                    qk = QK0[:, t % 2].rearrange("p (s u j) -> p s u j", u=2, j=RD // 2)
                    o = R2[:, t % 2].rearrange("p (s u j) -> p s u j", u=2, j=RD // 2)
                    g_.tensor_tensor(o[:, :, 0], qk[:, :, 1], tab_sin[:, t % TB], ALU.mult)
                    g_.tensor_tensor(o[:, :, 1], qk[:, :, 0], tab_sin[:, t % TB], ALU.mult).then_inc(rot2, 1)
                elif kind == "sc":
                    _, t, hf = step
                    pool.wait_ge(sc_copied, n)
                    part = PT[:, t % 2, hf].rearrange("p s g q -> p (s g) q")
                    g_.affine_select(out=part, in_=part, compare_op=ALU.is_ge, fill=0.0, base=0,
                                     pattern=[[0, 4], [1, P]], channel_multiplier=-1).then_inc(pT, 1)
                elif kind == "ret":
                    t = step[1]
                    if t == 0:
                        pool.wait_ge(gnorm_in, 16)
                    pool.wait_ge(tanh0, t + 1)
                    if t >= 2:
                        pool.wait_ge(y_ready, NTH[("ty", 0, t - 2)])
                    gate = VG[:, t % 4, D:2 * D]
                    link(g_.tensor_tensor(GC[:, t % 2], TH[:, t % 2], gate, ALU.mult))
                    link(g_.tensor_tensor(GC[:, t % 2], GC[:, t % 2], gate, ALU.add))
                    link(g_.tensor_tensor(GA[:, t % 2], GC[:, t % 2], gnorm[:, 0:D], ALU.mult))
                    g_.tensor_tensor(GC[:, t % 2], GC[:, t % 2], gnorm[:, D:2 * D], ALU.mult).then_inc(gates, 1)
                    pool.wait_ge(gvar, n)
                    g_.tensor_tensor(gsmall[:, t % 2, 3], gsmall[:, t % 2, 2], half[:, 0:RH], ALU.pow).then_inc(grstd, 1)
                elif kind in ("wo", "dn", "md"):
                    layer = LAYER.get(kind, step[1])
                    m = NTH[("ln", layer, step[-1])]
                    r = 2 * (layer % 2) + m % 2
                    pool.wait_ge(ln_var[layer], m)
                    g_.tensor_tensor(rstd[:, r:r + 1], veps[:, r:r + 1], half[:, 0:1], ALU.pow).then_inc(ln_rstd[layer], 1)
                elif kind == "cut":
                    m = step[2]
                    rows = P if m < FM - 1 else LAST
                    pool.wait_ge(h_head, n)
                    g_.tensor_tensor(HT0[0:rows, 1, m, :], HF[0:rows, n % 2, :], HT0[0:rows, 0, m, :],
                                     ALU.subtract).then_inc(h_rest, 1)
                elif kind == "qk" and n == 1:
                    pool.wait_ge(pe_done, PLACE[("wo", 0, NT - 1)][3])
                    link(g_.memset(V[:, :, :, 16:32], 0.0))
                    g_.memset(V[:, :, :, 16:17], 1.0).then_inc(v_init, 1)
                elif kind == "se":
                    _, b, g, j, s0 = step
                    pool.wait_ge(exped, n)
                    part = PE1[:, j % 2, s0:s0 + se_heads(j), 0:P]
                    g_.affine_select(out=part, in_=part, compare_op=ALU.is_ge, fill=0.0, base=0,
                                     pattern=[[0, se_heads(j)], [1, P]], channel_multiplier=-1).then_inc(causal, 1)


def constants():
    gammas = (1.0 - np.exp(np.linspace(np.log(1 / 32), np.log(1 / 64), RH))).astype(np.float32).astype(np.float64)
    con = np.zeros((P, C_TOT))
    part = np.arange(P)
    block = np.zeros((P, D))
    con[:, C_ID:C_ID + P] = np.eye(P)
    for g in range(2):
        own = gammas[4 * g + part // RD] ** P
        block[:, g * P:(g + 1) * P] = own[:, None] * (part[:, None] // RD == part[None, :] // RD)
        con[:, C_G128 + g] = own
    thetas = (1.0 / np.float32(10000.0) ** np.linspace(0.0, 1.0, RD // 2, dtype=np.float32)).astype(np.float32)
    for c in range(TB):
        angle = ((c * P + part).astype(np.float32)[:, None] * thetas[None, :]).astype(np.float32).astype(np.float64)
        con[:, C_COS + c * RD // 2:C_COS + (c + 1) * RD // 2] = np.cos(angle)
        con[:, C_SIN + c * RD // 2:C_SIN + (c + 1) * RD // 2] = np.sin(angle)
    con[:, C_DEC:C_DEC + RH] = gammas[None, :] ** part[:, None]
    con[:, C_DEC + RH:C_DEC + 2 * RH] = gammas[None, :] ** -part[:, None].astype(np.float64) / np.sqrt(RD)
    con[:, C_IOTA:C_IOTA + NE] = np.arange(NE)
    con[1:, C_REST] = SW
    con16 = np.zeros((P, 3 * P))
    con16[0, 2 * P:] = -SA
    con16[1, 2 * P:] = SA
    con16[:, 0:P] = np.eye(P)
    con16[:, P:2 * P] = np.where(part[None, :] > part[:, None], -60000.0, 0.0)
    return con.astype(np.float32), con16.astype(np.float16), block.astype(np.float32)


def tiled(w):
    k = w.shape[0] // P
    return np.ascontiguousarray(w.reshape(k, P, -1).transpose(1, 0, 2).reshape(P, -1))


def layout(i):
    turn = np.concatenate([np.concatenate([np.arange(0, RD, 2), np.arange(1, RD, 2)]) + h * RD for h in range(RH)])
    x = i["L0_attn_x"].reshape(NT * P, D)
    a = {"xT": tiled(x.T).reshape(P, KD, NB, TB * P).transpose(0, 2, 1, 3).reshape(P, -1), "x": np.ascontiguousarray(x)}
    a["wqkvg"] = tiled(np.concatenate([i["L0_attn_w_q"][:, turn], i["L0_attn_w_k"][:, turn], i["L0_attn_w_v"],
                                       i["L0_attn_w_g"]], 1))
    a["wo"] = np.concatenate([tiled(i["L0_attn_w_o"]), tiled(i["L1_attn_Wo"])], 1)
    a["wqkv1"] = tiled(np.concatenate([i[f"L1_attn_W{c}"].transpose(1, 0, 2).reshape(D, D) for c in "qkv"], 1))
    gate = np.concatenate([i["L1_ffn_We_gate_up"][e, :, :FE] for e in range(NE)] + [i["L1_ffn_Ws_gate_up"][:, :FS]], 1)
    up = np.concatenate([i["L1_ffn_We_gate_up"][e, :, FE:] for e in range(NE)] + [i["L1_ffn_Ws_gate_up"][:, FS:]], 1)
    a["wup"] = tiled(np.stack([gate.reshape(D, MC, MCW), up.reshape(D, MC, MCW)], 2).reshape(D, -1))
    down = np.concatenate([i["L1_ffn_We_down"].reshape(NE * FE, D), i["L1_ffn_Ws_down"]], 0)
    a["wdown"] = tiled(down[:(HK - 1) * P])
    last = np.concatenate([down[(HK - 1) * P:], np.zeros((P - LAST, D), np.float32)], 0)
    a["wtail"] = np.concatenate([last, tiled(np.concatenate([i["L1_ffn_W_router"].T, i["L1_ffn_W_sgate"].T], 1))], 1)
    a["w12"] = np.concatenate([i["L0_ffn_w1"].T, i["L0_ffn_w2"].T], 1)
    a["w3"] = np.ascontiguousarray(i["L0_ffn_w3"].T)
    a["bias_rows"] = np.concatenate([i["L0_attn_b_q"][turn], i["L0_attn_b_k"][turn], i["L0_attn_b_v"], i["L0_attn_b_g"],
                                     i["L0_attn_b_o"], i["L1_attn_bq"].reshape(-1), i["L1_attn_bk"].reshape(-1),
                                     i["L1_attn_bv"].reshape(-1), i["L1_attn_bo"]])
    a["gnorm_rows"] = np.concatenate([i["L0_attn_gn_weight"], i["L0_attn_gn_bias"]])
    a["consts"], a["consts16"], a["block_decay"] = constants()
    return a


def kernel(**inputs):
    import concourse.bacc as _bacc
    from concourse.bass_utils import run_bass_kernel_spmd as _run

    nc = _bacc.Bacc("TRN2", target_bir_lowering=False, num_devices=1)
    arrays, args = {}, []
    for name, a in layout({k: np.asarray(v) for k, v in inputs.items()}).items():
        a = np.ascontiguousarray(a)
        arrays[f"in_{name}"] = a
        args.append(nc.dram_tensor(f"in_{name}", a.shape, mybir.dt.from_np(a.dtype), kind="ExternalInput").ap())
    out = nc.dram_tensor("out", (NT * P, D), mybir.dt.float32, kind="ExternalOutput").ap()
    build_two_layers(nc, *args, out)
    r = _run(nc, [arrays], core_ids=[0])
    return r.results[0]["out"].reshape(NB, TB * P, D)
```
